# Optimizing a Trainium2 kernel written in Bass

```python
import numpy as np
import jax
import jax.numpy as jnp

def _softmax(x, axis=-1):
    return jax.nn.softmax(x, axis=axis)

def _gelu(x):
    return jax.nn.gelu(x, approximate=True)

def _silu(x):
    return jax.nn.silu(x)

def _sigmoid(x):
    return jax.nn.sigmoid(x)

def _layernorm(x, axis=-1, eps=1e-05):
    m = jnp.mean(x, axis=axis, keepdims=True)
    v = jnp.var(x, axis=axis, keepdims=True)
    return (x - m) / jnp.sqrt(v + eps)

def _scatter_add(tgt, idx, src, axis=0):
    return tgt.at[idx].add(src)

def _segment_sum(src, seg, n):
    return jax.ops.segment_sum(src, seg, n)
kernel_name = 'mk_xattn_ffn_d4_seqx_r8_98314d'

def setup_inputs(seed: int=0):
    np.random.seed(seed)
    _w = jnp.asarray

    def _rec_inputs():
        import jax
        import jax.numpy as jnp
        _rk = jax.random.key(seed)
        x = -1.394e-06 + 0.9999 * jax.random.normal(jax.random.fold_in(_rk, 1), (4, 256, 128), jnp.float32)
        _lenS = 256 - jax.random.randint(jax.random.fold_in(_rk, 7), (4,), 0, max(1, 256 // 4) + 1, jnp.int32)
        _lenS2 = 64 - jax.random.randint(jax.random.fold_in(_rk, 8), (4,), 0, max(1, 64 // 4) + 1, jnp.int32)
        _ctx_1024P = jax.random.normal(jax.random.fold_in(_rk, 11), (4, 16, 128), jnp.float32)
        _ctx_1024c = jax.random.dirichlet(jax.random.fold_in(_rk, 511), 0.3 * jnp.ones((16,), jnp.float32), (4, 64))
        _ctx_1024t = jnp.einsum('bsk,bkd->bsd', _ctx_1024c, _ctx_1024P)
        _ctx_1024t = _ctx_1024t * jax.lax.rsqrt(jnp.mean(jnp.square(_ctx_1024t)) + 1e-12) * 0.953939
        ctx_1024 = 7.22013e-05 + 1.00017 * (_ctx_1024t + 0.3 * jax.random.normal(jax.random.fold_in(_rk, 611), (4, 64, 128), jnp.float32))
        _validS = jnp.arange(256)[None, :] < _lenS[:, None]
        _validS2 = jnp.arange(64)[None, :] < _lenS2[:, None]
        _causal = jnp.tril(jnp.ones((256, 256), dtype=bool))
        mask_BxSxS2_ik0 = jnp.where(jnp.broadcast_to(_validS2[:, None, :], (4, 256, 64)), 0, 1).astype(jnp.int32)
        mask_SxS2_fk0 = jnp.where(jnp.broadcast_to(_validS2[0:1, :], (256, 64)), -1000000000.0, 0.0).astype(jnp.float32)
        return (x, ctx_1024, mask_BxSxS2_ik0, mask_SxS2_fk0)
    x, ctx_1024, mask_BxSxS2_ik0, mask_SxS2_fk0 = _rec_inputs()

    def _L0_xattn_setup():
        import jax, jax.numpy as jnp
        import numpy as np
        B, NKV, NQ, D, H = (4, 256, 128, 128, 16)
        HD = D // H
        key = jax.random.key(seed)
        ks = jax.random.split(key, 9)
        s = 0.02
        return {'x': jax.random.normal(ks[0], (B, NKV, D), jnp.float32), 'y': jax.random.normal(ks[1], (B, NQ, D), jnp.float32), 'mask': jax.random.randint(ks[2], (B, NQ, NKV), 0, 2, jnp.int32), 'W_kv': jax.random.normal(ks[3], (D, 2 * D), jnp.float32) * s, 'b_kv': jnp.zeros((2 * D,), jnp.float32), 'W_q': jax.random.normal(ks[4], (D, D), jnp.float32) * s, 'b_q': jnp.zeros((D,), jnp.float32), 'W_o': jax.random.normal(ks[5], (D, D), jnp.float32) * s, 'b_o': jnp.zeros((D,), jnp.float32)}
    _L0_xattn_all = _L0_xattn_setup()
    _L0_xattn_in = {k: v for k, v in _L0_xattn_all.items() if k in ('W_kv', 'b_kv', 'W_q', 'b_q', 'W_o', 'b_o')}
    del _L0_xattn_all

    def _L0_ffn_setup():
        import jax, jax.numpy as jnp
        import numpy as np
        TOP_K = 2
        key = jax.random.key(seed)
        ks = jax.random.split(key, 8)
        B, S, D = (2, 256, 128)
        N_r, N_s = (16, 2)
        u = jax.random.normal(ks[0], (B, S, D), dtype=jnp.float32)
        centroids = jax.random.normal(ks[1], (N_r, D), dtype=jnp.float32)
        expert_biases = jnp.zeros((N_r,), dtype=jnp.float32)
        Wr = jax.random.normal(ks[2], (N_r, D, D), dtype=jnp.float32) * (1.0 / np.sqrt(D))
        br = jax.random.normal(ks[3], (N_r, D), dtype=jnp.float32) * 0.01
        Ws = jax.random.normal(ks[4], (N_s, D, D), dtype=jnp.float32) * (1.0 / np.sqrt(D))
        bs = jax.random.normal(ks[5], (N_s, D), dtype=jnp.float32) * 0.01
        return {'u': u, 'centroids': centroids, 'expert_biases': expert_biases, 'Wr': Wr, 'br': br, 'Ws': Ws, 'bs': bs}
    _L0_ffn_all = _L0_ffn_setup()
    _L0_ffn_in = {k: v for k, v in _L0_ffn_all.items() if k in ('centroids', 'expert_biases', 'Wr', 'br', 'Ws', 'bs')}
    del _L0_ffn_all

    def _L1_xattn_setup():
        import jax, jax.numpy as jnp
        import numpy as np
        DIM = 128
        NUM_HEADS = 16
        DIM_HEAD = 64
        INNER = NUM_HEADS * DIM_HEAD
        SCALE = DIM_HEAD ** (-0.5)

        def _layernorm(x, gamma, beta, eps=1e-05):
            mu = jnp.mean(x, axis=-1, keepdims=True)
            var = jnp.mean(jnp.square(x - mu), axis=-1, keepdims=True)
            return (x - mu) * jax.lax.rsqrt(var + eps) * gamma + beta
        key = jax.random.key(seed)
        ks = jax.random.split(key, 8)
        B, SQ, SK = (2, 256, 512)
        x = jax.random.normal(ks[0], (B, SQ, DIM), dtype=jnp.float32)
        context = jax.random.normal(ks[1], (B, SK, DIM), dtype=jnp.float32)
        ln_gamma = jnp.ones((DIM,), jnp.float32)
        ln_beta = jnp.zeros((DIM,), jnp.float32)
        w_q = jax.random.normal(ks[2], (DIM, INNER), dtype=jnp.float32) / np.sqrt(DIM)
        w_kv = jax.random.normal(ks[3], (DIM, 2 * INNER), dtype=jnp.float32) / np.sqrt(DIM)
        w_out = jax.random.normal(ks[4], (INNER, DIM), dtype=jnp.float32) / np.sqrt(INNER)
        b_out = jnp.zeros((DIM,), jnp.float32)
        gate = jnp.array([0.5], jnp.float32)
        return {'x': x, 'context': context, 'ln_gamma': ln_gamma, 'ln_beta': ln_beta, 'w_q': w_q, 'w_kv': w_kv, 'w_out': w_out, 'b_out': b_out, 'gate': gate}
    _L1_xattn_all = _L1_xattn_setup()
    _L1_xattn_in = {k: v for k, v in _L1_xattn_all.items() if k in ('ln_gamma', 'ln_beta', 'w_q', 'w_kv', 'w_out', 'b_out', 'gate')}
    del _L1_xattn_all

    def _L1_ffn_setup():
        import jax, jax.numpy as jnp
        import numpy as np
        H = 128
        I = 256
        E = 32
        B, S = (4, 256)

        def _grouped_mm(a, w, group_sizes):
            return jax.lax.ragged_dot(a, w, group_sizes)

        def _swiglu(x, gw, uw, dw):
            return jax.nn.silu(x @ gw) * (x @ uw) @ dw
        key = jax.random.key(seed)
        ks = jax.random.split(key, 8)
        scale = 0.02
        inp = {'hidden_states': jax.random.normal(ks[0], (B, S, H), dtype=jnp.float32), 'gate_w': jax.random.normal(ks[1], (H, E), dtype=jnp.float32) * scale, 'shared_gate_w': jax.random.normal(ks[2], (H, I), dtype=jnp.float32) * scale, 'shared_up_w': jax.random.normal(ks[3], (H, I), dtype=jnp.float32) * scale, 'shared_down_w': jax.random.normal(ks[4], (I, H), dtype=jnp.float32) * scale, 'routed_gate_w': jax.random.normal(ks[5], (E, H, I), dtype=jnp.float32) * scale, 'routed_up_w': jax.random.normal(ks[6], (E, H, I), dtype=jnp.float32) * scale, 'routed_down_w': jax.random.normal(ks[7], (E, I, H), dtype=jnp.float32) * scale}
        return inp
    _L1_ffn_all = _L1_ffn_setup()
    _L1_ffn_in = {k: v for k, v in _L1_ffn_all.items() if k in ('gate_w', 'shared_gate_w', 'shared_up_w', 'shared_down_w', 'routed_gate_w', 'routed_up_w', 'routed_down_w')}
    del _L1_ffn_all

    def _L2_xattn_setup():
        import jax, jax.numpy as jnp
        import numpy as np
        B, SQ, SKV, D, H = (2, 256, 256, 128, 16)
        HD = D // H
        ROPE_BASE = 10000.0

        def _rope_interleaved(x):
            s, hd = (x.shape[1], x.shape[-1])
            dim = hd // 2
            freqs = jnp.exp(-jnp.arange(dim, dtype=x.dtype) * jnp.log(jnp.asarray(ROPE_BASE, x.dtype)) / dim)
            ang = jnp.arange(s, dtype=x.dtype)[:, None] * freqs[None, :]
            cos = jnp.cos(ang)[None, :, None, :]
            sin = jnp.sin(ang)[None, :, None, :]
            xe, xo = (x[..., ::2], x[..., 1::2])
            re = xe * cos - xo * sin
            ro = xe * sin + xo * cos
            return jnp.stack([re, ro], axis=-1).reshape(x.shape)
        key = jax.random.key(seed)
        ks = jax.random.split(key, 6)
        s = 1.0 / np.sqrt(D)
        return {'x_q': jax.random.normal(ks[0], (B, SQ, D), jnp.float32), 'x_kv': jax.random.normal(ks[1], (B, SKV, D), jnp.float32), 'wq': jax.random.normal(ks[2], (D, D), jnp.float32) * s, 'bq': jnp.zeros((D,), jnp.float32), 'wk': jax.random.normal(ks[3], (D, D), jnp.float32) * s, 'bk': jnp.zeros((D,), jnp.float32), 'wv': jax.random.normal(ks[4], (D, D), jnp.float32) * s, 'bv': jnp.zeros((D,), jnp.float32), 'wo': jax.random.normal(ks[5], (D, D), jnp.float32) * s, 'bo': jnp.zeros((D,), jnp.float32)}
    _L2_xattn_all = _L2_xattn_setup()
    _L2_xattn_in = {k: v for k, v in _L2_xattn_all.items() if k in ('wq', 'bq', 'wk', 'bk', 'wv', 'bv', 'wo', 'bo')}
    del _L2_xattn_all

    def _L2_ffn_setup():
        import jax, jax.numpy as jnp
        import numpy as np
        D_MODEL = 128
        NUM_HEADS = 4
        NUM_EXPERTS = 8
        TOP_K = 2
        D_FF = 128
        EPS = 1e-06

        def _rmsnorm(x, g):
            return x * jax.lax.rsqrt(jnp.mean(x * x, axis=-1, keepdims=True) + EPS) * g

        def _swiglu(x, w1, w2, w3):
            return jax.nn.silu(x @ w1.T) * (x @ w3.T) @ w2.T
        key = jax.random.key(seed)
        ks = jax.random.split(key, 16)
        d, e, f = (D_MODEL, NUM_EXPERTS, D_FF)
        dc = d // 4
        s = 0.02
        return {'X': jax.random.normal(ks[0], (2, 128, d), dtype=jnp.float32), 'g1': jnp.ones((d,), jnp.float32), 'g2': jnp.ones((d,), jnp.float32), 'Wq': jax.random.normal(ks[1], (d, d), jnp.float32) * s, 'Wkc': jax.random.normal(ks[2], (dc, d), jnp.float32) * s, 'Wvc': jax.random.normal(ks[3], (dc, d), jnp.float32) * s, 'Wo': jax.random.normal(ks[4], (d, d), jnp.float32) * s, 'Wr': jax.random.normal(ks[5], (e, d), jnp.float32) * s, 'expert_bias': jnp.zeros((e,), jnp.float32), 'sW1': jax.random.normal(ks[6], (f, d), jnp.float32) * s, 'sW2': jax.random.normal(ks[7], (d, f), jnp.float32) * s, 'sW3': jax.random.normal(ks[8], (f, d), jnp.float32) * s, 'eW1': jax.random.normal(ks[9], (e, f, d), jnp.float32) * s, 'eW2': jax.random.normal(ks[10], (e, d, f), jnp.float32) * s, 'eW3': jax.random.normal(ks[11], (e, f, d), jnp.float32) * s}
    _L2_ffn_all = _L2_ffn_setup()
    _L2_ffn_in = {k: v for k, v in _L2_ffn_all.items() if k in ('g1', 'g2', 'Wq', 'Wkc', 'Wvc', 'Wo', 'Wr', 'expert_bias', 'sW1', 'sW2', 'sW3', 'eW1', 'eW2', 'eW3')}
    del _L2_ffn_all

    def _L3_xattn_setup():
        import jax, jax.numpy as jnp
        import numpy as np
        B, S, D, H = (2, 256, 128, 16)
        A = D // H
        NEG = -1000000000.0
        key = jax.random.key(seed)
        ks = jax.random.split(key, 5)
        std = 1.0 / np.sqrt(D)
        query = jax.random.normal(ks[0], (B, S, D), dtype=jnp.float32)
        context = jax.random.normal(ks[1], (B, S, D), dtype=jnp.float32)
        Wq = jax.random.normal(ks[2], (D, D), dtype=jnp.float32) * std
        Wkv = jax.random.normal(ks[3], (2 * D, D), dtype=jnp.float32) * std
        Wout = jax.random.normal(ks[4], (D, D), dtype=jnp.float32) * std
        mask = jnp.where(jnp.tril(jnp.ones((S, S), dtype=bool)), 0.0, NEG).astype(jnp.float32)
        return {'query': query, 'context': context, 'Wq': Wq, 'Wkv': Wkv, 'Wout': Wout, 'mask': mask}
    _L3_xattn_all = _L3_xattn_setup()
    _L3_xattn_in = {k: v for k, v in _L3_xattn_all.items() if k in ('Wq', 'Wkv', 'Wout')}
    del _L3_xattn_all

    def _L3_ffn_setup():
        import jax, jax.numpy as jnp
        import numpy as np
        B, S, D, F, E = (8, 128, 128, 512, 8)
        EPS = 1e-05
        key = jax.random.key(seed)
        ks = jax.random.split(key, 4)
        s = 0.02
        return {'input_features': jax.random.normal(ks[0], (B, S, D), jnp.float32), 'centroids': jax.random.normal(ks[1], (E, D), jnp.float32) * 0.1, 'ln_g': jnp.ones((E, D), jnp.float32), 'ln_b': jnp.zeros((E, D), jnp.float32), 'w1': jax.random.normal(ks[2], (E, D, F), jnp.float32) * s, 'b1': jnp.zeros((E, F), jnp.float32), 'w2': jax.random.normal(ks[3], (E, F, D), jnp.float32) * s, 'b2': jnp.zeros((E, D), jnp.float32)}
    _L3_ffn_all = _L3_ffn_setup()
    _L3_ffn_in = {k: v for k, v in _L3_ffn_all.items() if k in ('centroids', 'ln_g', 'ln_b', 'w1', 'b1', 'w2', 'b2')}
    del _L3_ffn_all
    return {'x': x, 'ctx_1024': ctx_1024, 'mask_BxSxS2_ik0': mask_BxSxS2_ik0, 'mask_SxS2_fk0': mask_SxS2_fk0, 'L0_xattn_W_kv': _L0_xattn_in['W_kv'], 'L0_xattn_b_kv': _L0_xattn_in['b_kv'], 'L0_xattn_W_q': _L0_xattn_in['W_q'], 'L0_xattn_b_q': _L0_xattn_in['b_q'], 'L0_xattn_W_o': _L0_xattn_in['W_o'], 'L0_xattn_b_o': _L0_xattn_in['b_o'], 'L0_ffn_centroids': _L0_ffn_in['centroids'], 'L0_ffn_expert_biases': _L0_ffn_in['expert_biases'], 'L0_ffn_Wr': _L0_ffn_in['Wr'], 'L0_ffn_br': _L0_ffn_in['br'], 'L0_ffn_Ws': _L0_ffn_in['Ws'], 'L0_ffn_bs': _L0_ffn_in['bs'], 'L1_xattn_ln_gamma': _L1_xattn_in['ln_gamma'], 'L1_xattn_ln_beta': _L1_xattn_in['ln_beta'], 'L1_xattn_w_q': _L1_xattn_in['w_q'], 'L1_xattn_w_kv': _L1_xattn_in['w_kv'], 'L1_xattn_w_out': _L1_xattn_in['w_out'], 'L1_xattn_b_out': _L1_xattn_in['b_out'], 'L1_xattn_gate': _L1_xattn_in['gate'], 'L1_ffn_gate_w': _L1_ffn_in['gate_w'], 'L1_ffn_shared_gate_w': _L1_ffn_in['shared_gate_w'], 'L1_ffn_shared_up_w': _L1_ffn_in['shared_up_w'], 'L1_ffn_shared_down_w': _L1_ffn_in['shared_down_w'], 'L1_ffn_routed_gate_w': _L1_ffn_in['routed_gate_w'], 'L1_ffn_routed_up_w': _L1_ffn_in['routed_up_w'], 'L1_ffn_routed_down_w': _L1_ffn_in['routed_down_w'], 'L2_xattn_wq': _L2_xattn_in['wq'], 'L2_xattn_bq': _L2_xattn_in['bq'], 'L2_xattn_wk': _L2_xattn_in['wk'], 'L2_xattn_bk': _L2_xattn_in['bk'], 'L2_xattn_wv': _L2_xattn_in['wv'], 'L2_xattn_bv': _L2_xattn_in['bv'], 'L2_xattn_wo': _L2_xattn_in['wo'], 'L2_xattn_bo': _L2_xattn_in['bo'], 'L2_ffn_g1': _L2_ffn_in['g1'], 'L2_ffn_g2': _L2_ffn_in['g2'], 'L2_ffn_Wq': _L2_ffn_in['Wq'], 'L2_ffn_Wkc': _L2_ffn_in['Wkc'], 'L2_ffn_Wvc': _L2_ffn_in['Wvc'], 'L2_ffn_Wo': _L2_ffn_in['Wo'], 'L2_ffn_Wr': _L2_ffn_in['Wr'], 'L2_ffn_expert_bias': _L2_ffn_in['expert_bias'], 'L2_ffn_sW1': _L2_ffn_in['sW1'], 'L2_ffn_sW2': _L2_ffn_in['sW2'], 'L2_ffn_sW3': _L2_ffn_in['sW3'], 'L2_ffn_eW1': _L2_ffn_in['eW1'], 'L2_ffn_eW2': _L2_ffn_in['eW2'], 'L2_ffn_eW3': _L2_ffn_in['eW3'], 'L3_xattn_Wq': _L3_xattn_in['Wq'], 'L3_xattn_Wkv': _L3_xattn_in['Wkv'], 'L3_xattn_Wout': _L3_xattn_in['Wout'], 'L3_ffn_centroids': _L3_ffn_in['centroids'], 'L3_ffn_ln_g': _L3_ffn_in['ln_g'], 'L3_ffn_ln_b': _L3_ffn_in['ln_b'], 'L3_ffn_w1': _L3_ffn_in['w1'], 'L3_ffn_b1': _L3_ffn_in['b1'], 'L3_ffn_w2': _L3_ffn_in['w2'], 'L3_ffn_b2': _L3_ffn_in['b2']}

def reference(x, ctx_1024, mask_BxSxS2_ik0, mask_SxS2_fk0, L0_xattn_W_kv, L0_xattn_b_kv, L0_xattn_W_q, L0_xattn_b_q, L0_xattn_W_o, L0_xattn_b_o, L0_ffn_centroids, L0_ffn_expert_biases, L0_ffn_Wr, L0_ffn_br, L0_ffn_Ws, L0_ffn_bs, L1_xattn_ln_gamma, L1_xattn_ln_beta, L1_xattn_w_q, L1_xattn_w_kv, L1_xattn_w_out, L1_xattn_b_out, L1_xattn_gate, L1_ffn_gate_w, L1_ffn_shared_gate_w, L1_ffn_shared_up_w, L1_ffn_shared_down_w, L1_ffn_routed_gate_w, L1_ffn_routed_up_w, L1_ffn_routed_down_w, L2_xattn_wq, L2_xattn_bq, L2_xattn_wk, L2_xattn_bk, L2_xattn_wv, L2_xattn_bv, L2_xattn_wo, L2_xattn_bo, L2_ffn_g1, L2_ffn_g2, L2_ffn_Wq, L2_ffn_Wkc, L2_ffn_Wvc, L2_ffn_Wo, L2_ffn_Wr, L2_ffn_expert_bias, L2_ffn_sW1, L2_ffn_sW2, L2_ffn_sW3, L2_ffn_eW1, L2_ffn_eW2, L2_ffn_eW3, L3_xattn_Wq, L3_xattn_Wkv, L3_xattn_Wout, L3_ffn_centroids, L3_ffn_ln_g, L3_ffn_ln_b, L3_ffn_w1, L3_ffn_b1, L3_ffn_w2, L3_ffn_b2):
    import jax
    import jax.numpy as jnp

    def _L0_xattn_ref(x, y, mask, W_kv, b_kv, W_q, b_q, W_o, b_o):
        import jax, jax.numpy as jnp
        import numpy as np
        B, NKV, NQ, D, H = (4, 256, 128, 128, 16)
        HD = D // H
        b, nkv, _ = x.shape
        nq = y.shape[1]
        kv = x @ W_kv + b_kv
        q = y @ W_q + b_q
        kv = kv.reshape(b, nkv, H, 2 * HD).transpose(0, 2, 1, 3)
        q = q.reshape(b, nq, H, HD).transpose(0, 2, 1, 3)
        k, v = (kv[..., :HD], kv[..., HD:])
        scores = jnp.einsum('bhqd,bhkd->bhqk', q, k) / jnp.sqrt(jnp.float32(HD))
        scores = jnp.where(mask[:, None, :, :] == 0, jnp.float32(-1e+20), scores)
        attn = jax.nn.softmax(scores, axis=-1)
        vals = jnp.einsum('bhqk,bhkd->bhqd', attn, v)
        vals = vals.transpose(0, 2, 1, 3).reshape(b, nq, D)
        return vals @ W_o + b_o

    def _L0_ffn_ref(u, centroids, expert_biases, Wr, br, Ws, bs):
        import jax, jax.numpy as jnp
        import numpy as np
        TOP_K = 2
        N_r = centroids.shape[0]
        N_s = Ws.shape[0]
        raw_scores = jnp.einsum('bsd,ed->bse', u, centroids)
        s = jax.nn.softmax(raw_scores + expert_biases, axis=-1)
        topk_vals, topk_idx = jax.lax.top_k(s, TOP_K)
        g_topk = jnp.sum(jax.nn.one_hot(topk_idx, N_r, dtype=s.dtype) * topk_vals[..., None], axis=-2)
        xe = jnp.einsum('bsd,eod->bseo', u, Wr) + br
        routed = jnp.einsum('bse,bseo->bso', g_topk, xe)
        shared = (jnp.einsum('bsd,eod->bso', u, Ws) + jnp.sum(bs, axis=0)) / N_s
        return u + routed + shared

    def _L1_xattn_ref(x, context, ln_gamma, ln_beta, w_q, w_kv, w_out, b_out, gate):
        import jax, jax.numpy as jnp
        import numpy as np
        DIM = 128
        NUM_HEADS = 16
        DIM_HEAD = 64
        INNER = NUM_HEADS * DIM_HEAD
        SCALE = DIM_HEAD ** (-0.5)

        def _layernorm(x, gamma, beta, eps=1e-05):
            mu = jnp.mean(x, axis=-1, keepdims=True)
            var = jnp.mean(jnp.square(x - mu), axis=-1, keepdims=True)
            return (x - mu) * jax.lax.rsqrt(var + eps) * gamma + beta
        B, SQ, _ = x.shape
        SK = context.shape[1]
        xn = _layernorm(x, ln_gamma, ln_beta)
        q = (xn @ w_q).reshape(B, SQ, NUM_HEADS, DIM_HEAD)
        kv = context @ w_kv
        k, v = jnp.split(kv, 2, axis=-1)
        k = k.reshape(B, SK, NUM_HEADS, DIM_HEAD)
        v = v.reshape(B, SK, NUM_HEADS, DIM_HEAD)
        scores = jnp.einsum('bqhd,bkhd->bhqk', q * SCALE, k)
        attn = jax.nn.softmax(scores, axis=-1)
        out = jnp.einsum('bhqk,bkhd->bqhd', attn, v).reshape(B, SQ, INNER)
        out = out @ w_out + b_out
        return out * jnp.tanh(gate[0])

    def _L1_ffn_ref(hidden_states, gate_w, shared_gate_w, shared_up_w, shared_down_w, routed_gate_w, routed_up_w, routed_down_w):
        import jax, jax.numpy as jnp
        import numpy as np
        H = 128
        I = 256
        E = 32
        B, S = (4, 256)

        def _grouped_mm(a, w, group_sizes):
            return jax.lax.ragged_dot(a, w, group_sizes)

        def _swiglu(x, gw, uw, dw):
            return jax.nn.silu(x @ gw) * (x @ uw) @ dw
        b, s, h = hidden_states.shape
        x = hidden_states.reshape(-1, h)
        shared_out = _swiglu(x, shared_gate_w, shared_up_w, shared_down_w)
        logits = x @ gate_w
        topk_ids = jnp.argmax(logits, axis=-1)
        topk_val = jnp.max(logits, axis=-1)
        scores = jax.nn.sigmoid(topk_val)[:, None]
        xs = x * scores
        tokens_per_expert = jnp.zeros((E,), jnp.int32).at[topk_ids].add(1)
        order = jnp.argsort(topk_ids)
        sorted_x = xs[order]
        g = _grouped_mm(sorted_x, routed_gate_w, tokens_per_expert)
        u = _grouped_mm(sorted_x, routed_up_w, tokens_per_expert)
        d = _grouped_mm(jax.nn.silu(g) * u, routed_down_w, tokens_per_expert)
        inv = jnp.argsort(order)
        routed_out = d[inv]
        return (shared_out + routed_out).reshape(b, s, h)

    def _L2_xattn_ref(x_q, x_kv, wq, bq, wk, bk, wv, bv, wo, bo):
        import jax, jax.numpy as jnp
        import numpy as np
        B, SQ, SKV, D, H = (2, 256, 256, 128, 16)
        HD = D // H
        ROPE_BASE = 10000.0

        def _rope_interleaved(x):
            s, hd = (x.shape[1], x.shape[-1])
            dim = hd // 2
            freqs = jnp.exp(-jnp.arange(dim, dtype=x.dtype) * jnp.log(jnp.asarray(ROPE_BASE, x.dtype)) / dim)
            ang = jnp.arange(s, dtype=x.dtype)[:, None] * freqs[None, :]
            cos = jnp.cos(ang)[None, :, None, :]
            sin = jnp.sin(ang)[None, :, None, :]
            xe, xo = (x[..., ::2], x[..., 1::2])
            re = xe * cos - xo * sin
            ro = xe * sin + xo * cos
            return jnp.stack([re, ro], axis=-1).reshape(x.shape)
        b, sq, _ = x_q.shape
        skv = x_kv.shape[1]
        q = (jnp.einsum('bsd,ed->bse', x_q, wq) + bq).reshape(b, sq, H, HD)
        k = (jnp.einsum('bsd,ed->bse', x_kv, wk) + bk).reshape(b, skv, H, HD)
        v = (jnp.einsum('bsd,ed->bse', x_kv, wv) + bv).reshape(b, skv, H, HD)
        q = _rope_interleaved(q)
        k = _rope_interleaved(k)
        scores = jnp.einsum('bqhd,bkhd->bhqk', q, k) / jnp.sqrt(jnp.asarray(HD, q.dtype))
        attn = jax.nn.softmax(scores, axis=-1)
        ctx = jnp.einsum('bhqk,bkhd->bqhd', attn, v).reshape(b, sq, D)
        return jnp.einsum('bsd,ed->bse', ctx, wo) + bo

    def _L2_ffn_ref(X, g1, g2, Wq, Wkc, Wvc, Wo, Wr, expert_bias, sW1, sW2, sW3, eW1, eW2, eW3):
        import jax, jax.numpy as jnp
        import numpy as np
        D_MODEL = 128
        NUM_HEADS = 4
        NUM_EXPERTS = 8
        TOP_K = 2
        D_FF = 128
        EPS = 1e-06

        def _rmsnorm(x, g):
            return x * jax.lax.rsqrt(jnp.mean(x * x, axis=-1, keepdims=True) + EPS) * g

        def _swiglu(x, w1, w2, w3):
            return jax.nn.silu(x @ w1.T) * (x @ w3.T) @ w2.T
        B, S, d = X.shape
        H = NUM_HEADS
        dk = d // H
        scale = 1.0 / jnp.sqrt(jnp.float32(dk))
        nx = _rmsnorm(X, g1)
        Q = (nx @ Wq.T).reshape(B, S, H, dk).transpose(0, 2, 1, 3)
        Kc = nx @ Wkc.T
        Vc = nx @ Wvc.T
        scores = jnp.einsum('bhsd,btd->bhst', Q, Kc) * scale
        attn = jax.nn.softmax(scores, axis=-1)
        out = jnp.einsum('bhst,btd->bhsd', attn, Vc)
        out = out.transpose(0, 2, 1, 3).reshape(B, S, d) @ Wo.T
        X = X + out
        nx = _rmsnorm(X, g2)
        xf = nx.reshape(-1, d)
        logits = xf @ Wr.T + expert_bias
        rw = jax.nn.softmax(logits, axis=-1)
        topw, topi = jax.lax.top_k(rw, TOP_K)
        topw = jax.nn.softmax(topw, axis=-1)
        combine = jnp.sum(jax.nn.one_hot(topi, NUM_EXPERTS, dtype=xf.dtype) * topw[..., None], axis=1)
        shared = _swiglu(xf, sW1, sW2, sW3)
        h = jax.nn.silu(jnp.einsum('td,efd->etf', xf, eW1)) * jnp.einsum('td,efd->etf', xf, eW3)
        eo = jnp.einsum('etf,edf->etd', h, eW2)
        specialist = jnp.einsum('te,etd->td', combine, eo)
        moe_out = (shared + specialist).reshape(B, S, d)
        return X + moe_out

    def _L3_xattn_ref(query, context, Wq, Wkv, Wout, mask):
        import jax, jax.numpy as jnp
        import numpy as np
        B, S, D, H = (2, 256, 128, 16)
        A = D // H
        NEG = -1000000000.0
        b, q_len, d = query.shape
        c_len = context.shape[1]
        h, a = (H, A)
        scale = 1.0 / np.sqrt(d)
        q = query @ Wq.T
        kv = context @ Wkv.T
        k, v = jnp.split(kv, 2, axis=-1)
        q = q.reshape(b, q_len, h, a)
        k = k.reshape(b, c_len, h, a)
        v = v.reshape(b, c_len, h, a)
        scores = jnp.einsum('bqha,bkha->bqkh', q, k)
        scores = scores + mask[None, :, :, None]
        attn = jax.nn.softmax(scores * scale, axis=2)
        out = jnp.einsum('bqkh,bkha->bqha', attn, v).reshape(b, q_len, d)
        return out @ Wout.T

    def _L3_ffn_ref(input_features, centroids, ln_g, ln_b, w1, b1, w2, b2):
        import jax, jax.numpy as jnp
        import numpy as np
        B, S, D, F, E = (8, 128, 128, 512, 8)
        EPS = 1e-05
        x = input_features.reshape(-1, D)
        aff = jax.lax.stop_gradient(x @ centroids.T)
        eid = jnp.argmax(aff, axis=-1)
        alpha = jax.nn.sigmoid(jnp.sum(x * centroids[eid], axis=-1, keepdims=True))
        mu = jnp.mean(x, axis=-1, keepdims=True)
        var = jnp.mean((x - mu) ** 2, axis=-1, keepdims=True)
        xn = (x - mu) * jax.lax.rsqrt(var + EPS)
        xln = xn * ln_g[eid] + ln_b[eid]
        onehot = jax.nn.one_hot(eid, E, dtype=x.dtype)
        ffn = jnp.zeros_like(x)
        for e in range(E):
            h = jax.nn.relu(xln @ w1[e] + b1[e])
            ffn = ffn + onehot[:, e:e + 1] * (h @ w2[e] + b2[e])
        out = x + alpha * ffn
        return out.reshape(input_features.shape)
    x = x + _L0_xattn_ref(ctx_1024, _layernorm(x, axis=-1), mask_BxSxS2_ik0, L0_xattn_W_kv, L0_xattn_b_kv, L0_xattn_W_q, L0_xattn_b_q, L0_xattn_W_o, L0_xattn_b_o)
    x = x + _L0_ffn_ref(_layernorm(x, axis=-1), L0_ffn_centroids, L0_ffn_expert_biases, L0_ffn_Wr, L0_ffn_br, L0_ffn_Ws, L0_ffn_bs)
    x = x + _L1_xattn_ref(_layernorm(x, axis=-1), ctx_1024, L1_xattn_ln_gamma, L1_xattn_ln_beta, L1_xattn_w_q, L1_xattn_w_kv, L1_xattn_w_out, L1_xattn_b_out, L1_xattn_gate)
    x = x + _L1_ffn_ref(_layernorm(x, axis=-1), L1_ffn_gate_w, L1_ffn_shared_gate_w, L1_ffn_shared_up_w, L1_ffn_shared_down_w, L1_ffn_routed_gate_w, L1_ffn_routed_up_w, L1_ffn_routed_down_w)
    x = x + _L2_xattn_ref(_layernorm(x, axis=-1), ctx_1024, L2_xattn_wq, L2_xattn_bq, L2_xattn_wk, L2_xattn_bk, L2_xattn_wv, L2_xattn_bv, L2_xattn_wo, L2_xattn_bo)
    x = x + _L2_ffn_ref(_layernorm(x, axis=-1), L2_ffn_g1, L2_ffn_g2, L2_ffn_Wq, L2_ffn_Wkc, L2_ffn_Wvc, L2_ffn_Wo, L2_ffn_Wr, L2_ffn_expert_bias, L2_ffn_sW1, L2_ffn_sW2, L2_ffn_sW3, L2_ffn_eW1, L2_ffn_eW2, L2_ffn_eW3)
    x = x + _L3_xattn_ref(_layernorm(x, axis=-1), ctx_1024, L3_xattn_Wq, L3_xattn_Wkv, L3_xattn_Wout, mask_SxS2_fk0)
    x = x + _L3_ffn_ref(_layernorm(x, axis=-1), L3_ffn_centroids, L3_ffn_ln_g, L3_ffn_ln_b, L3_ffn_w1, L3_ffn_b1, L3_ffn_w2, L3_ffn_b2)
    return x

_drawn_inputs = setup_inputs


def setup_inputs(seed=0):
    import zlib

    import numpy as np

    out = dict(_drawn_inputs(seed))
    spreads = {'L0_xattn_b_kv': (0.0, 0.1),
     'L0_xattn_b_q': (0.0, 0.8),
     'L0_xattn_b_o': (0.0, 0.1),
     'L0_ffn_expert_biases': (0.0, 0.8),
     'L1_xattn_ln_gamma': (1.0, 0.6),
     'L1_xattn_ln_beta': (0.0, 0.8),
     'L1_xattn_b_out': (0.0, 0.367),
     'L2_xattn_bq': (0.0, 0.759),
     'L2_xattn_bk': (0.0, 0.8),
     'L2_xattn_bv': (0.0, 0.1),
     'L2_xattn_bo': (0.0, 0.1),
     'L2_ffn_g1': (1.0, 0.6),
     'L2_ffn_g2': (1.0, 0.6),
     'L2_ffn_expert_bias': (0.0, 0.8),
     'L3_ffn_ln_g': (1.0, 0.6),
     'L3_ffn_ln_b': (0.0, 0.8),
     'L3_ffn_b1': (0.0, 0.8),
     'L3_ffn_b2': (0.0, 1.289)}
    factors = {'L0_xattn_W_q': 8.0,
     'L0_ffn_br': 8.0,
     'L0_ffn_bs': 8.0,
     'L1_ffn_gate_w': 8.0,
     'L1_ffn_shared_gate_w': 8.0,
     'L1_ffn_shared_up_w': 8.0,
     'L1_ffn_shared_down_w': 8.0,
     'L1_ffn_routed_gate_w': 8.0,
     'L1_ffn_routed_up_w': 8.0,
     'L1_ffn_routed_down_w': 8.0,
     'L2_ffn_Wq': 8.0,
     'L2_ffn_Wkc': 8.0,
     'L2_ffn_Wvc': 8.0,
     'L2_ffn_Wo': 8.0,
     'L2_ffn_Wr': 8.0,
     'L2_ffn_sW1': 8.0,
     'L2_ffn_sW2': 8.0,
     'L2_ffn_sW3': 8.0,
     'L2_ffn_eW1': 8.0,
     'L2_ffn_eW2': 8.0,
     'L2_ffn_eW3': 8.0,
     'L3_ffn_w1': 4.826,
     'L3_ffn_w2': 3.834,
     'L3_xattn_Wq': 4.031}
    for name, (base, spread) in spreads.items():
        noise = np.random.default_rng([zlib.crc32(name.encode()), seed]).standard_normal(out[name].shape)
        drawn = base * np.exp(spread * noise) if base else spread * noise
        out[name] = jnp.asarray(drawn.astype(out[name].dtype))
    for name, factor in factors.items():
        out[name] = (out[name] * factor).astype(out[name].dtype)
    return out
```

```python
from contextlib import ExitStack

import numpy as np
import concourse.bass as bass
from concourse import mybir

F32 = mybir.dt.float32
BF16 = mybir.dt.bfloat16
I32 = mybir.dt.int32
U32 = mybir.dt.uint32
ALU = mybir.AluOpType
ACT = mybir.ActivationFunctionType
X = mybir.AxisListType.X

P = 128
B, S, D = 4, 256, 128
SC = 64
TILES = B * S // P
H = 16
BANK = 512
BIG = -1e20

CONSTS = [("ident", 128), ("count_ge", 128), ("ones", 128), ("headmask16", 16), ("headmask4", 4), ("headmask2", 2),
          ("cosq", 256), ("sinq", 256), ("rot", 128), ("expdesc", 32), ("token_at", 8), ("tile_end", 7),
          ("expert_at", 32), ("step_at", 40), ("neghalf", 8)]
PATTERNS = [("i64rep", 512), ("neghead16", 1024), ("neghead4", 1024), ("neghead8", 512)]
L0A = [("a0wk", 128), ("a0wv", 128), ("a0wq", 128), ("a0wo", 128), ("a0bv", 128), ("a0bo", 128),
       ("a0bk", 1), ("a0bq", 1)]
L0F = [("f0wr", 2048), ("f0ws", 256), ("f0cent", 16), ("f0eb", 16), ("f0br", 128)]
L1A = [("a1wk", 1024), ("a1wv", 1024), ("a1wq", 1024), ("a1wo", 1024), ("a1bo", 128), ("a1g", 128),
       ("a1b", 128), ("a1gate", 1)]
L1S = [("f1gw", 32), ("f1sgu", 512), ("f1sd", 256)]
L2A = [("a2wk", 128), ("a2wv", 128), ("a2wq", 128), ("a2wo", 128), ("a2bv", 128), ("a2bo", 128),
       ("a2bk", 1), ("a2bq", 1)]
L2F = [("f2g1", 128), ("f2g2", 128), ("f2wq", 128), ("f2wkc", 128), ("f2wvc", 32), ("f2wo", 128), ("f2wr", 8),
       ("f2eb", 8), ("f2w1", 1152), ("f2w3", 1152), ("f2w2", 1152)]
L3A = [("a3wk", 128), ("a3wv", 128), ("a3wq", 128), ("a3wo", 128), ("f3cent", 8), ("f3g", 8), ("f3b", 8),
       ("f3b1", 32), ("f3b2", 1024)]
L1M = 32 * 768
L3M = 8 * 1024
EARLY = 28 * 768
WORK = 11008
GROUPS = [("consts", CONSTS), ("patterns", PATTERNS), ("l0a", L0A), ("l0f", L0F), ("l1a", L1A), ("l1s", L1S),
          ("l2a", L2A), ("l2f", L2F), ("l3a", L3A)]


def words(group):
    return sum(n for _, n in group)


class Signal:

    def __init__(self, handle):
        self.handle, self.done = handle, 0


class Program:
    def __init__(self, nc, ctx, dram):
        self.nc, self.ctx, self.dram, self.signals = nc, ctx, dram, {}

        def sb(name, n, dt=F32):
            return ctx.enter_context(nc.sbuf_tensor(name, [P, n], dt))

        self.sb = sb
        self.c = {}
        self.loads = []
        self.work = sb("work", WORK)
        self.wmoe = sb("wmoe", L1M)
        late = L3M
        for name, group in GROUPS:
            if name == "patterns":
                t = self.work[:, 0:words(group)]
            elif name == "l0f":
                t = self.wmoe[:, EARLY:EARLY + words(group)]
            elif name in ("l2a", "l2f", "l3a"):
                t = self.wmoe[:, late:late + words(group)]
                late += words(group)
            else:
                t = sb(name, words(group))[:, :]
            at = 0
            for part, n in group:
                self.c[part] = t[:, at:at + n]
                at += n
            self.loads.append((name, t))
        self.x = sb("x", 1024)
        self.xn = sb("xn", 1024)
        self.xnT = sb("xnT", 1024)
        self.ctxn = sb("ctxn", 256)
        self.ctxT = sb("ctxT", 512)
        self.small = sb("small", 2048)
        self.maskT0 = self.work[:, 4096:5120].bitcast(I32)
        self.maskT3 = self.work[:, 5120:5376]
        self.mb = sb("mb", 1024, BF16)
        self.mb3 = sb("mb3", 768, BF16)
        self.i64 = sb("i64", 512, BF16)
        self.i64big = sb("i64big", 512, BF16)
        self.nh = {16: sb("nh16", 1024, BF16), 4: sb("nh4", 1024, BF16), 8: sb("nh8", 512, BF16)}
        self.identb = sb("identb", 128, BF16)
        self.ps = ctx.enter_context(nc.psum_tensor("ps", [P, 8, BANK], F32))
        self.load_sem = {}
        for name in ["x", "ctx", "mask"] + [n for n, _ in self.loads] + ["moe1", "moe1b", "moe3"]:
            self.load_sem[name] = ctx.enter_context(nc.semaphore(f"loaded_{name}"))

    def sig(self, name):
        if name not in self.signals:
            self.signals[name] = Signal(self.ctx.enter_context(self.nc.semaphore(name)))
        return self.signals[name]

    def tiles(self, t):
        return t[:, 0:1024].rearrange("p (t d) -> p t d", d=P)


def start_loads(k):
    with k.nc.Block() as block:
        @block.sync
        def _(sp):
            order = dict(k.loads)
            sp.dma_start(order["consts"], k.dram["consts"]).then_inc(k.load_sem["consts"], 16)
            sp.dma_start(order["patterns"], k.dram["patterns"]).then_inc(k.load_sem["patterns"], 16)
            sp.dma_start(k.x[:, :], k.dram["x"]).then_inc(k.load_sem["x"], 16)
            sp.dma_start(k.ctxn[:, :], k.dram["ctx"]).then_inc(k.load_sem["ctx"], 16)
            sp.dma_start(order["l0a"], k.dram["l0a"]).then_inc(k.load_sem["l0a"], 16)
            sp.dma_start(k.maskT0[0:SC, :], k.dram["mask0"]).then_inc(k.load_sem["mask"], 16)
            sp.dma_start(k.maskT3[0:SC, :], k.dram["mask3"]).then_inc(k.load_sem["mask"], 16)
            for name in ("l0f", "l1a", "l1s"):
                sp.dma_start(order[name], k.dram[name]).then_inc(k.load_sem[name], 16)
            sp.dma_start(k.wmoe[:, 0:EARLY], k.dram["moe1"][:, 0:EARLY]).then_inc(k.load_sem["moe1"], 16)


def constants(k):
    c = k.c
    cast, split, turned = k.sig("cast"), k.sig("split"), k.sig("turned")
    with k.nc.Block() as block:
        @block.vector
        def _(dve):
            dve.wait_ge(k.load_sem["consts"], 16)
            dve.tensor_copy(k.i64[:, :], c["i64rep"])
            dve.tensor_scalar(k.i64big[:, :], c["i64rep"], BIG, None, ALU.mult)
            dve.tensor_copy(k.nh[16][:, :], c["neghead16"])
            dve.tensor_copy(k.nh[4][:, :], c["neghead4"])
            dve.tensor_copy(k.nh[8][:, :], c["neghead8"])
            dve.tensor_copy(k.identb[:, :], c["ident"])
            dve.wait_ge(k.load_sem["mask"], 32)
            dve.tensor_scalar(k.mb[0:SC, :], k.maskT0[0:SC, :], 0.0, None, ALU.is_equal)
            rest = k.small[0:SC, 0:256]
            dve.tensor_copy(k.mb3[0:SC, 0:256], k.maskT3[0:SC, :]).then_inc(split.handle, 1)
            dve.wait_ge(split.handle, split.done + 1)
            dve.tensor_tensor(rest, k.maskT3[0:SC, :], k.mb3[0:SC, 0:256], ALU.subtract).then_inc(split.handle, 1)
            dve.wait_ge(split.handle, split.done + 2)
            dve.tensor_copy(k.mb3[0:SC, 256:512], rest).then_inc(split.handle, 1)
            dve.wait_ge(split.handle, split.done + 3)
            dve.tensor_tensor(k.mb3[0:SC, 512:768], rest, k.mb3[0:SC, 256:512], ALU.subtract)

        @block.tensor
        def _(pe):
            pe.wait_ge(k.load_sem["consts"], 16)
            pe.wait_ge(k.load_sem["ctx"], 16)
            for i in range(2):
                pe.transpose(k.ps[:, 0, i * P:(i + 1) * P], k.ctxn[:, i * P:(i + 1) * P],
                             c["ident"]).then_inc(turned.handle, 1)

        @block.scalar
        def _(act):
            act.wait_ge(turned.handle, turned.done + 2)
            v = k.ctxT[:, :].rearrange("p (b two s) -> p b two s", b=B, two=2)
            for i in range(2):
                act.activation(v[:, :, i, :], k.ps[:, 0, 0:256].rearrange("p (b s) -> p b s", b=B), ACT.Copy)
    split.done += 3
    turned.done += 2


def layernorm(k, src, dst, eps):
    nc = k.nc
    stats, aggr, var, rstd = k.sig("ln_stats"), k.sig("ln_aggr"), k.sig("ln_var"), k.sig("ln_rstd")
    st = k.small[:, 0:48].rearrange("p (t s) -> p t s", s=6)
    mv = k.small[:, 48:64].rearrange("p (t s) -> p t s", s=2)
    ve, rs = k.small[:, 64:72], k.small[:, 72:80]
    s3, d3 = k.tiles(src), k.tiles(dst)
    with nc.Block() as block:
        @block.vector
        def _(dve):
            with dve.Fori(0, TILES) as t:
                dve.bn_stats(st[:, t, :], s3[:, t, :]).then_inc(stats.handle, 1)
            dve.wait_ge(stats.handle, stats.done + TILES)
            for t in range(TILES):
                dve.bn_aggr(mv[:, t, :], st[:, t, :]).then_inc(aggr.handle, 1)
            dve.wait_ge(aggr.handle, aggr.done + TILES)
            dve.tensor_scalar(ve, mv[:, :, 1], eps, None, ALU.add).then_inc(var.handle, 1)
            dve.wait_ge(rstd.handle, rstd.done + 1)
            with dve.Fori(0, TILES) as t:
                dve.tensor_scalar(d3[:, t, :], s3[:, t, :], mv[:, t, 0:1], rs[:, bass.ds(t, 1)],
                                  ALU.subtract, ALU.mult)

        @block.gpsimd
        def _(pool):
            pool.wait_ge(var.handle, var.done + 1)
            pool.tensor_tensor(rs, ve, k.c["neghalf"], ALU.pow).then_inc(rstd.handle, 1)
    stats.done += TILES
    aggr.done += TILES
    var.done += 1
    rstd.done += 1


def rmsnorm(k, src, dst, gain, eps):
    nc = k.nc
    step, rstd = k.sig("rms_step"), k.sig("ln_rstd")
    ve, rs = k.small[:, 64:72], k.small[:, 72:80]
    sq = k.tiles(k.work)
    s3, d3 = k.tiles(src), k.tiles(dst)
    with nc.Block() as block:
        @block.vector
        def _(dve):
            dve.tensor_tensor(sq, s3, s3, ALU.mult).then_inc(step.handle, 1)
            dve.wait_ge(step.handle, step.done + 1)
            dve.tensor_reduce(rs, sq, X, ALU.add).then_inc(step.handle, 1)
            dve.wait_ge(step.handle, step.done + 2)
            dve.tensor_scalar(ve, rs, 1.0 / D, eps, ALU.mult, ALU.add).then_inc(step.handle, 1)
            dve.wait_ge(rstd.handle, rstd.done + 1)
            for t in range(TILES):
                dve.scalar_tensor_tensor(d3[:, t, :], s3[:, t, :], rs[:, t:t + 1], gain, ALU.mult, ALU.mult)

        @block.gpsimd
        def _(pool):
            pool.wait_ge(step.handle, step.done + 3)
            pool.tensor_tensor(rs, ve, k.c["neghalf"], ALU.pow).then_inc(rstd.handle, 1)
    step.done += 3
    rstd.done += 1


def affine(k, gain, bias):
    step = k.sig("affine_step")
    x3 = k.tiles(k.xn)
    with k.nc.Block() as block:
        @block.vector
        def _(dve):
            dve.tensor_tensor(x3, x3, gain[:, None, :].to_broadcast([P, TILES, D]), ALU.mult).then_inc(step.handle, 1)
            dve.wait_ge(step.handle, step.done + 1)
            dve.tensor_tensor(x3, x3, bias[:, None, :].to_broadcast([P, TILES, D]), ALU.add)
    step.done += 1


def turn(k, src, dst):
    turned = k.sig("turned")
    s3 = k.tiles(src)
    with k.nc.Block() as block:
        @block.tensor
        def _(pe):
            for t in range(TILES):
                pe.transpose(k.ps[:, t // 4, (t % 4) * P:(t % 4 + 1) * P], s3[:, t, :],
                             k.c["ident"]).then_inc(turned.handle, 1)

        @block.scalar
        def _(act):
            act.wait_ge(turned.handle, turned.done + 4)
            act.activation(dst[:, 0:512], k.ps[:, 0, :], ACT.Copy)

        @block.vector
        def _(dve):
            dve.wait_ge(turned.handle, turned.done + 8)
            dve.tensor_copy(dst[:, 512:1024], k.ps[:, 1, :])
    turned.done += TILES


def add_rows(k, dst, row, also=None):
    step = k.sig("addrow")
    d3 = k.tiles(dst)
    with k.nc.Block() as block:
        @block.gpsimd
        def _(pool):
            if row is not None:
                pool.tensor_tensor(d3, d3, row[:, None, :].to_broadcast([P, TILES, D]), ALU.add).then_inc(step.handle, 1)
                pool.wait_ge(step.handle, step.done + 1)
            if also is not None:
                pool.tensor_tensor(d3, d3, k.tiles(also), ALU.add)
    if row is not None:
        step.done += 1


class Core:

    def __init__(self, k, heads, hd, keys):
        self.heads, self.hd, self.keys = heads, hd, keys
        self.ct = heads * keys // P
        self.groups = heads * hd // P
        self.cols = self.ct * P
        w, at = k.work, 0

        def take(n):
            nonlocal at
            at += n
            assert at <= WORK
            return w[:, at - n:at]

        self.qT = take(self.groups * 1024).rearrange("p (b g n) -> p b g n", b=B, g=self.groups)
        self.o = self.qT.rearrange("p b g n -> p (b g n)").rearrange("p (t n) -> p t n", t=TILES)
        self.kblk = take(B * self.cols).rearrange("p (b n) -> p b n", b=B)
        self.probs = take(2 * self.ct * 256).rearrange("p (r j n) -> p r j n", r=2, j=self.ct)
        if keys == SC:
            self.v = take(B * self.ct * 2 * (hd + 1)).rearrange("p (b j c) -> p b j c", b=B, j=self.ct)
        else:
            self.v = take(TILES * (hd + 1)).rearrange("p (t c) -> p t c", t=TILES)
        self.ot = k.small[:, 1024:1024 + 2 * self.groups * P if self.groups == 1 else 2048]
        self.otw = self.groups * P
        self.kT = self.probs.rearrange("p r j n -> p (r j n)")[:, 0:self.groups * 256]
        self.raw = self.probs.rearrange("p r j n -> p (r j n)")[:, 0:1024]

    def group(self, j):
        return j if self.groups > 1 else 0

    def kview(self):
        return self.kblk.rearrange("p b (g h s) -> p b g h s", g=self.groups, s=self.keys)


def project_k(k, a, wk, bk, rope):
    c = k.c
    proj, kept, rot, step = k.sig("k_proj"), k.sig("k_kept"), k.sig("k_rot"), k.sig("k_step")
    ctx = k.ctxT[:, :].rearrange("p (b two s) -> p b two s", b=B, two=2)[:, :, 0, :]
    g = a.groups
    with k.nc.Block() as block:
        @block.tensor
        def _(pe):
            for i in range(g):
                pe.matmul(k.ps[:, i, 0:256], wk[:, i * P:(i + 1) * P], ctx, start=True, stop=True).then_inc(proj.handle, 1)
            if rope:
                pe.wait_ge(kept.handle, kept.done + 1)
                pe.matmul(k.ps[:, 4, 0:256], c["rot"], a.kT, start=True, stop=True).then_inc(rot.handle, 1)

        @block.scalar
        def _(act):
            for i in range(g):
                act.wait_ge(proj.handle, proj.done + i + 1)
                act.activation(a.kT[:, i * 256:(i + 1) * 256], k.ps[:, i, 0:256], ACT.Identity,
                               bias=bk if bk is not None else 0.0).then_inc(kept.handle, 1)

        if rope:
            @block.vector
            def _(dve):
                tmp = k.small[:, 128:384].rearrange("p (b s) -> p b s", b=B)
                kt = a.kT.rearrange("p (b s) -> p b s", b=B)
                sin = c["sinq"][:, None, 0:SC].to_broadcast([P, B, SC])
                cos = c["cosq"][:, None, 0:SC].to_broadcast([P, B, SC])
                dve.wait_ge(rot.handle, rot.done + 1)
                dve.tensor_tensor(tmp, k.ps[:, 4, 0:256].rearrange("p (b s) -> p b s", b=B), sin,
                                  ALU.mult)
                dve.tensor_tensor(kt, kt, cos, ALU.mult).then_inc(step.handle, 1)
                dve.wait_ge(step.handle, step.done + 1)
                dve.tensor_tensor(kt, kt, tmp, ALU.add)
    proj.done += g
    kept.done += g
    if rope:
        rot.done += 1
        step.done += 1
    hm = c["headmask16"] if g == 1 else c["headmask2"]
    hg = a.heads // g
    kv = a.kview()
    kt = a.kT.rearrange("p (g b s) -> p g b s", g=g, b=B)

    def spread(eng, b):
        for i in range(g):
            eng.tensor_tensor(kv[:, b, i], kt[:, i, b, None, :].to_broadcast([P, hg, SC]),
                              hm[:, :, None].to_broadcast([P, hg, SC]), ALU.mult)

    with k.nc.Block() as block:
        @block.vector
        def _(dve):
            for b in range(3):
                spread(dve, b)

        @block.gpsimd
        def _(pool):
            spread(pool, 3)


def project_v(k, a, wv, bv):
    proj, cleared = k.sig("v_proj"), k.sig("v_cleared")
    hd, half = a.hd, a.ct
    n = a.heads * hd
    ctx = k.ctxT[:, :].rearrange("p (b n) -> p b n", b=B)
    with k.nc.Block() as block:
        @block.gpsimd
        def _(pool):
            pool.memset(a.v, 0.0).then_inc(cleared.handle, 1)

        @block.tensor
        def _(pe):
            for b in range(B):
                pe.matmul(k.ps[:, b, 0:n], ctx[:, b, :], wv, start=True, stop=True).then_inc(proj.handle, 1)

        @block.vector
        def _(dve):
            dve.wait_ge(cleared.handle, cleared.done + 1)
            for par in range(2):
                rows = slice(64 * par, 64 * par + 64)
                at = par * (hd + 1)
                dve.memset(a.v[rows, :, :, at + hd:at + hd + 1], 1.0)
                for b in range(B):
                    dve.wait_ge(proj.handle, proj.done + b + 1)
                    src = k.ps[rows, b, 0:n].rearrange("p (j two d) -> p j two d", two=2, d=hd)[:, :, par, :]
                    dst = a.v[rows, b, :, at:at + hd]
                    if bv is None:
                        dve.tensor_copy(dst, src)
                    else:
                        dve.tensor_tensor(dst, src, bv[rows, :].rearrange("p (j two d) -> p j two d", two=2, d=hd)[:, :, par, :],
                                          ALU.add)
    cleared.done += 1
    proj.done += B


def project_q(k, a, wq, bq, rope):
    c = k.c
    proj, kept, rot, step = k.sig("q_proj"), k.sig("q_kept"), k.sig("q_rot"), k.sig("q_step")
    g = a.groups
    halves = [[a.raw[:, h * 512:(h + 1) * 512].rearrange("p (b s) -> p b s", s=S) if rope
               else a.qT[:, 2 * h:2 * h + 2, i, :] for h in range(2)] for i in range(g)]
    with k.nc.Block() as block:
        @block.tensor
        def _(pe):
            for i in range(g):
                for h in range(2):
                    pe.matmul(k.ps[:, 2 * i + h, :], wq[:, i * P:(i + 1) * P], k.xnT[:, h * 512:(h + 1) * 512],
                              start=True, stop=True).then_inc(proj.handle, 1)
            if rope:
                for h in range(2):
                    pe.wait_ge(kept.handle, kept.done + h + 1)
                    pe.matmul(k.ps[:, 4 + h, :], c["rot"], a.raw[:, h * 512:(h + 1) * 512],
                              start=True, stop=True).then_inc(rot.handle, 1)

        @block.scalar
        def _(act):
            for i in range(g):
                for h in range(2):
                    act.wait_ge(proj.handle, proj.done + 2 * i + h + 1)
                    act.activation(halves[i][h], k.ps[:, 2 * i + h, :].rearrange("p (b s) -> p b s", s=S), ACT.Identity,
                                   bias=bq if bq is not None else 0.0).then_inc(kept.handle, 1)

        if rope:
            @block.vector
            def _(dve):
                sin = c["sinq"][:, None, :].to_broadcast([P, 2, S])
                cos = c["cosq"][:, None, :].to_broadcast([P, 2, S])
                tmp = k.small[:, 0:512].rearrange("p (b s) -> p b s", s=S)
                for h in range(2):
                    q = a.qT[:, 2 * h:2 * h + 2, 0, :]
                    r = a.raw[:, h * 512:(h + 1) * 512].rearrange("p (b s) -> p b s", s=S)
                    dve.wait_ge(kept.handle, kept.done + h + 1)
                    dve.tensor_tensor(q, r, cos, ALU.mult)
                    dve.wait_ge(rot.handle, rot.done + h + 1)
                    if h:
                        dve.wait_ge(step.handle, step.done + 2 * h)
                    dve.tensor_tensor(tmp, k.ps[:, 4 + h, :].rearrange("p (b s) -> p b s", s=S), sin,
                                      ALU.mult).then_inc(step.handle, 1)
                    dve.wait_ge(step.handle, step.done + 2 * h + 1)
                    dve.tensor_tensor(q, q, tmp, ALU.add).then_inc(step.handle, 1)
    proj.done += 2 * g
    kept.done += 2 * g
    if rope:
        rot.done += 2
        step.done += 4


def attend(k, a, mask, scale, wo, dst):
    nc, c = k.nc, k.c
    ct, cols, heads, hd = a.ct, a.cols, a.heads, a.hd
    banks = cols // BANK
    scored, topped = k.sig("scored"), k.sig("topped")
    mx = k.small[:, 0:TILES * heads]
    mx3 = mx.rearrange("p (t h) -> p t h", h=heads)
    slots = 4
    with nc.Block() as block:
        @block.tensor
        def _(pe):
            for t in range(TILES):
                if t >= slots:
                    pe.wait_ge(topped.handle, topped.done + t - slots + 1)
                tok = slice(t % 2 * P, (t % 2 + 1) * P)
                for n in range(banks):
                    out = k.ps[:, banks * (t % slots) + n, :]
                    if a.groups == 1:
                        ins = pe.matmul(out, a.qT[:, t // 2, 0, tok], a.kblk[:, t // 2, n * BANK:(n + 1) * BANK],
                                  start=True, stop=not mask)
                        for m, (by_key, ident) in enumerate(mask):
                            ins = pe.matmul(out, by_key(t // 2, t % 2 * P, P), ident, start=False,
                                            stop=m == len(mask) - 1)
                    else:
                        for j in range(4):
                            ins = pe.matmul(out[:, j * P:(j + 1) * P], a.qT[:, t // 2, j, tok],
                                            a.kblk[:, t // 2, j * P:(j + 1) * P], start=True, stop=True)
                ins.then_inc(scored.handle, 1)

        @block.vector
        def _(dve):
            for t in range(TILES):
                dve.wait_ge(scored.handle, scored.done + t + 1)
                b0 = banks * (t % slots)
                dve.tensor_reduce(mx3[:, t, :], k.ps[:, b0:b0 + banks, :].rearrange("p b (h s) -> p (b h) s", s=a.keys),
                                  X, ALU.max).then_inc(topped.handle, 1)
    scored.done += TILES
    topped.done += TILES

    step, turned = k.sig("max_step"), k.sig("turned")
    rest = k.small[:, 128:128 + TILES * heads].rearrange("p (t h) -> p t h", h=heads)
    parts = k.mparts[:, 0:TILES * 3 * heads].rearrange("p (t q h) -> p t q h", q=3, h=heads)
    mT = k.mT[0:3 * heads, :]
    psb = k.ps[:, 0:2, :].rearrange("p b n -> p (b n)").bitcast(BF16)
    with nc.Block() as block:
        @block.vector
        def _(dve):
            dve.tensor_copy(parts[:, :, 0, :], mx3).then_inc(step.handle, 1)
            dve.wait_ge(step.handle, step.done + 1)
            dve.tensor_tensor(rest, mx3, parts[:, :, 0, :], ALU.subtract).then_inc(step.handle, 1)
            dve.wait_ge(step.handle, step.done + 2)
            dve.tensor_copy(parts[:, :, 1, :], rest).then_inc(step.handle, 1)
            dve.wait_ge(step.handle, step.done + 3)
            dve.tensor_tensor(parts[:, :, 2, :], rest, parts[:, :, 1, :], ALU.subtract).then_inc(step.handle, 1)
            dve.wait_ge(turned.handle, turned.done + TILES)
            dve.tensor_copy(mT[:, :], psb[0:3 * heads, 0:1024])

        @block.tensor
        def _(pe):
            pe.wait_ge(step.handle, step.done + 4)
            for t in range(TILES):
                pe.transpose(psb[0:3 * heads, t * P:(t + 1) * P], parts[:, t].rearrange("p q h -> p (q h)"),
                             k.identb[:, :]).then_inc(turned.handle, 1)
    step.done += 4
    turned.done += TILES

    made, expd, summed, freed, recipd = (k.sig("st_made"), k.sig("expd"), k.sig("pv_done"), k.sig("o_done"),
                                         k.sig("recipd"))
    pairs = ct // 2
    nh = k.nh[heads]
    if a.keys == SC:
        vw = 2 * (hd + 1)
        per = min(ct, BANK // vw // 2 * 2) if hd == 64 else ct
        per = 2 if hd == 64 else ct
        vcols = per * vw
    else:
        per, vcols = ct, heads * (hd + 1)
    obanks = ct // per
    with nc.Block() as block:
        @block.tensor
        def _(pe):
            for b in range(B + 1):
                if b < B:
                    for i in range(pairs):
                        n = b * pairs + i
                        if n >= 4:
                            pe.wait_ge(expd.handle, expd.done + n - 3)
                        for jj in range(2):
                            j = 2 * i + jj
                            out = k.ps[:, n % 4, jj * 256:(jj + 1) * 256]
                            pe.matmul(out, a.kblk[:, b, j * P:(j + 1) * P], a.qT[:, b, a.group(j), :],
                                      start=True, stop=False)
                            for by_key, ident in mask:
                                pe.matmul(out, ident[:, 0:P], by_key(b, 0, S), start=False, stop=False)
                            ins = pe.matmul(out, nh[0:3 * heads, j * P:(j + 1) * P], mT[:, b * S:(b + 1) * S],
                                            start=False, stop=True)
                        ins.then_inc(made.handle, 1)
                if b >= 1:
                    c0 = b - 1
                    pe.wait_ge(expd.handle, expd.done + pairs * b)
                    for tl in range(2):
                        t = 2 * c0 + tl
                        if t >= 2:
                            pe.wait_ge(freed.handle, freed.done + t - 1)
                        for j in range(ct):
                            lhs = a.probs[:, c0 % 2, j, tl * P:(tl + 1) * P]
                            bank = 4 + (t % 2) * obanks + j // per
                            if a.keys == SC:
                                ins = pe.matmul(k.ps[:, bank, (j % per) * vw:(j % per + 1) * vw], lhs,
                                                a.v[:, c0, j, :], start=True, stop=True)
                            else:
                                ins = pe.matmul(k.ps[:, bank, j // 2 * (hd + 1):(j // 2 + 1) * (hd + 1)], lhs,
                                                a.v[:, 2 * c0 + j % 2, :], start=j % 2 == 0, stop=j % 2 == 1)
                        ins.then_inc(summed.handle, 1)

        @block.scalar
        def _(act):
            for b in range(B):
                if b >= 2:
                    act.wait_ge(summed.handle, summed.done + 2 * (b - 1))
                for i in range(pairs):
                    n = b * pairs + i
                    act.wait_ge(made.handle, made.done + n + 1)
                    act.activation(a.probs[:, b % 2, 2 * i:2 * i + 2, :],
                                   k.ps[:, n % 4, :].rearrange("p (j n) -> p j n", j=2), ACT.Exp,
                                   scale=scale).then_inc(expd.handle, 1)

        @block.vector
        def _(dve):
            rec = k.small[:, 256:256 + 2 * heads]
            for t in range(TILES):
                dve.wait_ge(summed.handle, summed.done + t + 1)
                b0 = 4 + (t % 2) * obanks
                hb = heads // obanks
                acc = k.ps[:, b0:b0 + obanks, 0:vcols].rearrange("p b (h c) -> p b h c", c=hd + 1)
                r = rec[:, (t % 2) * heads:(t % 2 + 1) * heads].rearrange("p (b h o) -> p b h o", b=obanks, o=1)
                if obanks == 1:
                    acc, r = acc[:, 0], r[:, 0]
                    out = a.o[:, t, :].rearrange("p (h c) -> p h c", c=hd)
                    parts_ = [(acc, r, out, [P, heads, hd])]
                else:
                    out = a.o[:, t, :].rearrange("p (b h c) -> p b h c", b=obanks, c=hd)
                    parts_ = [(acc[:, i], r[:, i], out[:, i], [P, hb, hd]) for i in range(obanks)]
                for n_, (pa, pr, po, shape) in enumerate(parts_):
                    dve.reciprocal(pr, pa[:, :, hd:hd + 1]).then_inc(recipd.handle, 1)
                    dve.wait_ge(recipd.handle, recipd.done + t * obanks + n_ + 1)
                    ins = dve.tensor_tensor(po, pa[:, :, 0:hd], pr.to_broadcast(shape), ALU.mult)
                ins.then_inc(freed.handle, 1)
    made.done += B * pairs
    expd.done += B * pairs
    summed.done += TILES
    freed.done += TILES
    recipd.done += TILES * obanks

    kept, out_made, added = k.sig("ot_kept"), k.sig("wo_made"), k.sig("wo_added")
    g = a.groups
    d3 = k.tiles(dst)
    with nc.Block() as block:
        @block.tensor
        def _(pe):
            for t in range(TILES + 1):
                if t < TILES:
                    if t >= 2:
                        pe.wait_ge(kept.handle, kept.done + t - 1)
                    for i in range(g):
                        ins = pe.transpose(k.ps[:, t % 2, i * P:(i + 1) * P], a.o[:, t, i * P:(i + 1) * P], c["ident"])
                    ins.then_inc(turned.handle, 1)
                if t >= 1:
                    u = t - 1
                    pe.wait_ge(kept.handle, kept.done + u + 1)
                    if u >= 2:
                        pe.wait_ge(added.handle, added.done + u - 1)
                    for i in range(g):
                        ins = pe.matmul(k.ps[:, 2 + u % 2, 0:P], a.ot[:, (u % 2) * a.otw + i * P:(u % 2) * a.otw + (i + 1) * P],
                                        wo[:, i * P:(i + 1) * P], start=i == 0, stop=i == g - 1)
                    ins.then_inc(out_made.handle, 1)

        @block.scalar
        def _(act):
            for t in range(TILES):
                act.wait_ge(turned.handle, turned.done + t + 1)
                if t >= 2:
                    act.wait_ge(out_made.handle, out_made.done + t - 1)
                act.activation(a.ot[:, (t % 2) * a.otw:(t % 2 + 1) * a.otw], k.ps[:, t % 2, 0:a.otw],
                               ACT.Copy).then_inc(kept.handle, 1)

        @block.vector
        def _(dve):
            for t in range(TILES):
                dve.wait_ge(out_made.handle, out_made.done + t + 1)
                dve.tensor_tensor(d3[:, t, :], k.ps[:, 2 + t % 2, 0:P], d3[:, t, :], ALU.add).then_inc(added.handle, 1)
    turned.done += TILES
    kept.done += TILES
    out_made.done += TILES
    added.done += TILES


def first_argmax(dve, step, n, val, top, hot, tmp, desc, e):
    shape = [P, TILES, e]
    d = desc[:, None, 0:e].to_broadcast(shape)
    dve.tensor_reduce(top, val, X, ALU.max).then_inc(step, 1)
    dve.wait_ge(step, n + 1)
    dve.tensor_tensor(hot, val, top[:, :, None].to_broadcast(shape), ALU.is_equal).then_inc(step, 1)
    dve.wait_ge(step, n + 2)
    dve.tensor_tensor(hot, hot, d, ALU.mult).then_inc(step, 1)
    dve.wait_ge(step, n + 3)
    dve.tensor_reduce(tmp, hot, X, ALU.max).then_inc(step, 1)
    dve.wait_ge(step, n + 4)
    dve.tensor_tensor(hot, tmp[:, :, None].to_broadcast(shape), d, ALU.is_equal).then_inc(step, 1)
    dve.wait_ge(step, n + 5)
    return n + 5


def logits(k, w, e, dst):
    made = k.sig("logits_made")
    with k.nc.Block() as block:
        @block.tensor
        def _(pe):
            for t in range(TILES):
                ins = pe.matmul(k.ps[:, 0, t * e:(t + 1) * e], k.xnT[:, t * P:(t + 1) * P], w, start=True, stop=True)
            ins.then_inc(made.handle, 1)

        @block.scalar
        def _(act):
            act.wait_ge(made.handle, made.done + 1)
            act.activation(dst, k.ps[:, 0, 0:TILES * e], ACT.Copy)
    made.done += 1


def softmax_top2(k, lg, e, bias, hot1, hot2, p1, p2, scratch):
    step, expd = k.sig("gate_step"), k.sig("gate_exp")
    v = lg.rearrange("p (t e) -> p t e", e=e)
    shape = [P, TILES, e]
    tmp, rest = scratch[:, 0:8], scratch[:, 8:8 + TILES * e].rearrange("p (t e) -> p t e", e=e)
    n0 = step.done
    with k.nc.Block() as block:
        @block.vector
        def _(dve):
            s = step.handle
            dve.tensor_tensor(v, v, bias[:, None, :].to_broadcast(shape), ALU.add).then_inc(s, 1)
            dve.wait_ge(s, n0 + 1)
            dve.tensor_reduce(tmp, v, X, ALU.max).then_inc(s, 1)
            dve.wait_ge(s, n0 + 2)
            dve.tensor_tensor(v, v, tmp[:, :, None].to_broadcast(shape), ALU.subtract).then_inc(s, 1)
            dve.wait_ge(expd.handle, expd.done + 1)
            dve.tensor_reduce(tmp, v, X, ALU.add).then_inc(s, 1)
            dve.wait_ge(s, n0 + 4)
            dve.reciprocal(tmp, tmp).then_inc(s, 1)
            dve.wait_ge(s, n0 + 5)
            dve.tensor_tensor(v, v, tmp[:, :, None].to_broadcast(shape), ALU.mult).then_inc(s, 1)
            dve.wait_ge(s, n0 + 6)
            n = first_argmax(dve, s, n0 + 6, v, p1, hot1, tmp, k.c["expdesc"], e)
            dve.scalar_tensor_tensor(rest, hot1, -2.0, v, ALU.mult, ALU.add).then_inc(s, 1)
            dve.wait_ge(s, n + 1)
            first_argmax(dve, s, n + 1, rest, p2, hot2, tmp, k.c["expdesc"], e)

        @block.scalar
        def _(act):
            act.wait_ge(step.handle, n0 + 3)
            act.activation(lg, lg, ACT.Exp).then_inc(expd.handle, 1)
    step.done += 17
    expd.done += 1


def moe_linear(k):
    c, nc = k.c, k.nc
    w = k.work
    lg = w[:, 0:128]
    hot1 = w[:, 128:256].rearrange("p (t e) -> p t e", e=16)
    hot2 = w[:, 256:384].rearrange("p (t e) -> p t e", e=16)
    p1, p2 = w[:, 384:392], w[:, 392:400]
    gate = w[:, 400:400 + 144].rearrange("p (t e) -> p t e", e=18)
    gateT = w[:, 1024:2048]
    scratch = w[:, 600:800]
    ws = w[:, 800:928]
    logits(k, c["f0cent"], 16, lg)
    softmax_top2(k, lg, 16, c["f0eb"], hot1, hot2, p1, p2, scratch)
    step, turned, made, done = k.sig("lin_step"), k.sig("turned"), k.sig("lin_made"), k.sig("lin_done")
    n0 = step.done
    kept = k.sig("lin_kept")
    x3 = k.tiles(k.x)
    with nc.Block() as block:
        @block.vector
        def _(dve):
            s = step.handle
            dve.tensor_tensor(hot1, hot1, hot2, ALU.add).then_inc(s, 1)
            dve.wait_ge(s, n0 + 1)
            dve.memset(gate[:, :, 16:18], 0.5)
            dve.tensor_tensor(gate[:, :, 0:16], hot1, lg.rearrange("p (t e) -> p t e", e=16), ALU.mult).then_inc(s, 1)
            dve.tensor_tensor(ws, c["f0ws"][:, 0:128], c["f0ws"][:, 128:256], ALU.add).then_inc(s, 1)
            dve.wait_ge(s, n0 + 3)
            dve.tensor_scalar(ws, ws, 0.5, None, ALU.mult).then_inc(s, 1)

        @block.gpsimd
        def _(pool):
            pool.tensor_tensor(k.x[:, :], k.x[:, :], k.xn[:, :], ALU.add)

        @block.tensor
        def _(pe):
            pe.wait_ge(step.handle, n0 + 4)
            for t in range(TILES):
                pe.transpose(k.ps[0:18, t // 4, t % 4 * P:(t % 4 + 1) * P], gate[:, t, :], c["ident"]).then_inc(turned.handle, 1)

        @block.scalar
        def _(act):
            act.wait_ge(turned.handle, turned.done + TILES)
            for h in range(2):
                act.activation(gateT[0:18, h * 512:(h + 1) * 512], k.ps[0:18, h, :], ACT.Copy)
    turned.done += TILES
    step.done += 4
    with nc.Block() as block:
        @block.tensor
        def _(pe):
            n = 0
            for t in range(TILES):
                tok = slice(t * P, (t + 1) * P)
                for q in range(5):
                    if n >= 8:
                        pe.wait_ge(done.handle, done.done + n - 7)
                    if q < 4:
                        ins = pe.matmul(k.ps[:, n % 8, :], k.xnT[:, tok], c["f0wr"][:, q * 512:(q + 1) * 512],
                                        start=True, stop=True)
                    else:
                        pe.matmul(k.ps[:, n % 8, 0:P], k.xnT[:, tok], ws, start=True, stop=False)
                        ins = pe.matmul(k.ps[:, n % 8, 0:P], gateT[0:18, tok], c["f0br"][0:18, :], start=False, stop=True)
                    ins.then_inc(made.handle, 1)
                    n += 1

        @block.vector
        def _(dve):
            n = m = 0
            for t in range(TILES):
                for q in range(5):
                    dve.wait_ge(made.handle, made.done + n + 1)
                    for i in range(4 if q < 4 else 1):
                        if m:
                            dve.wait_ge(kept.handle, kept.done + m)
                        out = k.ps[:, n % 8, i * P:(i + 1) * P]
                        if q < 4:
                            e = 4 * q + i
                            ins = dve.scalar_tensor_tensor(x3[:, t, :], out, gate[:, t, e:e + 1], x3[:, t, :],
                                                           ALU.mult, ALU.add)
                        else:
                            ins = dve.tensor_tensor(x3[:, t, :], out, x3[:, t, :], ALU.add)
                        ins.then_inc(kept.handle, 1)
                        m += 1
                    n += 1
                    dve.wait_ge(kept.handle, kept.done + m)
                    dve.tensor_copy(k.small[0:1, 0:1], k.c["ones"][0:1, 0:1]).then_inc(done.handle, 1)
    made.done += 40
    done.done += 40
    kept.done += 17 * TILES


def routing(k, e, w, score, rows):
    nc, c = k.nc, k.c
    lg = w["lg"]
    shape = [P, TILES, e]
    lg3 = lg.rearrange("p (t e) -> p t e", e=e)
    hot = w["hot"].rearrange("p (t e) -> p t e", e=e)
    step, expd, made = k.sig("route_step"), k.sig("gate_exp"), k.sig("route_made")
    n0 = step.done
    top, tmp8, pos, posi = w["top"], w["tmp8"], w["pos"], w["posi"]
    hotb, tot, incl, t1 = w["hotb"], w["tot"], w["incl"], w["t1"]
    ends, reach, mtab = w["ends"], w["reach"], w["mtab"]
    with nc.Block() as block:
        @block.vector
        def _(dve):
            s = step.handle
            n = first_argmax(dve, s, n0, lg3, top, hot, tmp8, c["expdesc"], e)
            dve.tensor_copy(hotb, w["hot"]).then_inc(s, 1)
            dve.wait_ge(expd.handle, expd.done + 1)
            dve.tensor_scalar(score, score, 1.0, None, ALU.add).then_inc(s, 1)
            dve.wait_ge(s, n + 2)
            dve.reciprocal(score, score).then_inc(s, 1)
            dve.wait_ge(made.handle, made.done + 2)
            dve.tensor_copy(tot.rearrange("p (e t) -> p t e", t=TILES),
                            k.ps[:, 2, 0:TILES * e].rearrange("p (t e) -> p t e", e=e)).then_inc(s, 1)
            dve.wait_ge(s, n + 4)
            dve.tensor_tensor_scan(incl, w["one256"], tot, 0.0,
                                   ALU.mult, ALU.add).then_inc(s, 1)
            dve.wait_ge(s, n + 5)
            inc3 = incl.rearrange("p (e t) -> p t e", t=TILES)
            t13 = t1.rearrange("p (t e) -> p t e", e=e)
            dve.tensor_tensor(t13, k.ps[:, 1, 0:TILES * e].rearrange("p (t e) -> p t e", e=e), inc3, ALU.add).then_inc(s, 1)
            dve.wait_ge(s, n + 6)
            dve.tensor_tensor(t1, t1, w["hot"], ALU.mult).then_inc(s, 1)
            dve.wait_ge(s, n + 7)
            dve.tensor_reduce(pos, t13, X, ALU.add).then_inc(s, 1)
            dve.wait_ge(s, n + 8)
            dve.tensor_copy(posi, pos).then_inc(s, 1)
            dve.tensor_copy(ends, incl.rearrange("p (e t) -> p e t", t=TILES)[:, :, TILES - 1]).then_inc(s, 1)
            dve.wait_ge(s, n + 10)
            dve.tensor_tensor(t13, ends[:, None, :].to_broadcast(shape), c["token_at"][:, :, None].to_broadcast(shape),
                              ALU.is_gt).then_inc(s, 1)
            dve.wait_ge(s, n + 11)
            m3 = mtab[:, 0:TILES * e].rearrange("p (t e) -> p t e", e=e)
            dve.tensor_copy(m3[:, :, 0:1], t13[:, :, 0:1])
            dve.tensor_tensor(m3[:, :, 1:e], t13[:, :, 1:e], t13[:, :, 0:e - 1], ALU.subtract)
            dve.memset(mtab[:, TILES * e:TILES * e + 1], 0.0)
            r3 = reach[0:1, 0:e * 7].rearrange("p (e t) -> p e t", t=7)
            dve.tensor_tensor(r3, ends[0:1, :, None].to_broadcast([1, e, 7]),
                              c["tile_end"][0:1, None, :].to_broadcast([1, e, 7]), ALU.is_gt).then_inc(s, 1)
            dve.wait_ge(s, n + 12)
            dve.tensor_reduce(w["re"][0:1, :], r3, X, ALU.add).then_inc(s, 1)
            dve.wait_ge(s, n + 13)
            dve.tensor_tensor(w["re"][0:1, :], w["re"][0:1, :], c["expert_at"][0:1, 0:e], ALU.add).then_inc(s, 1)
            dve.wait_ge(s, n + 14)
            steps = TILES + e
            p3 = w["walk"][0:1, 0:steps * (e - 1)].rearrange("p (i e) -> p i e", e=e - 1)
            dve.tensor_tensor(p3, c["step_at"][0:1, 0:steps, None].to_broadcast([1, steps, e - 1]),
                              w["re"][0:1, None, 0:e - 1].to_broadcast([1, steps, e - 1]), ALU.is_gt).then_inc(s, 1)
            dve.wait_ge(s, n + 15)
            ef, tf, mf = w["wf"][0:1, 0:40], w["wf"][0:1, 40:80], w["wf"][0:1, 80:120]
            dve.tensor_reduce(ef[:, 0:steps], p3, X, ALU.add).then_inc(s, 1)
            dve.wait_ge(s, n + 16)
            dve.tensor_tensor(tf[:, 0:steps], c["step_at"][0:1, 0:steps], ef[:, 0:steps], ALU.subtract).then_inc(s, 1)
            dve.wait_ge(s, n + 17)
            dve.scalar_tensor_tensor(mf[:, 0:steps], tf[:, 0:steps], float(e), ef[:, 0:steps], ALU.mult, ALU.add).then_inc(s, 1)
            dve.wait_ge(s, n + 18)
            dve.tensor_scalar(mf[:, 0:steps], mf[:, 0:steps], float(TILES * e), None, ALU.min)
            dve.tensor_scalar(tf[:, 0:steps], tf[:, 0:steps], float(TILES - 1), None, ALU.min).then_inc(s, 1)
            dve.wait_ge(s, n + 19)
            dve.tensor_copy(w["wi"][0:1, 0:40], ef)
            dve.tensor_copy(w["wi"][0:1, 40:80], tf)
            dve.tensor_copy(w["wi"][0:1, 80:120], mf)

        @block.scalar
        def _(act):
            act.wait_ge(step.handle, n0 + 5)
            act.activation(score, top, ACT.Exp, scale=-1.0).then_inc(expd.handle, 1)

        @block.tensor
        def _(pe):
            pe.wait_ge(step.handle, n0 + 6)
            pe.matmul(k.ps[:, 1, 0:TILES * e], w["geb"], hotb, start=True, stop=True).then_inc(made.handle, 1)
            pe.matmul(k.ps[:, 2, 0:TILES * e], w["oneb"], hotb, start=True, stop=True).then_inc(made.handle, 1)
    step.done += 24
    expd.done += 1
    made.done += 2


def route_buffers(k, e, base):
    sizes = [("lg", 8 * e), ("hot", 8 * e), ("tot", 8 * e), ("incl", 8 * e), ("t1", 8 * e), ("one256", 8 * e),
             ("mtab", 8 * e + 8), ("ends", e), ("re", e), ("walk", (8 + e) * (e - 1)), ("wf", 120),
             ("top", 8), ("tmp8", 8), ("pos", 8), ("score", 8), ("hotb", 4 * e), ("geb", 64), ("oneb", 64),
             ("posi", 8), ("wi", 120)]
    w = {}
    for name, n in sizes:
        v = k.work[:, base:base + n]
        base += n
        if name in ("hotb", "geb", "oneb"):
            v = v.bitcast(BF16)
        if name in ("posi", "wi"):
            v = v.bitcast(I32)
        w[name] = v
    assert base <= WORK, base
    w["reach"] = w["lg"]
    with k.nc.Block() as block:
        @block.vector
        def _(dve):
            dve.memset(w["one256"], 1.0)
            dve.memset(w["wf"], 0.0)
            dve.tensor_copy(w["geb"], k.c["count_ge"])
            dve.tensor_copy(w["oneb"], k.c["ones"])
    return w


def scatter_rows(k, w, rows, scratch, sorted_rows):
    sent, back = k.sig("rows_scattered"), k.sig("sorted_loaded")
    r3 = k.tiles(rows)
    with k.nc.Block() as block:
        @block.gpsimd
        def _(pool):
            for t in range(TILES):
                pool.indirect_dma_start(out=scratch, out_offset=bass.IndirectOffsetOnAxis(
                    ap=w["posi"][:, t:t + 1].bitcast(U32), axis=0), in_=r3[:, t, :], in_offset=None).then_inc(sent.handle, 16)

        @block.sync
        def _(sp):
            sp.wait_ge(sent.handle, sent.done + 16 * TILES)
            sp.dma_start(k.tiles(sorted_rows), scratch.rearrange("(t p) d -> p t d", p=P)).then_inc(back.handle, 16)
            sp.wait_ge(back.handle, back.done + 16)
    sent.done += 16 * TILES
    back.done += 16


def gather_rows(k, w, sorted_rows, scratch, rows):
    sent, back = k.sig("sorted_stored"), k.sig("rows_gathered")
    r3 = k.tiles(rows)
    with k.nc.Block() as block:
        @block.sync
        def _(sp):
            sp.dma_start(scratch.rearrange("(t p) d -> p t d", p=P), k.tiles(sorted_rows)).then_inc(sent.handle, 16)

        @block.gpsimd
        def _(pool):
            pool.wait_ge(sent.handle, sent.done + 16)
            for t in range(TILES):
                pool.indirect_dma_start(out=r3[:, t, :], out_offset=None, in_=scratch, in_offset=bass.IndirectOffsetOnAxis(
                    ap=w["posi"][:, t:t + 1].bitcast(U32), axis=0)).then_inc(back.handle, 16)
            pool.wait_ge(back.handle, back.done + 16 * TILES)
    sent.done += 16
    back.done += 16 * TILES


def walk_experts(k, w, e, srcT, y, layer):
    nc = k.nc
    steps = TILES + e
    gated = layer == 1
    ft = 2 if gated else 4
    each = 768 if gated else 1024
    wm = k.wmoe[:, 0:e * each].rearrange("p (e n) -> p e n", e=e)
    staged, up, act_done, hid, trn, hT_done, down, acc = (k.sig(n) for n in (
        "staged", "up_made", "silu_done", "hidden", "hidden_turned", "hT_kept", "down_made", "y_added"))
    base = {s: s.done for s in (staged, up, act_done, hid, trn, hT_done, down, acc)}
    at = 4096
    stage = [k.work[:, at + i * P:at + (i + 1) * P] for i in range(2)]
    sg = [k.work[:, at + 256 + i * 256:at + 512 + i * 256] for i in range(2)]
    hb = [k.work[:, at + 768 + i * 512:at + 768 + i * 512 + ft * P] for i in range(2)]
    ht = [k.work[:, at + 1792 + i * 512:at + 1792 + i * 512 + ft * P] for i in range(2)]
    tmp = [k.work[:, at + 2816 + i * P:at + 2816 + (i + 1) * P] for i in range(2)]
    y3 = k.tiles(y)
    s3 = srcT.rearrange("p (t n) -> p t n", n=P)
    mtab = w["mtab"]
    wi = w["wi"]

    def wait(eng, sig, n):
        eng.wait_ge(sig.handle, base[sig] + n)

    def index(eng, row, i, top):
        return eng.value_load(wi[0:1, bass.ds(i + 40 * row, 1)], min_val=0, max_val=top)

    def turns(eng, first, body):
        body(0, 0, True)
        body(1, 1, True)
        with eng.Fori(2, steps, 2) as i:
            body(i, 0, False)
            body(i + 1, 1, False)
        for j in range(first):
            body(steps + j, j % 2, None)

    with nc.Block() as block:
        @block.tensor
        def _(pe):
            def up_product(i, r, peeled):
                ex = index(pe, 0, i, e - 1)
                wait(pe, staged, i + 1)
                if not peeled:
                    wait(pe, hid, i - 1)
                pe.matmul(k.ps[:, r, :], stage[r], wm[:, ex, 0:512], start=True, stop=True).then_inc(up.handle, 1)

            def turn_hidden(i, r, peeled):
                wait(pe, hid, i + 1)
                if not peeled:
                    wait(pe, hT_done, i - 1)
                for f in range(ft):
                    ins = pe.transpose(k.ps[:, 2 + r, f * P:(f + 1) * P], hb[r][:, f * P:(f + 1) * P], k.c["ident"])
                ins.then_inc(trn.handle, 1)

            def down_product(i, r, peeled):
                ex = index(pe, 0, i, e - 1)
                wait(pe, hT_done, i + 1)
                if not peeled:
                    wait(pe, acc, i - 1)
                for f in range(ft):
                    ins = pe.matmul(k.ps[:, 4 + r, 0:P], ht[r][:, f * P:(f + 1) * P],
                                    wm[:, ex, 512 + f * P:512 + (f + 1) * P], start=f == 0, stop=f == ft - 1)
                ins.then_inc(down.handle, 1)

            up_product(0, 0, True)
            up_product(1, 1, True)
            turn_hidden(0, 0, True)
            up_product(2, 0, False)
            turn_hidden(1, 1, True)
            down_product(0, 0, True)
            up_product(3, 1, False)
            turn_hidden(2, 0, False)
            down_product(1, 1, True)
            with pe.Fori(4, steps, 2) as i:
                up_product(i, 0, False)
                turn_hidden(i - 1, 1, False)
                down_product(i - 2, 0, False)
                up_product(i + 1, 1, False)
                turn_hidden(i, 0, False)
                down_product(i - 1, 1, False)
            turn_hidden(steps - 1, 1, False)
            down_product(steps - 2, 0, False)
            down_product(steps - 1, 1, False)

        @block.scalar
        def _(act):
            def stage_in(i, r, peeled):
                t = index(act, 1, i, TILES - 1)
                if not peeled:
                    wait(act, up, i - 1)
                if gated:
                    act.activation(stage[r], s3[:, t, :], ACT.Copy).then_inc(staged.handle, 1)
                else:
                    ex = index(act, 0, i, e - 1)
                    act.activation(stage[r], s3[:, t, :], ACT.Identity, scale=k.c["f3g"][:, bass.ds(ex, 1)],
                                   bias=k.c["f3b"][:, bass.ds(ex, 1)]).then_inc(staged.handle, 1)

            def silu(i, r, peeled):
                wait(act, up, i + 1)
                if not peeled:
                    wait(act, hid, i - 1)
                act.activation(sg[r], k.ps[:, r, 0:256], ACT.Silu).then_inc(act_done.handle, 1)

            def relu(i, r, peeled):
                ex = index(act, 0, i, e - 1)
                wait(act, trn, i + 1)
                if not peeled:
                    wait(act, down, i - 1)
                for f in range(ft):
                    ins = act.activation(ht[r][:, f * P:(f + 1) * P], k.ps[:, 2 + r, f * P:(f + 1) * P], ACT.Relu,
                                         bias=k.c["f3b1"].rearrange("p (e f) -> p e f", f=4)[:, ex, f:f + 1])
                ins.then_inc(hT_done.handle, 1)

            after = silu if gated else relu
            stage_in(0, 0, True)
            stage_in(1, 1, True)
            after(0, 0, True)
            stage_in(2, 0, False)
            after(1, 1, True)
            stage_in(3, 1, False)
            with act.Fori(2, steps - 2, 2) as i:
                after(i, 0, False)
                stage_in(i + 2, 0, False)
                after(i + 1, 1, False)
                stage_in(i + 3, 1, False)
            after(steps - 2, 0, False)
            after(steps - 1, 1, False)

        @block.vector
        def _(dve):
            def hidden(i, r, peeled):
                if gated:
                    wait(dve, act_done, i + 1)
                else:
                    wait(dve, up, i + 1)
                if not peeled:
                    wait(dve, trn, i - 1)
                if gated:
                    dve.tensor_tensor(hb[r], k.ps[:, r, 256:512], sg[r], ALU.mult).then_inc(hid.handle, 1)
                else:
                    dve.tensor_copy(hb[r], k.ps[:, r, :]).then_inc(hid.handle, 1)

            def keep_turned(i, r, peeled):
                if not gated:
                    return
                wait(dve, trn, i + 1)
                if not peeled:
                    wait(dve, down, i - 1)
                dve.tensor_copy(ht[r], k.ps[:, 2 + r, 0:ft * P]).then_inc(hT_done.handle, 1)

            def add_up(i, r, peeled):
                t = index(dve, 1, i, TILES - 1)
                m = index(dve, 2, i, TILES * e)
                wait(dve, down, i + 1)
                if not (peeled and r == 0):
                    wait(dve, acc, i)
                src = k.ps[:, 4 + r, 0:P]
                if not gated:
                    ex = index(dve, 0, i, e - 1)
                    dve.tensor_tensor(tmp[r], src, k.c["f3b2"].rearrange("p (e n) -> p e n", e=e)[:, ex, :],
                                      ALU.add).then_inc(act_done.handle, 1)
                    wait(dve, act_done, i + 1)
                    src = tmp[r]
                dve.scalar_tensor_tensor(y3[:, t, :], src, mtab[:, bass.ds(m, 1)], y3[:, t, :],
                                         ALU.mult, ALU.add).then_inc(acc.handle, 1)

            dve.memset(y[:, 0:1024], 0.0)
            hidden(0, 0, True)
            hidden(1, 1, True)
            keep_turned(0, 0, True)
            hidden(2, 0, False)
            keep_turned(1, 1, True)
            add_up(0, 0, True)
            hidden(3, 1, False)
            keep_turned(2, 0, False)
            add_up(1, 1, True)
            with dve.Fori(4, steps, 2) as i:
                hidden(i, 0, False)
                keep_turned(i - 1, 1, False)
                add_up(i - 2, 0, False)
                hidden(i + 1, 1, False)
                keep_turned(i, 0, False)
                add_up(i - 1, 1, False)
            keep_turned(steps - 1, 1, False)
            add_up(steps - 2, 0, False)
            add_up(steps - 1, 1, False)
    for s in base:
        s.done += steps


def swiglu_dense(k, experts, wg, wu, wd, ft, weights, dst):
    nc = k.nc
    made, silud, hid, down, acc = (k.sig(n) for n in ("up_made", "silu_done", "hidden", "down_made", "y_added"))
    b = {s: s.done for s in (made, silud, hid, down, acc)}
    sg = [k.work[:, 4096 + i * 512:4608 + i * 512] for i in range(2)]
    h = [k.work[:, 5120 + i * 512 * ft:5120 + (i + 1) * 512 * ft] for i in range(2)]
    d3 = k.tiles(dst)
    items = [(e, half) for e in experts for half in range(2)]

    with nc.Block() as block:
        @block.tensor
        def _(pe):
            for i in range(len(items) + 1):
                if i < len(items):
                    e, half = items[i]
                    for f in range(ft):
                        n = i * ft + f
                        if n >= 2:
                            pe.wait_ge(hid.handle, b[hid] + n - 1)
                        rhs = k.xnT[:, half * 512:(half + 1) * 512]
                        pe.matmul(k.ps[:, 2 * (n % 2), :], wg(e, f), rhs, start=True, stop=True)
                        pe.matmul(k.ps[:, 2 * (n % 2) + 1, :], wu(e, f), rhs, start=True, stop=True).then_inc(made.handle, 1)
                if i >= 1:
                    m = i - 1
                    e, half = items[m]
                    pe.wait_ge(hid.handle, b[hid] + ft * (m + 1))
                    if m >= 2:
                        pe.wait_ge(acc.handle, b[acc] + 4 * (m - 1))
                    for q in range(4):
                        for f in range(ft):
                            ins = pe.matmul(k.ps[:, 4 + m % 2, q * P:(q + 1) * P],
                                            h[m % 2][:, f * 512 + q * P:f * 512 + (q + 1) * P], wd(e, f),
                                            start=f == 0, stop=f == ft - 1)
                    ins.then_inc(down.handle, 1)

        @block.scalar
        def _(act):
            for n in range(len(items) * ft):
                act.wait_ge(made.handle, b[made] + n + 1)
                if n >= 2:
                    act.wait_ge(hid.handle, b[hid] + n - 1)
                act.activation(sg[n % 2], k.ps[:, 2 * (n % 2), :], ACT.Silu).then_inc(silud.handle, 1)

        @block.vector
        def _(dve):
            def hidden(n):
                i, f = n // ft, n % ft
                dve.wait_ge(silud.handle, b[silud] + n + 1)
                if i >= 2:
                    dve.wait_ge(down.handle, b[down] + i - 1)
                dve.tensor_tensor(h[i % 2][:, f * 512:(f + 1) * 512], k.ps[:, 2 * (n % 2) + 1, :], sg[n % 2],
                                  ALU.mult).then_inc(hid.handle, 1)

            def add_up(m):
                e, half = items[m]
                dve.wait_ge(down.handle, b[down] + m + 1)
                for q in range(4):
                    t = half * 4 + q
                    if m >= 2 and q == 0:
                        dve.wait_ge(acc.handle, b[acc] + 4 * m - 4)
                    src = k.ps[:, 4 + m % 2, q * P:(q + 1) * P]
                    wt = weights(e, t)
                    if wt is None:
                        dve.tensor_tensor(d3[:, t, :], src, d3[:, t, :], ALU.add).then_inc(acc.handle, 1)
                    else:
                        dve.scalar_tensor_tensor(d3[:, t, :], src, wt, d3[:, t, :], ALU.mult, ALU.add).then_inc(acc.handle, 1)

            for i in range(len(items)):
                for f in range(ft):
                    hidden(i * ft + f)
                if i >= 1:
                    add_up(i - 1)
            add_up(len(items) - 1)
    made.done += len(items) * ft
    silud.done += len(items) * ft
    hid.done += len(items) * ft
    down.done += len(items)
    acc.done += 4 * len(items)


def wait_load(k, names):
    with k.nc.Block() as block:
        @block.sync
        def _(sp):
            for name in names:
                sp.wait_ge(k.load_sem[name], 32 if name == "mask" else 16)


def build(nc, dram):
    with ExitStack() as ctx:
        k = Program(nc, ctx, dram)
        c = k.c
        k.mparts = k.sb("mparts", TILES * 48, BF16)
        k.mT = k.sb("mT", 1024, BF16)
        start_loads(k)
        wait_load(k, ["consts", "patterns", "x", "ctx", "mask", "l0a"])
        constants(k)

        a = Core(k, H, 8, SC)
        project_k(k, a, c["a0wk"], c["a0bk"], False)
        project_v(k, a, c["a0wv"], c["a0bv"])
        layernorm(k, k.x, k.xn, 1e-5)
        turn(k, k.xn, k.xnT)
        add_rows(k, k.x, c["a0bo"])
        project_q(k, a, c["a0wq"], c["a0bq"], False)
        mask0 = [(lambda b, at, n: k.mb[0:SC, b * S + at:b * S + at + n], k.i64big[0:SC, :])]
        attend(k, a, mask0, 8 ** -0.5, c["a0wo"], k.x)

        layernorm(k, k.x, k.xn, 1e-5)
        turn(k, k.xn, k.xnT)
        wait_load(k, ["l0f"])
        moe_linear(k)

        with nc.Block() as block:
            @block.sync
            def _(sp):
                sp.dma_start(k.wmoe[:, EARLY:L1M], dram["moe1"][:, EARLY:L1M]).then_inc(k.load_sem["moe1b"], 16)

        layernorm(k, k.x, k.xn, 1e-5)
        layernorm(k, k.xn, k.xn, 1e-5)
        wait_load(k, ["l1a"])
        affine(k, c["a1g"], c["a1b"])
        turn(k, k.xn, k.xnT)
        gate_step = k.sig("tanh_step")
        with nc.Block() as block:
            @block.scalar
            def _(act):
                act.activation(k.small[:, 100:101], c["a1gate"], ACT.Tanh).then_inc(gate_step.handle, 1)

            @block.vector
            def _(dve):
                dve.wait_ge(gate_step.handle, 1)
                dve.tensor_scalar(c["a1wo"], c["a1wo"], k.small[:, 100:101], None, ALU.mult)
                dve.tensor_scalar(c["a1bo"], c["a1bo"], k.small[:, 100:101], None, ALU.mult)
        add_rows(k, k.x, c["a1bo"])
        for half in range(2):
            a = Core(k, 8, 64, SC)
            part = slice(half * 512, half * 512 + 512)
            project_k(k, a, c["a1wk"][:, part], None, False)
            project_v(k, a, c["a1wv"][:, part], None)
            project_q(k, a, c["a1wq"][:, part], None, False)
            attend(k, a, [], 64 ** -0.5, c["a1wo"][:, part], k.x)

        layernorm(k, k.x, k.xn, 1e-5)
        turn(k, k.xn, k.xnT)
        wait_load(k, ["l1s"])
        w = route_buffers(k, 32, 7168)
        logits(k, c["f1gw"], 32, w["lg"])
        xs, xsT, y = k.work[:, 0:1024], k.work[:, 1024:2048], k.work[:, 2048:3072]
        srt = k.work[:, 3072:4096]
        routing(k, 32, w, w["score"], None)
        with nc.Block() as block:
            @block.vector
            def _(dve):
                dve.tensor_tensor(k.tiles(xs), k.tiles(k.xn), w["score"][:, :, None].to_broadcast([P, TILES, D]), ALU.mult)
        scatter_rows(k, w, xs, dram["scratch0"], srt)
        turn(k, srt, xsT)
        wait_load(k, ["moe1", "moe1b"])
        walk_experts(k, w, 32, xsT, y, 1)
        gather_rows(k, w, y, dram["scratch1"], xs)
        add_rows(k, k.x, None, xs)
        sgu, sd = c["f1sgu"], c["f1sd"]
        swiglu_dense(k, [0], lambda e, f: sgu[:, f * P:(f + 1) * P], lambda e, f: sgu[:, 256 + f * P:256 + (f + 1) * P],
                     lambda e, f: sd[:, f * P:(f + 1) * P], 2, lambda e, t: None, k.x)
        with nc.Block() as block:
            @block.sync
            def _(sp):
                for name in ("l2a", "l2f", "l3a"):
                    sp.dma_start(dict(k.loads)[name], dram[name]).then_inc(k.load_sem[name], 16)
                sp.dma_start(k.wmoe[:, 0:L3M], dram["moe3"]).then_inc(k.load_sem["moe3"], 16)

        a = Core(k, H, 8, SC)
        wait_load(k, ["l2a"])
        project_k(k, a, c["a2wk"], c["a2bk"], True)
        project_v(k, a, c["a2wv"], c["a2bv"])
        layernorm(k, k.x, k.xn, 1e-5)
        turn(k, k.xn, k.xnT)
        add_rows(k, k.x, c["a2bo"])
        project_q(k, a, c["a2wq"], c["a2bq"], True)
        attend(k, a, [], 8 ** -0.5, c["a2wo"], k.x)

        wait_load(k, ["l2f", "l3a"])
        xl = k.sb("xl", 1024)
        layernorm(k, k.x, xl, 1e-5)
        rmsnorm(k, xl, k.xn, c["f2g1"], 1e-6)
        turn(k, k.xn, k.xnT)
        a = Core(k, 4, 32, S)
        kept, made = k.sig("k_kept"), k.sig("v_proj")
        with nc.Block() as block:
            @block.tensor
            def _(pe):
                for h in range(2):
                    pe.matmul(k.ps[:, h, :], c["f2wkc"], k.xnT[:, h * 512:(h + 1) * 512], start=True,
                              stop=True).then_inc(kept.handle, 1)
                for t in range(TILES):
                    ins = pe.matmul(k.ps[:, 2, t * 32:(t + 1) * 32], k.xnT[:, t * P:(t + 1) * P], c["f2wvc"],
                                    start=True, stop=True)
                ins.then_inc(made.handle, 1)

            @block.vector
            def _(dve):
                for b in range(B):
                    dve.wait_ge(kept.handle, kept.done + b // 2 + 1)
                    src = k.ps[:, b // 2, b % 2 * S:(b % 2 + 1) * S]
                    dve.tensor_tensor(a.kblk[:, b, :].rearrange("p (h s) -> p h s", s=S),
                                      src[:, None, :].to_broadcast([P, 4, S]),
                                      c["headmask4"][:, :, None].to_broadcast([P, 4, S]), ALU.mult)

            @block.scalar
            def _(act):
                act.wait_ge(made.handle, made.done + 1)
                act.activation(a.v[:, :, 0:32], k.ps[:, 2, 0:256].rearrange("p (t d) -> p t d", d=32), ACT.Copy)

            @block.gpsimd
            def _(pool):
                pool.memset(a.v[:, :, 32:33], 1.0)
        kept.done += 2
        made.done += 1
        project_q(k, a, c["f2wq"], None, False)
        attend(k, a, [], 32 ** -0.5, c["f2wo"], xl)
        rmsnorm(k, xl, k.xn, c["f2g2"], 1e-6)
        turn(k, k.xn, k.xnT)
        wk = k.work
        lg = wk[:, 0:64]
        hot1 = wk[:, 64:128].rearrange("p (t e) -> p t e", e=8)
        hot2 = wk[:, 128:192].rearrange("p (t e) -> p t e", e=8)
        p1, p2, comb = wk[:, 192:200], wk[:, 200:208], wk[:, 208:272].rearrange("p (t e) -> p t e", e=8)
        logits(k, c["f2wr"], 8, lg)
        softmax_top2(k, lg, 8, c["f2eb"], hot1, hot2, p1, p2, wk[:, 300:400])
        step, expd = k.sig("gate_step"), k.sig("gate_exp")
        n0 = step.done
        with nc.Block() as block:
            @block.vector
            def _(dve):
                s = step.handle
                dve.tensor_tensor(p2, p2, p1, ALU.subtract).then_inc(s, 1)
                dve.wait_ge(expd.handle, expd.done + 1)
                dve.tensor_scalar(p1, p2, 1.0, None, ALU.add).then_inc(s, 1)
                dve.wait_ge(s, n0 + 2)
                dve.reciprocal(p1, p1).then_inc(s, 1)
                dve.wait_ge(s, n0 + 3)
                dve.tensor_tensor(p2, p2, p1, ALU.mult).then_inc(s, 1)
                dve.tensor_tensor(hot1, hot1, p1[:, :, None].to_broadcast([P, TILES, 8]), ALU.mult).then_inc(s, 1)
                dve.wait_ge(s, n0 + 5)
                dve.tensor_tensor(hot2, hot2, p2[:, :, None].to_broadcast([P, TILES, 8]), ALU.mult).then_inc(s, 1)
                dve.wait_ge(s, n0 + 6)
                dve.tensor_tensor(comb, hot1, hot2, ALU.add)

            @block.scalar
            def _(act):
                act.wait_ge(step.handle, n0 + 1)
                act.activation(p2, p2, ACT.Exp).then_inc(expd.handle, 1)
        step.done += 6
        expd.done += 1
        swiglu_dense(k, list(range(9)), lambda e, f: c["f2w1"][:, e * P:(e + 1) * P],
                     lambda e, f: c["f2w3"][:, e * P:(e + 1) * P], lambda e, f: c["f2w2"][:, e * P:(e + 1) * P], 1,
                     lambda e, t: comb[:, t, e:e + 1] if e < 8 else None, xl)
        add_rows(k, k.x, None, xl)

        a = Core(k, H, 8, SC)
        project_k(k, a, c["a3wk"], None, False)
        project_v(k, a, c["a3wv"], None)
        layernorm(k, k.x, k.xn, 1e-5)
        turn(k, k.xn, k.xnT)
        project_q(k, a, c["a3wq"], None, False)
        mask3 = [(lambda b, at, n, q=q: k.mb3[0:SC, q * 256 + at:q * 256 + at + n], k.i64[0:SC, :]) for q in range(3)]
        attend(k, a, mask3, D ** -0.5, c["a3wo"], k.x)

        layernorm(k, k.x, k.xn, 1e-5)
        turn(k, k.xn, k.xnT)
        w = route_buffers(k, 8, 7168)
        logits(k, c["f3cent"], 8, w["lg"])
        routing(k, 8, w, w["score"], None)
        layernorm(k, k.xn, xs, 1e-5)
        scatter_rows(k, w, xs, dram["scratch0"], srt)
        turn(k, srt, xsT)
        wait_load(k, ["moe3"])
        walk_experts(k, w, 8, xsT, y, 3)
        gather_rows(k, w, y, dram["scratch1"], xs)
        step = k.sig("addrow")
        with nc.Block() as block:
            @block.vector
            def _(dve):
                dve.tensor_tensor(k.tiles(xs), k.tiles(xs), w["score"][:, :, None].to_broadcast([P, TILES, D]),
                                  ALU.mult).then_inc(step.handle, 1)
                dve.tensor_tensor(k.x[:, :], k.x[:, :], k.xn[:, :], ALU.add).then_inc(step.handle, 1)
                dve.wait_ge(step.handle, step.done + 2)
                dve.tensor_tensor(k.x[:, :], k.x[:, :], xs, ALU.add)
        step.done += 2
        stored = k.sig("stored")
        with nc.Block() as block:
            @block.sync
            def _(sp):
                sp.dma_start(dram["out"], k.x[:, :]).then_inc(stored.handle, 16)
                sp.wait_ge(stored.handle, 16)


def shape_constants():
    r = np.arange(P)
    f = {}
    f["ident"] = np.eye(P)
    f["count_ge"] = -1.0 * (r[:, None] >= r[None, :])
    f["ones"] = np.ones((P, P))
    f["headmask16"] = r[:, None] // 8 == np.arange(16)
    f["headmask4"] = r[:, None] // 32 == np.arange(4)
    f["headmask2"] = r[:, None] // 64 == np.arange(2)
    f["i64rep"] = r[:, None] % 128 == np.arange(512) % 64
    for name, heads, n, keys in (("neghead16", 16, 1024, 64), ("neghead4", 4, 1024, 256), ("neghead8", 8, 512, 64)):
        f[name] = -((r[:, None] % heads == np.arange(n) // keys) & (r[:, None] < 3 * heads)).astype(np.float32)
    dim = 4
    freqs = np.exp(-np.arange(dim, dtype=np.float32) * np.log(np.float32(10000.0)) / np.float32(dim)).astype(np.float32)
    ang = (np.arange(S, dtype=np.float32)[None, :] * freqs[(r % 8) // 2][:, None]).astype(np.float32)
    f["cosq"], f["sinq"] = np.cos(ang), np.sin(ang)
    rot = np.zeros((P, P))
    rot[r[1::2], r[0::2]] = -1.0
    rot[r[0::2], r[1::2]] = 1.0
    f["rot"] = rot
    f["expdesc"] = np.broadcast_to(64 - np.arange(32), (P, 32))
    f["token_at"] = r[:, None] + P * np.arange(8)
    f["tile_end"] = np.broadcast_to(P * np.arange(1, 8), (P, 7))
    f["expert_at"] = np.broadcast_to(np.arange(32), (P, 32))
    f["step_at"] = np.broadcast_to(np.arange(40), (P, 40))
    f["neghalf"] = np.full((P, 8), -0.5)
    return {n: np.asarray(v, np.float32) for n, v in f.items()}


def kernel(**i):
    import concourse.bacc as bacc
    from concourse.bass_utils import run_bass_kernel_spmd as run

    i = {n: np.asarray(v) for n, v in i.items()}

    def rows(v):
        v = v.reshape(1, -1)
        return np.broadcast_to(v, (P, v.shape[1]))

    def by_in(w):
        return w.transpose(1, 0, 2).reshape(w.shape[1], -1)

    def by_tile(w):
        return w.reshape(-1, P, w.shape[-1]).transpose(1, 0, 2).reshape(P, -1)

    def pad(v):
        out = np.zeros((P, v.shape[1]), v.dtype)
        out[0:v.shape[0]] = v
        return out

    f = shape_constants()
    wkv, bkv = i["L0_xattn_W_kv"].reshape(D, H, 2, 8), i["L0_xattn_b_kv"].reshape(H, 2, 8)
    f["a0wk"], f["a0wv"] = wkv[:, :, 0].reshape(D, D), wkv[:, :, 1].reshape(D, D)
    f["a0bk"], f["a0bv"] = bkv[:, 0].reshape(D, 1), rows(bkv[:, 1])
    f["a0wq"], f["a0bq"] = i["L0_xattn_W_q"], i["L0_xattn_b_q"].reshape(D, 1)
    f["a0wo"], f["a0bo"] = i["L0_xattn_W_o"], rows(i["L0_xattn_b_o"])
    f["f0wr"] = by_in(i["L0_ffn_Wr"].transpose(0, 2, 1))
    f["f0ws"] = by_in(i["L0_ffn_Ws"].transpose(0, 2, 1))
    f["f0cent"], f["f0eb"] = i["L0_ffn_centroids"].T, rows(i["L0_ffn_expert_biases"])
    f["f0br"] = pad(np.concatenate([i["L0_ffn_br"], i["L0_ffn_bs"]]))
    f["a1wk"], f["a1wv"] = i["L1_xattn_w_kv"][:, :1024], i["L1_xattn_w_kv"][:, 1024:]
    f["a1wq"], f["a1wo"] = i["L1_xattn_w_q"], by_tile(i["L1_xattn_w_out"])
    f["a1bo"], f["a1g"], f["a1b"] = rows(i["L1_xattn_b_out"]), rows(i["L1_xattn_ln_gamma"]), rows(i["L1_xattn_ln_beta"])
    f["a1gate"] = rows(i["L1_xattn_gate"])
    f["f1gw"] = i["L1_ffn_gate_w"]
    f["f1sgu"] = np.concatenate([i["L1_ffn_shared_gate_w"], i["L1_ffn_shared_up_w"]], 1)
    f["f1sd"] = by_tile(i["L1_ffn_shared_down_w"])
    for n in "kvq":
        f[f"a2w{n}"] = i[f"L2_xattn_w{n}"].T
    f["a2wo"], f["a2bo"] = i["L2_xattn_wo"].T, rows(i["L2_xattn_bo"])
    f["a2bk"], f["a2bq"], f["a2bv"] = i["L2_xattn_bk"].reshape(D, 1), i["L2_xattn_bq"].reshape(D, 1), rows(i["L2_xattn_bv"])
    f["f2g1"], f["f2g2"] = rows(i["L2_ffn_g1"]), rows(i["L2_ffn_g2"])
    f["f2wq"], f["f2wkc"], f["f2wvc"] = i["L2_ffn_Wq"].T, np.tile(i["L2_ffn_Wkc"].T, (1, 4)), i["L2_ffn_Wvc"].T
    f["f2wo"], f["f2wr"], f["f2eb"] = i["L2_ffn_Wo"].T, i["L2_ffn_Wr"].T, rows(i["L2_ffn_expert_bias"])
    for n in "123":
        both = np.concatenate([i[f"L2_ffn_eW{n}"], i[f"L2_ffn_sW{n}"][None]])
        f[f"f2w{n}"] = by_in(both.transpose(0, 2, 1))
    f["a3wk"], f["a3wv"] = i["L3_xattn_Wkv"][:D].T, i["L3_xattn_Wkv"][D:].T
    f["a3wq"], f["a3wo"] = i["L3_xattn_Wq"].T, i["L3_xattn_Wout"].T
    f["f3cent"], f["f3g"], f["f3b"] = i["L3_ffn_centroids"].T, i["L3_ffn_ln_g"].T, i["L3_ffn_ln_b"].T
    f["f3b1"] = i["L3_ffn_b1"].reshape(8, 4, P).transpose(2, 0, 1).reshape(P, 32)
    f["f3b2"] = rows(i["L3_ffn_b2"])

    arrays = {}
    for name, group in GROUPS:
        for n, wd in group:
            assert f[n].shape == (P, wd), (n, f[n].shape)
        arrays[name] = np.concatenate([f[n] for n, _ in group], 1)
    arrays["moe1"] = by_in(np.concatenate([
        i["L1_ffn_routed_gate_w"], i["L1_ffn_routed_up_w"],
        i["L1_ffn_routed_down_w"].reshape(32, 2, P, D).transpose(0, 2, 1, 3).reshape(32, P, 256)], 2))
    arrays["moe3"] = by_in(np.concatenate([
        i["L3_ffn_w1"], i["L3_ffn_w2"].reshape(8, 4, P, D).transpose(0, 2, 1, 3).reshape(8, P, 512)], 2))
    arrays["x"] = by_tile(i["x"].reshape(B * S, D))
    arrays["ctx"] = by_tile(i["ctx_1024"].reshape(B * SC, D))
    arrays["mask0"] = i["mask_BxSxS2_ik0"].transpose(2, 0, 1).reshape(SC, B * S)
    arrays["mask3"] = i["mask_SxS2_fk0"].T
    arrays = {n: np.ascontiguousarray(a) for n, a in arrays.items()}

    nc = bacc.Bacc("TRN2", target_bir_lowering=False, num_devices=1)
    dram = {n: nc.dram_tensor(n + "_in", a.shape, mybir.dt.from_np(a.dtype), kind="ExternalInput").ap()
            for n, a in arrays.items()}
    dram["out"] = nc.dram_tensor("out", [P, TILES * D], F32, kind="ExternalOutput").ap()
    dram["scratch0"] = nc.dram_tensor("sorted_in", [B * S, D], F32, kind="Internal").ap()
    dram["scratch1"] = nc.dram_tensor("sorted_out", [B * S, D], F32, kind="Internal").ap()
    build(nc, dram)
    r = run(nc, [{n + "_in": a for n, a in arrays.items()}], core_ids=[0])
    out = r.results[0]["out"]
    return out.reshape(P, TILES, D).transpose(1, 0, 2).reshape(B, S, D)
```

```python
from contextlib import ExitStack

import numpy as np
import concourse.bass as bass
from concourse import mybir

F32 = mybir.dt.float32
BF16 = mybir.dt.bfloat16
I32 = mybir.dt.int32
U32 = mybir.dt.uint32
ALU = mybir.AluOpType
ACT = mybir.ActivationFunctionType
X = mybir.AxisListType.X

P = 128
B, S, D = 4, 256, 128
SC = 64
TILES = B * S // P
H = 16
BANK = 512
BIG = -1e20
E5, E6 = 1e-5, 1e-6
LN = (1.0, E5)
LN_LN = (1.0 + E5, E5 * E5)
LN_RMS = (1.0 + E6, E6 * E5)

CONSTS = [("ident", 128), ("count_ge", 128), ("ones", 128), ("headmask16", 16), ("headmask4", 4), ("headmask2", 2),
          ("cosq", 256), ("sinq", 256), ("rot", 128), ("expdesc", 32), ("token_at", 8), ("tile_end", 7),
          ("expert_at", 32), ("step_at", 40), ("neghalf", 8)]
PATTERNS = [("i64rep", 512), ("neghead16", 1024), ("neghead4", 1024), ("neghead8", 512)]
L0A = [("a0wk", 128), ("a0wv", 128), ("a0wq", 128), ("a0wo", 128), ("a0bv", 128), ("a0bo", 128),
       ("a0bk", 1), ("a0bq", 1)]
L0F = [("f0wr", 2048), ("f0ws", 256), ("f0cent", 16), ("f0eb", 16), ("f0br", 128)]
L1A = [("a1wk", 1024), ("a1wv", 1024), ("a1wq", 1024), ("a1wo", 1024), ("a1bo", 128), ("a1g", 1),
       ("a1b", 1), ("a1gate", 1)]
L1S = [("f1gw", 32), ("f1sgu", 512), ("f1sd", 256)]
L2A = [("a2wk", 128), ("a2wv", 128), ("a2wq", 128), ("a2wo", 128), ("a2bv", 128), ("a2bo", 128),
       ("a2bk", 1), ("a2bq", 1)]
L2F = [("f2g1", 1), ("f2g2", 1), ("f2wq", 128), ("f2wkc", 128), ("f2wvc", 32), ("f2wo", 128), ("f2wr", 8),
       ("f2eb", 8), ("f2w1", 1152), ("f2w3", 1152), ("f2w2", 1152)]
L3A = [("a3wk", 128), ("a3wv", 128), ("a3wq", 128), ("a3wo", 128), ("f3cent", 8), ("f3g", 8), ("f3b", 8),
       ("f3b1", 32), ("f3b2", 1024)]
L1M = 32 * 768
L3M = 8 * 1024
EARLY = 28 * 768
WORK = 11008
GROUPS = [("consts", CONSTS), ("patterns", PATTERNS), ("l0a", L0A), ("l0f", L0F), ("l1a", L1A), ("l1s", L1S),
          ("l2a", L2A), ("l2f", L2F), ("l3a", L3A)]


def words(group):
    return sum(n for _, n in group)


class Signal:

    def __init__(self, handle):
        self.handle, self.done = handle, 0


class Program:
    def __init__(self, nc, ctx, dram):
        self.nc, self.ctx, self.dram, self.signals = nc, ctx, dram, {}

        def sb(name, n, dt=F32):
            return ctx.enter_context(nc.sbuf_tensor(name, [P, n], dt))

        self.sb = sb
        self.c = {}
        self.loads = []
        self.work = sb("work", WORK)
        self.wmoe = sb("wmoe", L1M)
        late = L3M
        for name, group in GROUPS:
            if name == "patterns":
                t = self.work[:, 0:words(group)]
            elif name == "l0f":
                t = self.wmoe[:, EARLY:EARLY + words(group)]
            elif name in ("l2a", "l2f", "l3a"):
                t = self.wmoe[:, late:late + words(group)]
                late += words(group)
            else:
                t = sb(name, words(group))[:, :]
            at = 0
            for part, n in group:
                self.c[part] = t[:, at:at + n]
                at += n
            self.loads.append((name, t))
        self.x = sb("x", 1024)
        self.xn = sb("xn", 1024)
        self.xnT = sb("xnT", 1024)
        self.ctxn = sb("ctxn", 256)
        self.ctxT = sb("ctxT", 512)
        self.small = sb("small", 2048)
        self.maskT0 = self.work[:, 4096:5120].bitcast(I32)
        self.maskT3 = self.work[:, 5120:5376]
        self.mb = sb("mb", 1024, BF16)
        self.mb3 = sb("mb3", 768, BF16)
        self.i64 = sb("i64", 512, BF16)
        self.i64big = sb("i64big", 512, BF16)
        self.nh = {16: sb("nh16", 1024, BF16), 4: sb("nh4", 1024, BF16), 8: sb("nh8", 512, BF16)}
        self.identb = sb("identb", 128, BF16)
        self.ps = ctx.enter_context(nc.psum_tensor("ps", [P, 8, BANK], F32))
        self.load_sem = {}
        for name in ["x", "ctx", "mask"] + [n for n, _ in self.loads] + ["moe1", "moe1b", "moe3"]:
            self.load_sem[name] = ctx.enter_context(nc.semaphore(f"loaded_{name}"))

    def sig(self, name):
        if name not in self.signals:
            self.signals[name] = Signal(self.ctx.enter_context(self.nc.semaphore(name)))
        return self.signals[name]

    def tiles(self, t):
        return t[:, 0:1024].rearrange("p (t d) -> p t d", d=P)


def start_loads(k):
    with k.nc.Block() as block:
        @block.sync
        def _(sp):
            order = dict(k.loads)
            sp.dma_start(order["consts"], k.dram["consts"]).then_inc(k.load_sem["consts"], 16)
            sp.dma_start(order["patterns"], k.dram["patterns"]).then_inc(k.load_sem["patterns"], 16)
            sp.dma_start(k.x[:, :], k.dram["x"]).then_inc(k.load_sem["x"], 16)
            sp.dma_start(k.ctxn[:, :], k.dram["ctx"]).then_inc(k.load_sem["ctx"], 16)
            sp.dma_start(order["l0a"], k.dram["l0a"]).then_inc(k.load_sem["l0a"], 16)
            sp.dma_start(k.maskT0[0:SC, :], k.dram["mask0"]).then_inc(k.load_sem["mask"], 16)
            sp.dma_start(k.maskT3[0:SC, :], k.dram["mask3"]).then_inc(k.load_sem["mask"], 16)
            for name in ("l0f", "l1a", "l1s"):
                sp.dma_start(order[name], k.dram[name]).then_inc(k.load_sem[name], 16)
            sp.dma_start(k.wmoe[:, 0:EARLY], k.dram["moe1"][:, 0:EARLY]).then_inc(k.load_sem["moe1"], 16)


def constants(k):
    c = k.c
    cast, split, turned = k.sig("cast"), k.sig("split"), k.sig("turned")
    with k.nc.Block() as block:
        @block.vector
        def _(dve):
            dve.wait_ge(k.load_sem["consts"], 16)
            dve.tensor_copy(k.i64[:, :], c["i64rep"])
            dve.tensor_scalar(k.i64big[:, :], c["i64rep"], BIG, None, ALU.mult)
            dve.tensor_copy(k.nh[16][:, :], c["neghead16"])
            dve.tensor_copy(k.nh[4][:, :], c["neghead4"])
            dve.tensor_copy(k.nh[8][:, :], c["neghead8"])
            dve.tensor_copy(k.identb[:, :], c["ident"])
            dve.wait_ge(k.load_sem["mask"], 32)
            dve.tensor_scalar(k.mb[0:SC, :], k.maskT0[0:SC, :], 0.0, None, ALU.is_equal)
            rest = k.small[0:SC, 0:256]
            dve.tensor_copy(k.mb3[0:SC, 0:256], k.maskT3[0:SC, :]).then_inc(split.handle, 1)
            dve.wait_ge(split.handle, split.done + 1)
            dve.tensor_tensor(rest, k.maskT3[0:SC, :], k.mb3[0:SC, 0:256], ALU.subtract).then_inc(split.handle, 1)
            dve.wait_ge(split.handle, split.done + 2)
            dve.tensor_copy(k.mb3[0:SC, 256:512], rest).then_inc(split.handle, 1)
            dve.wait_ge(split.handle, split.done + 3)
            dve.tensor_tensor(k.mb3[0:SC, 512:768], rest, k.mb3[0:SC, 256:512], ALU.subtract)

        @block.tensor
        def _(pe):
            pe.wait_ge(k.load_sem["consts"], 16)
            pe.wait_ge(k.load_sem["ctx"], 16)
            for i in range(2):
                pe.transpose(k.ps[:, 0, i * P:(i + 1) * P], k.ctxn[:, i * P:(i + 1) * P],
                             c["ident"]).then_inc(turned.handle, 1)

        @block.scalar
        def _(act):
            act.wait_ge(turned.handle, turned.done + 2)
            v = k.ctxT[:, :].rearrange("p (b two s) -> p b two s", b=B, two=2)
            for i in range(2):
                act.activation(v[:, :, i, :], k.ps[:, 0, 0:256].rearrange("p (b s) -> p b s", b=B), ACT.Copy)
    split.done += 3
    turned.done += 2


def norm_turn(k, outs, turned_src=0, scale=None, bias=None, eps=1e-5, turn_it=True):
    stats, aggr, var, rstd, normed, turned = (k.sig(n) for n in (
        "ln_stats", "ln_aggr", "ln_var", "ln_rstd", "normed", "turned"))
    st = k.small[:, 0:48].rearrange("p (t s) -> p t s", s=6)
    mv = k.small[:, 48:64].rearrange("p (t s) -> p t s", s=2)
    n = len(outs)
    ve = k.small[:, 64:64 + 8 * n].rearrange("p (o t) -> p o t", o=n)
    rs = k.small[:, 96:96 + 8 * n].rearrange("p (o t) -> p o t", o=n)
    x3 = k.tiles(k.x)
    order = [turned_src] + [o for o in range(n) if o != turned_src]
    src = k.tiles(outs[turned_src][0])
    with k.nc.Block() as block:
        @block.vector
        def _(dve):
            for t in range(TILES):
                dve.bn_stats(st[:, t, :], x3[:, t, :]).then_inc(stats.handle, 1)
            for t in range(TILES):
                dve.wait_ge(stats.handle, stats.done + t + 1)
                dve.bn_aggr(mv[:, t, :], st[:, t, :]).then_inc(aggr.handle, 1)
            dve.wait_ge(aggr.handle, aggr.done + TILES)
            for o in range(n):
                dve.tensor_scalar(ve[:, o], mv[:, :, 1], outs[o][1][0], outs[o][1][1], ALU.mult,
                                  ALU.add).then_inc(var.handle, 1)
            dve.wait_ge(rstd.handle, rstd.done + 1)
            for o in order:
                for t in range(TILES):
                    dve.tensor_scalar(k.tiles(outs[o][0])[:, t, :], x3[:, t, :], mv[:, t, 0:1], rs[:, o, t:t + 1],
                                      ALU.subtract, ALU.mult).then_inc(normed.handle, 1)
                if o == turned_src and turn_it:
                    dve.wait_ge(turned.handle, turned.done + 8)
                    if bias is not None:
                        dve.tensor_scalar(k.xnT[:, 512:1024], k.ps[:, 1, :], scale, bias, ALU.mult, ALU.add)
                    elif scale is not None:
                        dve.tensor_scalar(k.xnT[:, 512:1024], k.ps[:, 1, :], scale, None, ALU.mult)
                    else:
                        dve.tensor_copy(k.xnT[:, 512:1024], k.ps[:, 1, :])

        @block.gpsimd
        def _(pool):
            pool.wait_ge(var.handle, var.done + n)
            half = k.c["neghalf"][:, 0:1].to_broadcast([P, 8 * n])
            pool.tensor_tensor(k.small[:, 96:96 + 8 * n], k.small[:, 64:64 + 8 * n], half, ALU.pow).then_inc(rstd.handle, 1)

        if turn_it:
            @block.tensor
            def _(pe):
                for t in range(TILES):
                    pe.wait_ge(normed.handle, normed.done + t + 1)
                    pe.transpose(k.ps[:, t // 4, (t % 4) * P:(t % 4 + 1) * P], src[:, t, :],
                                 k.c["ident"]).then_inc(turned.handle, 1)

            @block.scalar
            def _(act):
                act.wait_ge(turned.handle, turned.done + 4)
                if scale is None:
                    act.activation(k.xnT[:, 0:512], k.ps[:, 0, :], ACT.Copy)
                else:
                    act.activation(k.xnT[:, 0:512], k.ps[:, 0, :], ACT.Identity, scale=scale,
                                   bias=bias if bias is not None else 0.0)
    stats.done += TILES
    aggr.done += TILES
    var.done += n
    rstd.done += 1
    normed.done += n * TILES
    if turn_it:
        turned.done += TILES


def rms_turn(k, src, gain, eps):
    step, rstd, normed, turned = k.sig("rms_step"), k.sig("ln_rstd"), k.sig("normed"), k.sig("turned")
    ms, ve, rs = k.small[:, 48:56], k.small[:, 64:72], k.small[:, 72:80]
    sq, dst = k.tiles(k.work), k.tiles(k.xn)
    s3 = k.tiles(src)
    with k.nc.Block() as block:
        @block.vector
        def _(dve):
            dve.tensor_tensor(sq, s3, s3, ALU.mult).then_inc(step.handle, 1)
            dve.wait_ge(step.handle, step.done + 1)
            dve.tensor_reduce(ms, sq, X, ALU.add).then_inc(step.handle, 1)
            dve.wait_ge(step.handle, step.done + 2)
            dve.tensor_scalar(ve, ms, 1.0 / D, eps, ALU.mult, ALU.add).then_inc(step.handle, 1)
            dve.wait_ge(rstd.handle, rstd.done + 1)
            for t in range(TILES):
                dve.tensor_scalar(dst[:, t, :], s3[:, t, :], rs[:, t:t + 1], None, ALU.mult).then_inc(normed.handle, 1)
            dve.wait_ge(turned.handle, turned.done + 8)
            dve.tensor_scalar(k.xnT[:, 512:1024], k.ps[:, 1, :], gain, None, ALU.mult)

        @block.gpsimd
        def _(pool):
            pool.wait_ge(step.handle, step.done + 3)
            pool.tensor_tensor(rs, ve, k.c["neghalf"], ALU.pow).then_inc(rstd.handle, 1)

        @block.tensor
        def _(pe):
            for t in range(TILES):
                pe.wait_ge(normed.handle, normed.done + t + 1)
                pe.transpose(k.ps[:, t // 4, (t % 4) * P:(t % 4 + 1) * P], dst[:, t, :],
                             k.c["ident"]).then_inc(turned.handle, 1)

        @block.scalar
        def _(act):
            act.wait_ge(turned.handle, turned.done + 4)
            act.activation(k.xnT[:, 0:512], k.ps[:, 0, :], ACT.Identity, scale=gain)
    step.done += 3
    rstd.done += 1
    normed.done += TILES
    turned.done += TILES


def turn(k, src, dst):
    turned = k.sig("turned")
    s3 = k.tiles(src)
    with k.nc.Block() as block:
        @block.tensor
        def _(pe):
            for t in range(TILES):
                pe.transpose(k.ps[:, t // 4, (t % 4) * P:(t % 4 + 1) * P], s3[:, t, :],
                             k.c["ident"]).then_inc(turned.handle, 1)

        @block.scalar
        def _(act):
            act.wait_ge(turned.handle, turned.done + 4)
            act.activation(dst[:, 0:512], k.ps[:, 0, :], ACT.Copy)

        @block.vector
        def _(dve):
            dve.wait_ge(turned.handle, turned.done + 8)
            dve.tensor_copy(dst[:, 512:1024], k.ps[:, 1, :])
    turned.done += TILES


def add_row(k, pool, dst, row):
    d3 = k.tiles(dst)
    pool.tensor_tensor(d3, d3, row[:, None, :].to_broadcast([P, TILES, D]), ALU.add)


class Core:

    def __init__(self, k, heads, hd, keys):
        self.heads, self.hd, self.keys = heads, hd, keys
        self.ct = heads * keys // P
        self.groups = heads * hd // P
        self.cols = self.ct * P
        w, at = k.work, 0

        def take(n):
            nonlocal at
            at += n
            assert at <= WORK
            return w[:, at - n:at]

        self.qT = take(self.groups * 1024).rearrange("p (b g n) -> p b g n", b=B, g=self.groups)
        self.o = self.qT.rearrange("p b g n -> p (b g n)").rearrange("p (t n) -> p t n", t=TILES)
        self.kblk = take(B * self.cols).rearrange("p (b n) -> p b n", b=B)
        self.probs = take(2 * self.ct * 256).rearrange("p (r j n) -> p r j n", r=2, j=self.ct)
        if keys == SC:
            self.v = take(B * self.ct * 2 * (hd + 1)).rearrange("p (b j c) -> p b j c", b=B, j=self.ct)
        else:
            self.v = take(TILES * (hd + 1)).rearrange("p (t c) -> p t c", t=TILES)
        self.ot = k.small[:, 1024:1024 + 2 * self.groups * P if self.groups == 1 else 2048]
        self.otw = self.groups * P
        self.kT = self.probs.rearrange("p r j n -> p (r j n)")[:, 0:self.groups * 256]
        self.raw = self.probs.rearrange("p r j n -> p (r j n)")[:, 0:1024]

    def group(self, j):
        return j if self.groups > 1 else 0

    def kview(self):
        return self.kblk.rearrange("p b (g h s) -> p b g h s", g=self.groups, s=self.keys)


def project_kv(k, a, wk, bk, rope, wv, bv, beside=None):
    c = k.c
    kproj, kept, rot, step, vproj, cleared, ready = (k.sig(n) for n in (
        "k_proj", "k_kept", "k_rot", "k_step", "v_proj", "v_cleared", "k_ready"))
    ctx4 = k.ctxT[:, :].rearrange("p (b two s) -> p b two s", b=B, two=2)
    g, hd = a.groups, a.hd
    n = a.heads * hd
    hm = c["headmask16"] if g == 1 else c["headmask2"]
    hg = a.heads // g
    kv = a.kview()
    kt = a.kT.rearrange("p (g b s) -> p g b s", g=g, b=B)

    def spread(eng, b):
        for i in range(g):
            eng.tensor_tensor(kv[:, b, i], kt[:, i, b, None, :].to_broadcast([P, hg, SC]),
                              hm[:, :, None].to_broadcast([P, hg, SC]), ALU.mult)

    with k.nc.Block() as block:
        @block.tensor
        def _(pe):
            for i in range(g):
                pe.matmul(k.ps[:, i, 0:256], wk[:, i * P:(i + 1) * P], ctx4[:, :, 0, :], start=True,
                          stop=True).then_inc(kproj.handle, 1)
            for b in range(B):
                pe.matmul(k.ps[:, 4 + b, 0:n], ctx4[:, b].rearrange("p two s -> p (two s)"), wv, start=True,
                          stop=True).then_inc(vproj.handle, 1)
            if rope:
                pe.wait_ge(kept.handle, kept.done + 1)
                pe.matmul(k.ps[:, 1, 0:256], c["rot"], a.kT, start=True, stop=True).then_inc(rot.handle, 1)

        @block.scalar
        def _(act):
            for i in range(g):
                act.wait_ge(kproj.handle, kproj.done + i + 1)
                act.activation(a.kT[:, i * 256:(i + 1) * 256], k.ps[:, i, 0:256], ACT.Identity,
                               bias=bk if bk is not None else 0.0).then_inc(kept.handle, 1)

        @block.gpsimd
        def _(pool):
            pool.memset(a.v, 0.0).then_inc(cleared.handle, 1)
            if beside:
                beside[0](pool)
            else:
                pool.wait_ge(ready.handle, ready.done + 1)
                spread(pool, 3)

        if beside:
            block.sync(beside[1])

        @block.vector
        def _(dve):
            if rope:
                tmp = k.small[:, 128:384].rearrange("p (b s) -> p b s", b=B)
                kr = a.kT.rearrange("p (b s) -> p b s", b=B)
                sin = c["sinq"][:, None, 0:SC].to_broadcast([P, B, SC])
                cos = c["cosq"][:, None, 0:SC].to_broadcast([P, B, SC])
                dve.wait_ge(rot.handle, rot.done + 1)
                dve.tensor_tensor(tmp, k.ps[:, 1, 0:256].rearrange("p (b s) -> p b s", b=B), sin, ALU.mult)
                dve.tensor_tensor(kr, kr, cos, ALU.mult).then_inc(step.handle, 1)
                dve.wait_ge(step.handle, step.done + 1)
                dve.tensor_tensor(kr, kr, tmp, ALU.add).then_inc(ready.handle, 1)
            else:
                dve.wait_ge(kept.handle, kept.done + g)
                dve.memset(k.small[0:1, 80:81], 0.0).then_inc(ready.handle, 1)
            dve.wait_ge(ready.handle, ready.done + 1)
            for b in range(B if beside else B - 1):
                spread(dve, b)
            dve.wait_ge(cleared.handle, cleared.done + 1)
            for par in range(2):
                rows = slice(64 * par, 64 * par + 64)
                at = par * (hd + 1)
                dve.memset(a.v[rows, :, :, at + hd:at + hd + 1], 1.0)
                for b in range(B):
                    dve.wait_ge(vproj.handle, vproj.done + b + 1)
                    src = k.ps[rows, 4 + b, 0:n].rearrange("p (j two d) -> p j two d", two=2, d=hd)[:, :, par, :]
                    dst = a.v[rows, b, :, at:at + hd]
                    if bv is None:
                        dve.tensor_copy(dst, src)
                    else:
                        row = bv[rows, :].rearrange("p (j two d) -> p j two d", two=2, d=hd)[:, :, par, :]
                        dve.tensor_tensor(dst, src, row, ALU.add)
    kproj.done += g
    kept.done += g
    vproj.done += B
    cleared.done += 1
    ready.done += 1
    if rope:
        rot.done += 1
        step.done += 1


def project_q(k, a, wq, bq, rope, row=None):
    c = k.c
    proj, kept, rot, step = k.sig("q_proj"), k.sig("q_kept"), k.sig("q_rot"), k.sig("q_step")
    g = a.groups
    halves = [[a.raw[:, h * 512:(h + 1) * 512].rearrange("p (b s) -> p b s", s=S) if rope
               else a.qT[:, 2 * h:2 * h + 2, i, :] for h in range(2)] for i in range(g)]
    with k.nc.Block() as block:
        @block.tensor
        def _(pe):
            for i in range(g):
                for h in range(2):
                    pe.matmul(k.ps[:, 2 * i + h, :], wq[:, i * P:(i + 1) * P], k.xnT[:, h * 512:(h + 1) * 512],
                              start=True, stop=True).then_inc(proj.handle, 1)
            if rope:
                for h in range(2):
                    pe.wait_ge(kept.handle, kept.done + h + 1)
                    pe.matmul(k.ps[:, 4 + h, :], c["rot"], a.raw[:, h * 512:(h + 1) * 512],
                              start=True, stop=True).then_inc(rot.handle, 1)

        @block.scalar
        def _(act):
            for i in range(g):
                for h in range(2):
                    act.wait_ge(proj.handle, proj.done + 2 * i + h + 1)
                    act.activation(halves[i][h], k.ps[:, 2 * i + h, :].rearrange("p (b s) -> p b s", s=S), ACT.Identity,
                                   bias=bq if bq is not None else 0.0).then_inc(kept.handle, 1)

        if row is not None:
            @block.gpsimd
            def _(pool):
                add_row(k, pool, k.x, row)

        if rope:
            @block.vector
            def _(dve):
                sin = c["sinq"][:, None, :].to_broadcast([P, 2, S])
                cos = c["cosq"][:, None, :].to_broadcast([P, 2, S])
                tmp = k.small[:, 0:512].rearrange("p (b s) -> p b s", s=S)
                for h in range(2):
                    q = a.qT[:, 2 * h:2 * h + 2, 0, :]
                    r = a.raw[:, h * 512:(h + 1) * 512].rearrange("p (b s) -> p b s", s=S)
                    dve.wait_ge(kept.handle, kept.done + h + 1)
                    dve.tensor_tensor(q, r, cos, ALU.mult)
                    dve.wait_ge(rot.handle, rot.done + h + 1)
                    if h:
                        dve.wait_ge(step.handle, step.done + 2 * h)
                    dve.tensor_tensor(tmp, k.ps[:, 4 + h, :].rearrange("p (b s) -> p b s", s=S), sin,
                                      ALU.mult).then_inc(step.handle, 1)
                    dve.wait_ge(step.handle, step.done + 2 * h + 1)
                    dve.tensor_tensor(q, q, tmp, ALU.add).then_inc(step.handle, 1)
    proj.done += 2 * g
    kept.done += 2 * g
    if rope:
        rot.done += 2
        step.done += 4


def attend(k, a, mask, scale, wo, dst):
    nc, c = k.nc, k.c
    ct, cols, heads, hd = a.ct, a.cols, a.heads, a.hd
    banks = cols // BANK
    scored, topped = k.sig("scored"), k.sig("topped")
    mx = k.small[:, 0:TILES * heads]
    mx3 = mx.rearrange("p (t h) -> p t h", h=heads)
    slots = 4
    with nc.Block() as block:
        @block.tensor
        def _(pe):
            for t in range(TILES):
                if t >= slots:
                    pe.wait_ge(topped.handle, topped.done + t - slots + 1)
                tok = slice(t % 2 * P, (t % 2 + 1) * P)
                for n in range(banks):
                    out = k.ps[:, banks * (t % slots) + n, :]
                    if a.groups == 1:
                        ins = pe.matmul(out, a.qT[:, t // 2, 0, tok], a.kblk[:, t // 2, n * BANK:(n + 1) * BANK],
                                  start=True, stop=not mask)
                        for m, (by_key, ident) in enumerate(mask):
                            ins = pe.matmul(out, by_key(t // 2, t % 2 * P, P), ident, start=False,
                                            stop=m == len(mask) - 1)
                    else:
                        for j in range(4):
                            ins = pe.matmul(out[:, j * P:(j + 1) * P], a.qT[:, t // 2, j, tok],
                                            a.kblk[:, t // 2, j * P:(j + 1) * P], start=True, stop=True)
                ins.then_inc(scored.handle, 1)

        @block.vector
        def _(dve):
            for t in range(TILES):
                dve.wait_ge(scored.handle, scored.done + t + 1)
                b0 = banks * (t % slots)
                dve.tensor_reduce(mx3[:, t, :], k.ps[:, b0:b0 + banks, :].rearrange("p b (h s) -> p (b h) s", s=a.keys),
                                  X, ALU.max).then_inc(topped.handle, 1)
    scored.done += TILES
    topped.done += TILES

    step, turned = k.sig("max_step"), k.sig("turned")
    rest = k.small[:, 128:128 + TILES * heads].rearrange("p (t h) -> p t h", h=heads)
    parts = k.mparts[:, 0:TILES * 3 * heads].rearrange("p (t q h) -> p t q h", q=3, h=heads)
    mT = k.mT[0:3 * heads, :]
    psb = k.ps[:, 0:2, :].rearrange("p b n -> p (b n)").bitcast(BF16)
    with nc.Block() as block:
        @block.vector
        def _(dve):
            dve.tensor_copy(parts[:, :, 0, :], mx3).then_inc(step.handle, 1)
            dve.wait_ge(step.handle, step.done + 1)
            dve.tensor_tensor(rest, mx3, parts[:, :, 0, :], ALU.subtract).then_inc(step.handle, 1)
            dve.wait_ge(step.handle, step.done + 2)
            dve.tensor_copy(parts[:, :, 1, :], rest).then_inc(step.handle, 1)
            dve.wait_ge(step.handle, step.done + 3)
            dve.tensor_tensor(parts[:, :, 2, :], rest, parts[:, :, 1, :], ALU.subtract).then_inc(step.handle, 1)
            dve.wait_ge(turned.handle, turned.done + TILES)
            dve.tensor_copy(mT[:, :], psb[0:3 * heads, 0:1024])

        @block.tensor
        def _(pe):
            pe.wait_ge(step.handle, step.done + 4)
            for t in range(TILES):
                pe.transpose(psb[0:3 * heads, t * P:(t + 1) * P], parts[:, t].rearrange("p q h -> p (q h)"),
                             k.identb[:, :]).then_inc(turned.handle, 1)
    step.done += 4
    turned.done += TILES

    made, expd, summed, freed, recipd = (k.sig("st_made"), k.sig("expd"), k.sig("pv_done"), k.sig("o_done"),
                                         k.sig("recipd"))
    pairs = ct // 2
    nh = k.nh[heads]
    if a.keys == SC:
        vw = 2 * (hd + 1)
        per = min(ct, BANK // vw // 2 * 2) if hd == 64 else ct
        per = 2 if hd == 64 else ct
        vcols = per * vw
    else:
        per, vcols = ct, heads * (hd + 1)
    obanks = ct // per
    with nc.Block() as block:
        @block.tensor
        def _(pe):
            for b in range(B + 1):
                if b < B:
                    for i in range(pairs):
                        n = b * pairs + i
                        if n >= 4:
                            pe.wait_ge(expd.handle, expd.done + n - 3)
                        for jj in range(2):
                            j = 2 * i + jj
                            out = k.ps[:, n % 4, jj * 256:(jj + 1) * 256]
                            pe.matmul(out, a.kblk[:, b, j * P:(j + 1) * P], a.qT[:, b, a.group(j), :],
                                      start=True, stop=False)
                            for by_key, ident in mask:
                                pe.matmul(out, ident[:, 0:P], by_key(b, 0, S), start=False, stop=False)
                            ins = pe.matmul(out, nh[0:3 * heads, j * P:(j + 1) * P], mT[:, b * S:(b + 1) * S],
                                            start=False, stop=True)
                        ins.then_inc(made.handle, 1)
                if b >= 1:
                    c0 = b - 1
                    pe.wait_ge(expd.handle, expd.done + pairs * b)
                    for tl in range(2):
                        t = 2 * c0 + tl
                        if t >= 2:
                            pe.wait_ge(freed.handle, freed.done + t - 1)
                        for j in range(ct):
                            lhs = a.probs[:, c0 % 2, j, tl * P:(tl + 1) * P]
                            bank = 4 + (t % 2) * obanks + j // per
                            if a.keys == SC:
                                ins = pe.matmul(k.ps[:, bank, (j % per) * vw:(j % per + 1) * vw], lhs,
                                                a.v[:, c0, j, :], start=True, stop=True)
                            else:
                                ins = pe.matmul(k.ps[:, bank, j // 2 * (hd + 1):(j // 2 + 1) * (hd + 1)], lhs,
                                                a.v[:, 2 * c0 + j % 2, :], start=j % 2 == 0, stop=j % 2 == 1)
                        ins.then_inc(summed.handle, 1)

        @block.scalar
        def _(act):
            for b in range(B):
                if b >= 2:
                    act.wait_ge(summed.handle, summed.done + 2 * (b - 1))
                for i in range(pairs):
                    n = b * pairs + i
                    act.wait_ge(made.handle, made.done + n + 1)
                    act.activation(a.probs[:, b % 2, 2 * i:2 * i + 2, :],
                                   k.ps[:, n % 4, :].rearrange("p (j n) -> p j n", j=2), ACT.Exp,
                                   scale=scale).then_inc(expd.handle, 1)

        @block.vector
        def _(dve):
            rec = k.small[:, 256:256 + 2 * heads]
            for t in range(TILES):
                dve.wait_ge(summed.handle, summed.done + t + 1)
                b0 = 4 + (t % 2) * obanks
                hb = heads // obanks
                acc = k.ps[:, b0:b0 + obanks, 0:vcols].rearrange("p b (h c) -> p b h c", c=hd + 1)
                r = rec[:, (t % 2) * heads:(t % 2 + 1) * heads].rearrange("p (b h o) -> p b h o", b=obanks, o=1)
                if obanks == 1:
                    acc, r = acc[:, 0], r[:, 0]
                    out = a.o[:, t, :].rearrange("p (h c) -> p h c", c=hd)
                    parts_ = [(acc, r, out, [P, heads, hd])]
                else:
                    out = a.o[:, t, :].rearrange("p (b h c) -> p b h c", b=obanks, c=hd)
                    parts_ = [(acc[:, i], r[:, i], out[:, i], [P, hb, hd]) for i in range(obanks)]
                for n_, (pa, pr, po, shape) in enumerate(parts_):
                    dve.reciprocal(pr, pa[:, :, hd:hd + 1]).then_inc(recipd.handle, 1)
                    dve.wait_ge(recipd.handle, recipd.done + t * obanks + n_ + 1)
                    ins = dve.tensor_tensor(po, pa[:, :, 0:hd], pr.to_broadcast(shape), ALU.mult)
                ins.then_inc(freed.handle, 1)
    made.done += B * pairs
    expd.done += B * pairs
    summed.done += TILES
    freed.done += TILES
    recipd.done += TILES * obanks

    kept, out_made, added = k.sig("ot_kept"), k.sig("wo_made"), k.sig("wo_added")
    g = a.groups
    d3 = k.tiles(dst)
    with nc.Block() as block:
        @block.tensor
        def _(pe):
            for t in range(TILES + 1):
                if t < TILES:
                    if t >= 2:
                        pe.wait_ge(kept.handle, kept.done + t - 1)
                    for i in range(g):
                        ins = pe.transpose(k.ps[:, t % 2, i * P:(i + 1) * P], a.o[:, t, i * P:(i + 1) * P], c["ident"])
                    ins.then_inc(turned.handle, 1)
                if t >= 1:
                    u = t - 1
                    pe.wait_ge(kept.handle, kept.done + u + 1)
                    if u >= 2:
                        pe.wait_ge(added.handle, added.done + u - 1)
                    for i in range(g):
                        ins = pe.matmul(k.ps[:, 2 + u % 2, 0:P], a.ot[:, (u % 2) * a.otw + i * P:(u % 2) * a.otw + (i + 1) * P],
                                        wo[:, i * P:(i + 1) * P], start=i == 0, stop=i == g - 1)
                    ins.then_inc(out_made.handle, 1)

        @block.scalar
        def _(act):
            for t in range(TILES):
                act.wait_ge(turned.handle, turned.done + t + 1)
                if t >= 2:
                    act.wait_ge(out_made.handle, out_made.done + t - 1)
                act.activation(a.ot[:, (t % 2) * a.otw:(t % 2 + 1) * a.otw], k.ps[:, t % 2, 0:a.otw],
                               ACT.Copy).then_inc(kept.handle, 1)

        @block.vector
        def _(dve):
            for t in range(TILES):
                dve.wait_ge(out_made.handle, out_made.done + t + 1)
                dve.tensor_tensor(d3[:, t, :], k.ps[:, 2 + t % 2, 0:P], d3[:, t, :], ALU.add).then_inc(added.handle, 1)
    turned.done += TILES
    kept.done += TILES
    out_made.done += TILES
    added.done += TILES


def first_argmax(dve, step, n, val, top, hot, tmp, desc, e):
    shape = [P, TILES, e]
    d = desc[:, None, 0:e].to_broadcast(shape)
    dve.tensor_reduce(top, val, X, ALU.max).then_inc(step, 1)
    dve.wait_ge(step, n + 1)
    dve.tensor_tensor(hot, val, top[:, :, None].to_broadcast(shape), ALU.is_equal).then_inc(step, 1)
    dve.wait_ge(step, n + 2)
    dve.tensor_tensor(hot, hot, d, ALU.mult).then_inc(step, 1)
    dve.wait_ge(step, n + 3)
    dve.tensor_reduce(tmp, hot, X, ALU.max).then_inc(step, 1)
    dve.wait_ge(step, n + 4)
    dve.tensor_tensor(hot, tmp[:, :, None].to_broadcast(shape), d, ALU.is_equal).then_inc(step, 1)
    dve.wait_ge(step, n + 5)
    return n + 5


def logits(k, w, e, dst):
    made = k.sig("logits_made")
    with k.nc.Block() as block:
        @block.tensor
        def _(pe):
            for t in range(TILES):
                ins = pe.matmul(k.ps[:, 0, t * e:(t + 1) * e], k.xnT[:, t * P:(t + 1) * P], w, start=True, stop=True)
            ins.then_inc(made.handle, 1)

        @block.scalar
        def _(act):
            act.wait_ge(made.handle, made.done + 1)
            act.activation(dst, k.ps[:, 0, 0:TILES * e], ACT.Copy)
    made.done += 1


def softmax_top2(k, lg, e, bias, hot1, hot2, p1, p2, scratch):
    step, expd = k.sig("gate_step"), k.sig("gate_exp")
    v = lg.rearrange("p (t e) -> p t e", e=e)
    shape = [P, TILES, e]
    tmp, rest = scratch[:, 0:8], scratch[:, 8:8 + TILES * e].rearrange("p (t e) -> p t e", e=e)
    n0 = step.done
    with k.nc.Block() as block:
        @block.vector
        def _(dve):
            s = step.handle
            dve.tensor_tensor(v, v, bias[:, None, :].to_broadcast(shape), ALU.add).then_inc(s, 1)
            dve.wait_ge(s, n0 + 1)
            dve.tensor_reduce(tmp, v, X, ALU.max).then_inc(s, 1)
            dve.wait_ge(s, n0 + 2)
            dve.tensor_tensor(v, v, tmp[:, :, None].to_broadcast(shape), ALU.subtract).then_inc(s, 1)
            dve.wait_ge(expd.handle, expd.done + 1)
            dve.tensor_reduce(tmp, v, X, ALU.add).then_inc(s, 1)
            dve.wait_ge(s, n0 + 4)
            dve.reciprocal(tmp, tmp).then_inc(s, 1)
            dve.wait_ge(s, n0 + 5)
            dve.tensor_tensor(v, v, tmp[:, :, None].to_broadcast(shape), ALU.mult).then_inc(s, 1)
            dve.wait_ge(s, n0 + 6)
            n = first_argmax(dve, s, n0 + 6, v, p1, hot1, tmp, k.c["expdesc"], e)
            dve.scalar_tensor_tensor(rest, hot1, -2.0, v, ALU.mult, ALU.add).then_inc(s, 1)
            dve.wait_ge(s, n + 1)
            first_argmax(dve, s, n + 1, rest, p2, hot2, tmp, k.c["expdesc"], e)

        @block.scalar
        def _(act):
            act.wait_ge(step.handle, n0 + 3)
            act.activation(lg, lg, ACT.Exp).then_inc(expd.handle, 1)
    step.done += 17
    expd.done += 1


def moe_linear(k):
    c, nc = k.c, k.nc
    w = k.work
    lg = w[:, 0:128]
    hot1 = w[:, 128:256].rearrange("p (t e) -> p t e", e=16)
    hot2 = w[:, 256:384].rearrange("p (t e) -> p t e", e=16)
    p1, p2 = w[:, 384:392], w[:, 392:400]
    gate = w[:, 400:400 + 144].rearrange("p (t e) -> p t e", e=18)
    gateT = w[:, 1024:2048]
    scratch = w[:, 600:800]
    ws = w[:, 800:928]
    logits(k, c["f0cent"], 16, lg)
    softmax_top2(k, lg, 16, c["f0eb"], hot1, hot2, p1, p2, scratch)
    step, turned, made, done = k.sig("lin_step"), k.sig("turned"), k.sig("lin_made"), k.sig("lin_done")
    n0 = step.done
    kept = k.sig("lin_kept")
    x3 = k.tiles(k.x)
    with nc.Block() as block:
        @block.vector
        def _(dve):
            s = step.handle
            dve.tensor_tensor(hot1, hot1, hot2, ALU.add).then_inc(s, 1)
            dve.wait_ge(s, n0 + 1)
            dve.memset(gate[:, :, 16:18], 0.5)
            dve.tensor_tensor(gate[:, :, 0:16], hot1, lg.rearrange("p (t e) -> p t e", e=16), ALU.mult).then_inc(s, 1)
            dve.tensor_tensor(ws, c["f0ws"][:, 0:128], c["f0ws"][:, 128:256], ALU.add).then_inc(s, 1)
            dve.wait_ge(s, n0 + 3)
            dve.tensor_scalar(ws, ws, 0.5, None, ALU.mult).then_inc(s, 1)

        @block.gpsimd
        def _(pool):
            pool.tensor_tensor(k.x[:, :], k.x[:, :], k.xn[:, :], ALU.add)

        @block.tensor
        def _(pe):
            pe.wait_ge(step.handle, n0 + 4)
            for t in range(TILES):
                pe.transpose(k.ps[0:18, t // 4, t % 4 * P:(t % 4 + 1) * P], gate[:, t, :], c["ident"]).then_inc(turned.handle, 1)

        @block.scalar
        def _(act):
            act.wait_ge(turned.handle, turned.done + TILES)
            for h in range(2):
                act.activation(gateT[0:18, h * 512:(h + 1) * 512], k.ps[0:18, h, :], ACT.Copy)
    turned.done += TILES
    step.done += 4
    with nc.Block() as block:
        @block.tensor
        def _(pe):
            n = 0
            for t in range(TILES):
                tok = slice(t * P, (t + 1) * P)
                for q in range(5):
                    if n >= 8:
                        pe.wait_ge(done.handle, done.done + n - 7)
                    if q < 4:
                        ins = pe.matmul(k.ps[:, n % 8, :], k.xnT[:, tok], c["f0wr"][:, q * 512:(q + 1) * 512],
                                        start=True, stop=True)
                    else:
                        pe.matmul(k.ps[:, n % 8, 0:P], k.xnT[:, tok], ws, start=True, stop=False)
                        ins = pe.matmul(k.ps[:, n % 8, 0:P], gateT[0:18, tok], c["f0br"][0:18, :], start=False, stop=True)
                    ins.then_inc(made.handle, 1)
                    n += 1

        @block.vector
        def _(dve):
            n = m = 0
            for t in range(TILES):
                for q in range(5):
                    dve.wait_ge(made.handle, made.done + n + 1)
                    for i in range(4 if q < 4 else 1):
                        if m:
                            dve.wait_ge(kept.handle, kept.done + m)
                        out = k.ps[:, n % 8, i * P:(i + 1) * P]
                        if q < 4:
                            e = 4 * q + i
                            ins = dve.scalar_tensor_tensor(x3[:, t, :], out, gate[:, t, e:e + 1], x3[:, t, :],
                                                           ALU.mult, ALU.add)
                        else:
                            ins = dve.tensor_tensor(x3[:, t, :], out, x3[:, t, :], ALU.add)
                        ins.then_inc(kept.handle, 1)
                        m += 1
                    n += 1
                    dve.wait_ge(kept.handle, kept.done + m)
                    dve.tensor_copy(k.small[0:1, 0:1], k.c["ones"][0:1, 0:1]).then_inc(done.handle, 1)
    made.done += 40
    done.done += 40
    kept.done += 17 * TILES


def routing(k, e, w, score, rows):
    nc, c = k.nc, k.c
    lg = w["lg"]
    shape = [P, TILES, e]
    lg3 = lg.rearrange("p (t e) -> p t e", e=e)
    hot = w["hot"].rearrange("p (t e) -> p t e", e=e)
    step, expd, made = k.sig("route_step"), k.sig("gate_exp"), k.sig("route_made")
    n0 = step.done
    top, tmp8, pos, posi = w["top"], w["tmp8"], w["pos"], w["posi"]
    hotb, tot, incl, t1 = w["hotb"], w["tot"], w["incl"], w["t1"]
    ends, reach, mtab = w["ends"], w["reach"], w["mtab"]
    with nc.Block() as block:
        @block.vector
        def _(dve):
            s = step.handle
            n = first_argmax(dve, s, n0, lg3, top, hot, tmp8, c["expdesc"], e)
            dve.tensor_copy(hotb, w["hot"]).then_inc(s, 1)
            dve.wait_ge(expd.handle, expd.done + 1)
            dve.tensor_scalar(score, score, 1.0, None, ALU.add).then_inc(s, 1)
            dve.wait_ge(s, n + 2)
            dve.reciprocal(score, score).then_inc(s, 1)
            dve.wait_ge(made.handle, made.done + 2)
            dve.tensor_copy(tot.rearrange("p (e t) -> p t e", t=TILES),
                            k.ps[:, 2, 0:TILES * e].rearrange("p (t e) -> p t e", e=e)).then_inc(s, 1)
            dve.wait_ge(s, n + 4)
            dve.tensor_tensor_scan(incl, w["one256"], tot, 0.0,
                                   ALU.mult, ALU.add).then_inc(s, 1)
            dve.wait_ge(s, n + 5)
            inc3 = incl.rearrange("p (e t) -> p t e", t=TILES)
            t13 = t1.rearrange("p (t e) -> p t e", e=e)
            dve.tensor_tensor(t13, k.ps[:, 1, 0:TILES * e].rearrange("p (t e) -> p t e", e=e), inc3, ALU.add).then_inc(s, 1)
            dve.wait_ge(s, n + 6)
            dve.tensor_tensor(t1, t1, w["hot"], ALU.mult).then_inc(s, 1)
            dve.wait_ge(s, n + 7)
            dve.tensor_reduce(pos, t13, X, ALU.add).then_inc(s, 1)
            dve.wait_ge(s, n + 8)
            dve.tensor_copy(posi, pos).then_inc(s, 1)
            dve.tensor_copy(ends, incl.rearrange("p (e t) -> p e t", t=TILES)[:, :, TILES - 1]).then_inc(s, 1)
            dve.wait_ge(s, n + 10)
            dve.tensor_tensor(t13, ends[:, None, :].to_broadcast(shape), c["token_at"][:, :, None].to_broadcast(shape),
                              ALU.is_gt).then_inc(s, 1)
            dve.wait_ge(s, n + 11)
            m3 = mtab[:, 0:TILES * e].rearrange("p (t e) -> p t e", e=e)
            dve.tensor_copy(m3[:, :, 0:1], t13[:, :, 0:1])
            dve.tensor_tensor(m3[:, :, 1:e], t13[:, :, 1:e], t13[:, :, 0:e - 1], ALU.subtract)
            dve.memset(mtab[:, TILES * e:TILES * e + 1], 0.0)
            r3 = reach[0:1, 0:e * 7].rearrange("p (e t) -> p e t", t=7)
            dve.tensor_tensor(r3, ends[0:1, :, None].to_broadcast([1, e, 7]),
                              c["tile_end"][0:1, None, :].to_broadcast([1, e, 7]), ALU.is_gt).then_inc(s, 1)
            dve.wait_ge(s, n + 12)
            dve.tensor_reduce(w["re"][0:1, :], r3, X, ALU.add).then_inc(s, 1)
            dve.wait_ge(s, n + 13)
            dve.tensor_tensor(w["re"][0:1, :], w["re"][0:1, :], c["expert_at"][0:1, 0:e], ALU.add).then_inc(s, 1)
            dve.wait_ge(s, n + 14)
            steps = TILES + e
            p3 = w["walk"][0:1, 0:steps * (e - 1)].rearrange("p (i e) -> p i e", e=e - 1)
            dve.tensor_tensor(p3, c["step_at"][0:1, 0:steps, None].to_broadcast([1, steps, e - 1]),
                              w["re"][0:1, None, 0:e - 1].to_broadcast([1, steps, e - 1]), ALU.is_gt).then_inc(s, 1)
            dve.wait_ge(s, n + 15)
            ef, tf, mf = w["wf"][0:1, 0:40], w["wf"][0:1, 40:80], w["wf"][0:1, 80:120]
            dve.tensor_reduce(ef[:, 0:steps], p3, X, ALU.add).then_inc(s, 1)
            dve.wait_ge(s, n + 16)
            dve.tensor_tensor(tf[:, 0:steps], c["step_at"][0:1, 0:steps], ef[:, 0:steps], ALU.subtract).then_inc(s, 1)
            dve.wait_ge(s, n + 17)
            dve.scalar_tensor_tensor(mf[:, 0:steps], tf[:, 0:steps], float(e), ef[:, 0:steps], ALU.mult, ALU.add).then_inc(s, 1)
            dve.wait_ge(s, n + 18)
            dve.tensor_scalar(mf[:, 0:steps], mf[:, 0:steps], float(TILES * e), None, ALU.min)
            dve.tensor_scalar(tf[:, 0:steps], tf[:, 0:steps], float(TILES - 1), None, ALU.min).then_inc(s, 1)
            dve.wait_ge(s, n + 19)
            dve.tensor_copy(w["wi"][0:1, 0:40], ef)
            dve.tensor_copy(w["wi"][0:1, 40:80], tf)
            dve.tensor_copy(w["wi"][0:1, 80:120], mf)

        @block.scalar
        def _(act):
            act.wait_ge(step.handle, n0 + 5)
            act.activation(score, top, ACT.Exp, scale=-1.0).then_inc(expd.handle, 1)

        @block.tensor
        def _(pe):
            pe.wait_ge(step.handle, n0 + 6)
            pe.matmul(k.ps[:, 1, 0:TILES * e], w["geb"], hotb, start=True, stop=True).then_inc(made.handle, 1)
            pe.matmul(k.ps[:, 2, 0:TILES * e], w["oneb"], hotb, start=True, stop=True).then_inc(made.handle, 1)
    step.done += 24
    expd.done += 1
    made.done += 2


def route_buffers(k, e, base):
    sizes = [("lg", 8 * e), ("hot", 8 * e), ("tot", 8 * e), ("incl", 8 * e), ("t1", 8 * e), ("one256", 8 * e),
             ("mtab", 8 * e + 8), ("ends", e), ("re", e), ("walk", (8 + e) * (e - 1)), ("wf", 120),
             ("top", 8), ("tmp8", 8), ("pos", 8), ("score", 8), ("hotb", 4 * e), ("geb", 64), ("oneb", 64),
             ("posi", 8), ("wi", 128)]
    w = {}
    for name, n in sizes:
        v = k.work[:, base:base + n]
        base += n
        if name in ("posi", "score"):
            v = k.small[:, 900 + 8 * (name == "posi"):908 + 8 * (name == "posi")]
            base -= n
        if name in ("hotb", "geb", "oneb"):
            v = v.bitcast(BF16)
        if name in ("posi", "wi"):
            v = v.bitcast(I32)
        w[name] = v
    assert base <= WORK, base
    w["reach"] = w["lg"]
    with k.nc.Block() as block:
        @block.vector
        def _(dve):
            dve.memset(w["one256"], 1.0)
            dve.memset(w["wf"], 0.0)
            dve.tensor_copy(w["geb"], k.c["count_ge"])
            dve.tensor_copy(w["oneb"], k.c["ones"])
    return w


def scatter_rows(k, w, rows, scratch, sorted_rows):
    sent, back = k.sig("rows_scattered"), k.sig("sorted_loaded")
    r3 = k.tiles(rows)
    at = sent.done, back.done

    def pool_part(pool):
        for t in range(TILES):
            pool.indirect_dma_start(out=scratch, out_offset=bass.IndirectOffsetOnAxis(
                ap=w["posi"][:, t:t + 1].bitcast(U32), axis=0), in_=r3[:, t, :], in_offset=None).then_inc(sent.handle, 16)

    def sync_part(sp):
        sp.wait_ge(sent.handle, at[0] + 16 * TILES)
        sp.dma_start(k.tiles(sorted_rows), scratch.rearrange("(t p) d -> p t d", p=P)).then_inc(back.handle, 16)
        sp.wait_ge(back.handle, at[1] + 16)

    sent.done += 16 * TILES
    back.done += 16
    return pool_part, sync_part


def gather_rows(k, w, sorted_rows, scratch, rows):
    sent, back = k.sig("sorted_stored"), k.sig("rows_gathered")
    r3 = k.tiles(rows)
    at = sent.done, back.done

    def pool_part(pool):
        pool.wait_ge(sent.handle, at[0] + 16)
        for t in range(TILES):
            pool.indirect_dma_start(out=r3[:, t, :], out_offset=None, in_=scratch, in_offset=bass.IndirectOffsetOnAxis(
                ap=w["posi"][:, t:t + 1].bitcast(U32), axis=0)).then_inc(back.handle, 16)
        pool.wait_ge(back.handle, at[1] + 16 * TILES)

    def sync_part(sp):
        sp.dma_start(scratch.rearrange("(t p) d -> p t d", p=P), k.tiles(sorted_rows)).then_inc(sent.handle, 16)

    sent.done += 16
    back.done += 16 * TILES
    return pool_part, sync_part


def move_rows(k, parts):
    with k.nc.Block() as block:
        block.gpsimd(parts[0])
        block.sync(parts[1])


def walk_experts(k, w, e, srcT, y, layer):
    nc = k.nc
    steps = TILES + e
    gated = layer == 1
    ft = 2 if gated else 4
    each = 768 if gated else 1024
    wm = k.wmoe[:, 0:e * each].rearrange("p (e n) -> p e n", e=e)
    staged, up, act_done, hid, trn, hT_done, down, acc = (k.sig(n) for n in (
        "staged", "up_made", "silu_done", "hidden", "hidden_turned", "hT_kept", "down_made", "y_added"))
    base = {s: s.done for s in (staged, up, act_done, hid, trn, hT_done, down, acc)}
    at = 4096
    stage = [k.work[:, at + i * P:at + (i + 1) * P] for i in range(2)]
    sg = [k.work[:, at + 256 + i * 256:at + 512 + i * 256] for i in range(2)]
    hb = [k.work[:, at + 768 + i * 512:at + 768 + i * 512 + ft * P] for i in range(2)]
    ht = [k.work[:, at + 1792 + i * 512:at + 1792 + i * 512 + ft * P] for i in range(2)]
    tmp = [k.work[:, at + 2816 + i * P:at + 2816 + (i + 1) * P] for i in range(2)]
    y3 = k.tiles(y)
    s3 = srcT.rearrange("p (t n) -> p t n", n=P)
    mtab = w["mtab"]
    wi = w["wi"]

    def wait(eng, sig, n):
        eng.wait_ge(sig.handle, base[sig] + n)

    def entries(eng, kind, row, i, n, top):
        _, values = nc.values_load_multi_w_load_instructions(
            wi[0:1, bass.ds(i + 40 * row, n)], engines=(kind,), min_val=0, max_val=top,
            skip_runtime_bounds_check_because="routing() clamps the table, whose entries count comparisons")
        return values

    PE, ACTE, DVE = mybir.EngineType.PE, mybir.EngineType.Activation, mybir.EngineType.DVE

    with nc.Block() as block:
        @block.tensor
        def _(pe):
            def up_product(i, r, ex, free=True):
                wait(pe, staged, i + 1)
                if free:
                    wait(pe, hid, i - 1)
                pe.matmul(k.ps[:, r, :], stage[r], wm[:, ex, 0:512], start=True, stop=True).then_inc(up.handle, 1)

            def turn_hidden(i, r, free=True):
                wait(pe, hid, i + 1)
                if free:
                    wait(pe, hT_done, i - 1)
                for f in range(ft):
                    ins = pe.transpose(k.ps[:, 2 + r, f * P:(f + 1) * P], hb[r][:, f * P:(f + 1) * P], k.c["ident"])
                ins.then_inc(trn.handle, 1)

            def down_product(i, r, ex, free=True):
                wait(pe, hT_done, i + 1)
                if free:
                    wait(pe, acc, i - 1)
                for f in range(ft):
                    ins = pe.matmul(k.ps[:, 4 + r, 0:P], ht[r][:, f * P:(f + 1) * P],
                                    wm[:, ex, 512 + f * P:512 + (f + 1) * P], start=f == 0, stop=f == ft - 1)
                ins.then_inc(down.handle, 1)

            ex = entries(pe, PE, 0, 0, 4, e - 1)
            for i in range(4):
                up_product(i, i % 2, ex[i], i >= 2)
                if i >= 1:
                    turn_hidden(i - 1, (i - 1) % 2, i - 1 >= 2)
                if i >= 2:
                    down_product(i - 2, i % 2, ex[i - 2], i - 2 >= 2)
            with pe.Fori(4, steps, 4) as i:
                ex = entries(pe, PE, 0, i - 2, 6, e - 1)
                for u in range(4):
                    up_product(i + u, u % 2, ex[u + 2])
                    turn_hidden(i + u - 1, (u + 1) % 2)
                    down_product(i + u - 2, u % 2, ex[u])
            ex = entries(pe, PE, 0, steps - 2, 2, e - 1)
            turn_hidden(steps - 1, 1)
            down_product(steps - 2, 0, ex[0])
            down_product(steps - 1, 1, ex[1])

        @block.scalar
        def _(act):
            def stage_in(i, r, t, ex, free=True):
                if free:
                    wait(act, up, i - 1)
                if gated:
                    act.activation(stage[r], s3[:, t, :], ACT.Copy).then_inc(staged.handle, 1)
                else:
                    act.activation(stage[r], s3[:, t, :], ACT.Identity, scale=k.c["f3g"][:, bass.ds(ex, 1)],
                                   bias=k.c["f3b"][:, bass.ds(ex, 1)]).then_inc(staged.handle, 1)

            def silu(i, r, ex, free=True):
                wait(act, up, i + 1)
                if free:
                    wait(act, hid, i - 1)
                act.activation(sg[r], k.ps[:, r, 0:256], ACT.Silu).then_inc(act_done.handle, 1)

            def relu(i, r, ex, free=True):
                wait(act, trn, i + 1)
                if free:
                    wait(act, down, i - 1)
                for f in range(ft):
                    ins = act.activation(ht[r][:, f * P:(f + 1) * P], k.ps[:, 2 + r, f * P:(f + 1) * P], ACT.Relu,
                                         bias=k.c["f3b1"].rearrange("p (e f) -> p e f", f=4)[:, ex, f:f + 1])
                ins.then_inc(hT_done.handle, 1)

            def expert(i, n):
                return [None] * n if gated else entries(act, ACTE, 0, i, n, e - 1)

            after = silu if gated else relu
            t, ex = entries(act, ACTE, 1, 0, 4, TILES - 1), expert(0, 4)
            stage_in(0, 0, t[0], ex[0], False)
            stage_in(1, 1, t[1], ex[1], False)
            after(0, 0, ex[0], False)
            stage_in(2, 0, t[2], ex[2])
            after(1, 1, ex[1], False)
            stage_in(3, 1, t[3], ex[3])
            with act.Fori(2, steps - 2, 4) as i:
                t, ex = entries(act, ACTE, 1, i + 2, 4, TILES - 1), expert(i, 6)
                for u in range(4):
                    after(i + u, u % 2, ex[u])
                    stage_in(i + u + 2, u % 2, t[u], ex[min(u + 2, len(ex) - 1)])
            ex = expert(steps - 2, 2)
            after(steps - 2, 0, ex[0])
            after(steps - 1, 1, ex[1])

        @block.vector
        def _(dve):
            def hidden(i, r, free=True):
                wait(dve, act_done if gated else up, i + 1)
                if free:
                    wait(dve, trn, i - 1)
                if gated:
                    dve.tensor_tensor(hb[r], k.ps[:, r, 256:512], sg[r], ALU.mult).then_inc(hid.handle, 1)
                else:
                    dve.tensor_copy(hb[r], k.ps[:, r, :]).then_inc(hid.handle, 1)

            def keep_turned(i, r, free=True):
                if not gated:
                    return
                wait(dve, trn, i + 1)
                if free:
                    wait(dve, down, i - 1)
                dve.tensor_copy(ht[r], k.ps[:, 2 + r, 0:ft * P]).then_inc(hT_done.handle, 1)

            def add_up(i, r, t, m, ex, free=True):
                wait(dve, down, i + 1)
                src = k.ps[:, 4 + r, 0:P]
                if not gated:
                    dve.tensor_tensor(tmp[r], src, k.c["f3b2"].rearrange("p (e n) -> p e n", e=e)[:, ex, :],
                                      ALU.add).then_inc(act_done.handle, 1)
                    wait(dve, act_done, i + 1)
                    src = tmp[r]
                if free:
                    wait(dve, acc, i)
                dve.scalar_tensor_tensor(y3[:, t, :], src, mtab[:, bass.ds(m, 1)], y3[:, t, :],
                                         ALU.mult, ALU.add).then_inc(acc.handle, 1)

            def indices(i, n):
                return (entries(dve, DVE, 1, i, n, TILES - 1), entries(dve, DVE, 2, i, n, TILES * e),
                        [None] * n if gated else entries(dve, DVE, 0, i, n, e - 1))

            dve.memset(y[:, 0:1024], 0.0)
            t, m, ex = indices(0, 2)
            for i in range(4):
                hidden(i, i % 2, i >= 2)
                if i >= 1:
                    keep_turned(i - 1, (i - 1) % 2, i - 1 >= 2)
                if i >= 2:
                    add_up(i - 2, i % 2, t[i - 2], m[i - 2], ex[i - 2], i >= 3)
            with dve.Fori(4, steps, 4) as i:
                t, m, ex = indices(i - 2, 4)
                for u in range(4):
                    hidden(i + u, u % 2)
                    keep_turned(i + u - 1, (u + 1) % 2)
                    add_up(i + u - 2, u % 2, t[u], m[u], ex[u])
            t, m, ex = indices(steps - 2, 2)
            keep_turned(steps - 1, 1)
            add_up(steps - 2, 0, t[0], m[0], ex[0])
            add_up(steps - 1, 1, t[1], m[1], ex[1])
    for s in base:
        s.done += steps


def swiglu_dense(k, experts, wg, wu, wd, ft, weights, dst, beside=None):
    nc = k.nc
    made, silud, hid, down, acc = (k.sig(n) for n in ("up_made", "silu_done", "hidden", "down_made", "y_added"))
    b = {s: s.done for s in (made, silud, hid, down, acc)}
    sg = [k.work[:, 4096 + i * 512:4608 + i * 512] for i in range(2)]
    h = [k.work[:, 5120 + i * 512 * ft:5120 + (i + 1) * 512 * ft] for i in range(2)]
    d3 = k.tiles(dst)
    items = [(e, half) for e in experts for half in range(2)]

    with nc.Block() as block:
        if beside:
            block.gpsimd(beside[0])
            block.sync(beside[1])

        @block.tensor
        def _(pe):
            for i in range(len(items) + 1):
                if i < len(items):
                    e, half = items[i]
                    for f in range(ft):
                        n = i * ft + f
                        if n >= 2:
                            pe.wait_ge(hid.handle, b[hid] + n - 1)
                        rhs = k.xnT[:, half * 512:(half + 1) * 512]
                        pe.matmul(k.ps[:, 2 * (n % 2), :], wg(e, f), rhs, start=True, stop=True)
                        pe.matmul(k.ps[:, 2 * (n % 2) + 1, :], wu(e, f), rhs, start=True, stop=True).then_inc(made.handle, 1)
                if i >= 1:
                    m = i - 1
                    e, half = items[m]
                    pe.wait_ge(hid.handle, b[hid] + ft * (m + 1))
                    if m >= 2:
                        pe.wait_ge(acc.handle, b[acc] + 4 * (m - 1))
                    for q in range(4):
                        for f in range(ft):
                            ins = pe.matmul(k.ps[:, 4 + m % 2, q * P:(q + 1) * P],
                                            h[m % 2][:, f * 512 + q * P:f * 512 + (q + 1) * P], wd(e, f),
                                            start=f == 0, stop=f == ft - 1)
                    ins.then_inc(down.handle, 1)

        @block.scalar
        def _(act):
            for n in range(len(items) * ft):
                act.wait_ge(made.handle, b[made] + n + 1)
                if n >= 2:
                    act.wait_ge(hid.handle, b[hid] + n - 1)
                act.activation(sg[n % 2], k.ps[:, 2 * (n % 2), :], ACT.Silu).then_inc(silud.handle, 1)

        @block.vector
        def _(dve):
            def hidden(n):
                i, f = n // ft, n % ft
                dve.wait_ge(silud.handle, b[silud] + n + 1)
                if i >= 2:
                    dve.wait_ge(down.handle, b[down] + i - 1)
                dve.tensor_tensor(h[i % 2][:, f * 512:(f + 1) * 512], k.ps[:, 2 * (n % 2) + 1, :], sg[n % 2],
                                  ALU.mult).then_inc(hid.handle, 1)

            def add_up(m):
                e, half = items[m]
                dve.wait_ge(down.handle, b[down] + m + 1)
                for q in range(4):
                    t = half * 4 + q
                    if m >= 2 and q == 0:
                        dve.wait_ge(acc.handle, b[acc] + 4 * m - 4)
                    src = k.ps[:, 4 + m % 2, q * P:(q + 1) * P]
                    wt = weights(e, t)
                    if wt is None:
                        dve.tensor_tensor(d3[:, t, :], src, d3[:, t, :], ALU.add).then_inc(acc.handle, 1)
                    else:
                        dve.scalar_tensor_tensor(d3[:, t, :], src, wt, d3[:, t, :], ALU.mult, ALU.add).then_inc(acc.handle, 1)

            for i in range(len(items)):
                for f in range(ft):
                    hidden(i * ft + f)
                if i >= 1:
                    add_up(i - 1)
            add_up(len(items) - 1)
    made.done += len(items) * ft
    silud.done += len(items) * ft
    hid.done += len(items) * ft
    down.done += len(items)
    acc.done += 4 * len(items)


def wait_load(k, names):
    with k.nc.Block() as block:
        @block.sync
        def _(sp):
            for name in names:
                sp.wait_ge(k.load_sem[name], 32 if name == "mask" else 16)


def build(nc, dram):
    with ExitStack() as ctx:
        k = Program(nc, ctx, dram)
        c = k.c
        k.mparts = k.sb("mparts", TILES * 48, BF16)
        k.mT = k.sb("mT", 1024, BF16)
        start_loads(k)
        wait_load(k, ["consts", "patterns", "x", "ctx", "mask", "l0a"])
        constants(k)

        a = Core(k, H, 8, SC)
        project_kv(k, a, c["a0wk"], c["a0bk"], False, c["a0wv"], c["a0bv"])
        norm_turn(k, [(k.xn, LN)])
        project_q(k, a, c["a0wq"], c["a0bq"], False, c["a0bo"])
        mask0 = [(lambda b, at, n: k.mb[0:SC, b * S + at:b * S + at + n], k.i64big[0:SC, :])]
        attend(k, a, mask0, 8 ** -0.5, c["a0wo"], k.x)

        norm_turn(k, [(k.xn, LN)])
        wait_load(k, ["l0f"])
        moe_linear(k)

        with nc.Block() as block:
            @block.sync
            def _(sp):
                sp.dma_start(k.wmoe[:, EARLY:L1M], dram["moe1"][:, EARLY:L1M]).then_inc(k.load_sem["moe1b"], 16)

        wait_load(k, ["l1a"])
        norm_turn(k, [(k.xn, LN_LN)], 0, c["a1g"], c["a1b"])
        gate_step = k.sig("tanh_step")
        with nc.Block() as block:
            @block.scalar
            def _(act):
                act.activation(k.small[:, 100:101], c["a1gate"], ACT.Tanh).then_inc(gate_step.handle, 1)

            @block.vector
            def _(dve):
                dve.wait_ge(gate_step.handle, 1)
                dve.tensor_scalar(c["a1wo"], c["a1wo"], k.small[:, 100:101], None, ALU.mult)
                dve.tensor_scalar(c["a1bo"], c["a1bo"], k.small[:, 100:101], None, ALU.mult)
        for half in range(2):
            a = Core(k, 8, 64, SC)
            part = slice(half * 512, half * 512 + 512)
            project_kv(k, a, c["a1wk"][:, part], None, False, c["a1wv"][:, part], None)
            project_q(k, a, c["a1wq"][:, part], None, False, c["a1bo"] if half == 0 else None)
            attend(k, a, [], 64 ** -0.5, c["a1wo"][:, part], k.x)

        norm_turn(k, [(k.xn, LN)])
        wait_load(k, ["l1s"])
        w = route_buffers(k, 32, 7168)
        logits(k, c["f1gw"], 32, w["lg"])
        y, srt, xsT = k.work[:, 0:1024], k.work[:, 1024:2048], k.work[:, 2048:3072]
        xs = k.small[:, 1024:2048]
        routing(k, 32, w, w["score"], None)
        with nc.Block() as block:
            @block.vector
            def _(dve):
                dve.tensor_tensor(k.tiles(xs), k.tiles(k.xn), w["score"][:, :, None].to_broadcast([P, TILES, D]), ALU.mult)
        scatter = scatter_rows(k, w, xs, dram["scratch0"], srt)
        sgu, sd = c["f1sgu"], c["f1sd"]
        swiglu_dense(k, [0], lambda e, f: sgu[:, f * P:(f + 1) * P], lambda e, f: sgu[:, 256 + f * P:256 + (f + 1) * P],
                     lambda e, f: sd[:, f * P:(f + 1) * P], 2, lambda e, t: None, k.x, scatter)
        turn(k, srt, xsT)
        wait_load(k, ["moe1", "moe1b"])
        walk_experts(k, w, 32, xsT, y, 1)
        gather = gather_rows(k, w, y, dram["scratch1"], xs)
        with nc.Block() as block:
            @block.sync
            def _(sp):
                for name in ("l2a", "l2f", "l3a"):
                    sp.dma_start(dict(k.loads)[name], dram[name]).then_inc(k.load_sem[name], 16)
                sp.dma_start(k.wmoe[:, 0:L3M], dram["moe3"]).then_inc(k.load_sem["moe3"], 16)

        a = Core(k, H, 8, SC)
        wait_load(k, ["l2a"])
        project_kv(k, a, c["a2wk"], c["a2bk"], True, c["a2wv"], c["a2bv"], gather)
        with nc.Block() as block:
            @block.vector
            def _(dve):
                dve.tensor_tensor(k.x[:, :], k.x[:, :], xs, ALU.add)
        norm_turn(k, [(k.xn, LN)])
        project_q(k, a, c["a2wq"], c["a2bq"], True, c["a2bo"])
        attend(k, a, [], 8 ** -0.5, c["a2wo"], k.x)

        wait_load(k, ["l2f", "l3a"])
        xl = k.sb("xl", 1024)
        norm_turn(k, [(xl, LN), (k.xn, LN_RMS)], 1, c["f2g1"])
        a = Core(k, 4, 32, S)
        kept, made = k.sig("k_kept"), k.sig("v_proj")
        with nc.Block() as block:
            @block.tensor
            def _(pe):
                for h in range(2):
                    pe.matmul(k.ps[:, h, :], c["f2wkc"], k.xnT[:, h * 512:(h + 1) * 512], start=True,
                              stop=True).then_inc(kept.handle, 1)
                for t in range(TILES):
                    ins = pe.matmul(k.ps[:, 2, t * 32:(t + 1) * 32], k.xnT[:, t * P:(t + 1) * P], c["f2wvc"],
                                    start=True, stop=True)
                ins.then_inc(made.handle, 1)

            @block.vector
            def _(dve):
                for b in range(B):
                    dve.wait_ge(kept.handle, kept.done + b // 2 + 1)
                    src = k.ps[:, b // 2, b % 2 * S:(b % 2 + 1) * S]
                    dve.tensor_tensor(a.kblk[:, b, :].rearrange("p (h s) -> p h s", s=S),
                                      src[:, None, :].to_broadcast([P, 4, S]),
                                      c["headmask4"][:, :, None].to_broadcast([P, 4, S]), ALU.mult)

            @block.scalar
            def _(act):
                act.wait_ge(made.handle, made.done + 1)
                act.activation(a.v[:, :, 0:32], k.ps[:, 2, 0:256].rearrange("p (t d) -> p t d", d=32), ACT.Copy)

            @block.gpsimd
            def _(pool):
                pool.memset(a.v[:, :, 32:33], 1.0)
        kept.done += 2
        made.done += 1
        project_q(k, a, c["f2wq"], None, False)
        attend(k, a, [], 32 ** -0.5, c["f2wo"], xl)
        rms_turn(k, xl, c["f2g2"], 1e-6)
        wk = k.work
        lg = wk[:, 0:64]
        hot1 = wk[:, 64:128].rearrange("p (t e) -> p t e", e=8)
        hot2 = wk[:, 128:192].rearrange("p (t e) -> p t e", e=8)
        p1, p2, comb = wk[:, 192:200], wk[:, 200:208], wk[:, 208:272].rearrange("p (t e) -> p t e", e=8)
        logits(k, c["f2wr"], 8, lg)
        softmax_top2(k, lg, 8, c["f2eb"], hot1, hot2, p1, p2, wk[:, 300:400])
        step, expd = k.sig("gate_step"), k.sig("gate_exp")
        n0 = step.done
        with nc.Block() as block:
            @block.vector
            def _(dve):
                s = step.handle
                dve.tensor_tensor(p2, p2, p1, ALU.subtract).then_inc(s, 1)
                dve.wait_ge(expd.handle, expd.done + 1)
                dve.tensor_scalar(p1, p2, 1.0, None, ALU.add).then_inc(s, 1)
                dve.wait_ge(s, n0 + 2)
                dve.reciprocal(p1, p1).then_inc(s, 1)
                dve.wait_ge(s, n0 + 3)
                dve.tensor_tensor(p2, p2, p1, ALU.mult).then_inc(s, 1)
                dve.tensor_tensor(hot1, hot1, p1[:, :, None].to_broadcast([P, TILES, 8]), ALU.mult).then_inc(s, 1)
                dve.wait_ge(s, n0 + 5)
                dve.tensor_tensor(hot2, hot2, p2[:, :, None].to_broadcast([P, TILES, 8]), ALU.mult).then_inc(s, 1)
                dve.wait_ge(s, n0 + 6)
                dve.tensor_tensor(comb, hot1, hot2, ALU.add)

            @block.scalar
            def _(act):
                act.wait_ge(step.handle, n0 + 1)
                act.activation(p2, p2, ACT.Exp).then_inc(expd.handle, 1)
        step.done += 6
        expd.done += 1
        swiglu_dense(k, list(range(9)), lambda e, f: c["f2w1"][:, e * P:(e + 1) * P],
                     lambda e, f: c["f2w3"][:, e * P:(e + 1) * P], lambda e, f: c["f2w2"][:, e * P:(e + 1) * P], 1,
                     lambda e, t: comb[:, t, e:e + 1] if e < 8 else None, xl)
        with nc.Block() as block:
            @block.vector
            def _(dve):
                dve.tensor_tensor(k.x[:, :], k.x[:, :], xl[:, :], ALU.add)

        a = Core(k, H, 8, SC)
        project_kv(k, a, c["a3wk"], None, False, c["a3wv"], None)
        norm_turn(k, [(k.xn, LN)])
        project_q(k, a, c["a3wq"], None, False)
        mask3 = [(lambda b, at, n, q=q: k.mb3[0:SC, q * 256 + at:q * 256 + at + n], k.i64[0:SC, :]) for q in range(3)]
        attend(k, a, mask3, D ** -0.5, c["a3wo"], k.x)

        norm_turn(k, [(k.xn, LN), (xs, LN_LN)])
        w = route_buffers(k, 8, 7168)
        logits(k, c["f3cent"], 8, w["lg"])
        routing(k, 8, w, w["score"], None)
        move_rows(k, scatter_rows(k, w, xs, dram["scratch0"], srt))
        turn(k, srt, xsT)
        wait_load(k, ["moe3"])
        walk_experts(k, w, 8, xsT, y, 3)
        move_rows(k, gather_rows(k, w, y, dram["scratch1"], xs))
        step = k.sig("addrow")
        with nc.Block() as block:
            @block.vector
            def _(dve):
                dve.tensor_tensor(k.tiles(xs), k.tiles(xs), w["score"][:, :, None].to_broadcast([P, TILES, D]),
                                  ALU.mult).then_inc(step.handle, 1)
                dve.tensor_tensor(k.x[:, :], k.x[:, :], k.xn[:, :], ALU.add).then_inc(step.handle, 1)
                dve.wait_ge(step.handle, step.done + 2)
                dve.tensor_tensor(k.x[:, :], k.x[:, :], xs, ALU.add)
        step.done += 2
        stored = k.sig("stored")
        with nc.Block() as block:
            @block.sync
            def _(sp):
                sp.dma_start(dram["out"], k.x[:, :]).then_inc(stored.handle, 16)
                sp.wait_ge(stored.handle, 16)


def shape_constants():
    r = np.arange(P)
    f = {}
    f["ident"] = np.eye(P)
    f["count_ge"] = -1.0 * (r[:, None] >= r[None, :])
    f["ones"] = np.ones((P, P))
    f["headmask16"] = r[:, None] // 8 == np.arange(16)
    f["headmask4"] = r[:, None] // 32 == np.arange(4)
    f["headmask2"] = r[:, None] // 64 == np.arange(2)
    f["i64rep"] = r[:, None] % 128 == np.arange(512) % 64
    for name, heads, n, keys in (("neghead16", 16, 1024, 64), ("neghead4", 4, 1024, 256), ("neghead8", 8, 512, 64)):
        f[name] = -((r[:, None] % heads == np.arange(n) // keys) & (r[:, None] < 3 * heads)).astype(np.float32)
    dim = 4
    freqs = np.exp(-np.arange(dim, dtype=np.float32) * np.log(np.float32(10000.0)) / np.float32(dim)).astype(np.float32)
    ang = (np.arange(S, dtype=np.float32)[None, :] * freqs[(r % 8) // 2][:, None]).astype(np.float32)
    f["cosq"], f["sinq"] = np.cos(ang), np.sin(ang)
    rot = np.zeros((P, P))
    rot[r[1::2], r[0::2]] = -1.0
    rot[r[0::2], r[1::2]] = 1.0
    f["rot"] = rot
    f["expdesc"] = np.broadcast_to(64 - np.arange(32), (P, 32))
    f["token_at"] = r[:, None] + P * np.arange(8)
    f["tile_end"] = np.broadcast_to(P * np.arange(1, 8), (P, 7))
    f["expert_at"] = np.broadcast_to(np.arange(32), (P, 32))
    f["step_at"] = np.broadcast_to(np.arange(40), (P, 40))
    f["neghalf"] = np.full((P, 8), -0.5)
    return {n: np.asarray(v, np.float32) for n, v in f.items()}


def kernel(**i):
    import concourse.bacc as bacc
    from concourse.bass_utils import run_bass_kernel_spmd as run

    i = {n: np.asarray(v) for n, v in i.items()}

    def rows(v):
        v = v.reshape(1, -1)
        return np.broadcast_to(v, (P, v.shape[1]))

    def by_in(w):
        return w.transpose(1, 0, 2).reshape(w.shape[1], -1)

    def by_tile(w):
        return w.reshape(-1, P, w.shape[-1]).transpose(1, 0, 2).reshape(P, -1)

    def pad(v):
        out = np.zeros((P, v.shape[1]), v.dtype)
        out[0:v.shape[0]] = v
        return out

    f = shape_constants()
    wkv, bkv = i["L0_xattn_W_kv"].reshape(D, H, 2, 8), i["L0_xattn_b_kv"].reshape(H, 2, 8)
    f["a0wk"], f["a0wv"] = wkv[:, :, 0].reshape(D, D), wkv[:, :, 1].reshape(D, D)
    f["a0bk"], f["a0bv"] = bkv[:, 0].reshape(D, 1), rows(bkv[:, 1])
    f["a0wq"], f["a0bq"] = i["L0_xattn_W_q"], i["L0_xattn_b_q"].reshape(D, 1)
    f["a0wo"], f["a0bo"] = i["L0_xattn_W_o"], rows(i["L0_xattn_b_o"])
    f["f0wr"] = by_in(i["L0_ffn_Wr"].transpose(0, 2, 1))
    f["f0ws"] = by_in(i["L0_ffn_Ws"].transpose(0, 2, 1))
    f["f0cent"], f["f0eb"] = i["L0_ffn_centroids"].T, rows(i["L0_ffn_expert_biases"])
    f["f0br"] = pad(np.concatenate([i["L0_ffn_br"], i["L0_ffn_bs"]]))
    f["a1wk"], f["a1wv"] = i["L1_xattn_w_kv"][:, :1024], i["L1_xattn_w_kv"][:, 1024:]
    f["a1wq"], f["a1wo"] = i["L1_xattn_w_q"], by_tile(i["L1_xattn_w_out"])
    f["a1bo"], f["a1g"], f["a1b"] = rows(i["L1_xattn_b_out"]), i["L1_xattn_ln_gamma"].reshape(D, 1), i["L1_xattn_ln_beta"].reshape(D, 1)
    f["a1gate"] = rows(i["L1_xattn_gate"])
    f["f1gw"] = i["L1_ffn_gate_w"]
    f["f1sgu"] = np.concatenate([i["L1_ffn_shared_gate_w"], i["L1_ffn_shared_up_w"]], 1)
    f["f1sd"] = by_tile(i["L1_ffn_shared_down_w"])
    for n in "kvq":
        f[f"a2w{n}"] = i[f"L2_xattn_w{n}"].T
    f["a2wo"], f["a2bo"] = i["L2_xattn_wo"].T, rows(i["L2_xattn_bo"])
    f["a2bk"], f["a2bq"], f["a2bv"] = i["L2_xattn_bk"].reshape(D, 1), i["L2_xattn_bq"].reshape(D, 1), rows(i["L2_xattn_bv"])
    f["f2g1"], f["f2g2"] = i["L2_ffn_g1"].reshape(D, 1), i["L2_ffn_g2"].reshape(D, 1)
    f["f2wq"], f["f2wkc"], f["f2wvc"] = i["L2_ffn_Wq"].T, np.tile(i["L2_ffn_Wkc"].T, (1, 4)), i["L2_ffn_Wvc"].T
    f["f2wo"], f["f2wr"], f["f2eb"] = i["L2_ffn_Wo"].T, i["L2_ffn_Wr"].T, rows(i["L2_ffn_expert_bias"])
    for n in "123":
        both = np.concatenate([i[f"L2_ffn_eW{n}"], i[f"L2_ffn_sW{n}"][None]])
        f[f"f2w{n}"] = by_in(both.transpose(0, 2, 1))
    f["a3wk"], f["a3wv"] = i["L3_xattn_Wkv"][:D].T, i["L3_xattn_Wkv"][D:].T
    f["a3wq"], f["a3wo"] = i["L3_xattn_Wq"].T, i["L3_xattn_Wout"].T
    f["f3cent"], f["f3g"], f["f3b"] = i["L3_ffn_centroids"].T, i["L3_ffn_ln_g"].T, i["L3_ffn_ln_b"].T
    f["f3b1"] = i["L3_ffn_b1"].reshape(8, 4, P).transpose(2, 0, 1).reshape(P, 32)
    f["f3b2"] = rows(i["L3_ffn_b2"])

    arrays = {}
    for name, group in GROUPS:
        for n, wd in group:
            assert f[n].shape == (P, wd), (n, f[n].shape)
        arrays[name] = np.concatenate([f[n] for n, _ in group], 1)
    arrays["moe1"] = by_in(np.concatenate([
        i["L1_ffn_routed_gate_w"], i["L1_ffn_routed_up_w"],
        i["L1_ffn_routed_down_w"].reshape(32, 2, P, D).transpose(0, 2, 1, 3).reshape(32, P, 256)], 2))
    arrays["moe3"] = by_in(np.concatenate([
        i["L3_ffn_w1"], i["L3_ffn_w2"].reshape(8, 4, P, D).transpose(0, 2, 1, 3).reshape(8, P, 512)], 2))
    arrays["x"] = by_tile(i["x"].reshape(B * S, D))
    arrays["ctx"] = by_tile(i["ctx_1024"].reshape(B * SC, D))
    arrays["mask0"] = i["mask_BxSxS2_ik0"].transpose(2, 0, 1).reshape(SC, B * S)
    arrays["mask3"] = i["mask_SxS2_fk0"].T
    arrays = {n: np.ascontiguousarray(a) for n, a in arrays.items()}

    nc = bacc.Bacc("TRN2", target_bir_lowering=False, num_devices=1)
    dram = {n: nc.dram_tensor(n + "_in", a.shape, mybir.dt.from_np(a.dtype), kind="ExternalInput").ap()
            for n, a in arrays.items()}
    dram["out"] = nc.dram_tensor("out", [P, TILES * D], F32, kind="ExternalOutput").ap()
    dram["scratch0"] = nc.dram_tensor("sorted_in", [B * S, D], F32, kind="Internal").ap()
    dram["scratch1"] = nc.dram_tensor("sorted_out", [B * S, D], F32, kind="Internal").ap()
    build(nc, dram)
    r = run(nc, [{n + "_in": a for n, a in arrays.items()}], core_ids=[0])
    out = r.results[0]["out"]
    return out.reshape(P, TILES, D).transpose(1, 0, 2).reshape(B, S, D)
```

```python
from contextlib import ExitStack

import numpy as np
import concourse.bass as bass
from concourse import mybir

F32 = mybir.dt.float32
BF16 = mybir.dt.bfloat16
I32 = mybir.dt.int32
U32 = mybir.dt.uint32
ALU = mybir.AluOpType
ACT = mybir.ActivationFunctionType
X = mybir.AxisListType.X

P = 128
B, S, D = 4, 256, 128
SC = 64
TILES = B * S // P
H = 16
BANK = 512
BIG = -1e20
Q_PARTS, K_PARTS = (0, 0, 1, 0, 2, 1), (0, 1, 0, 2, 0, 1)
PART_AT = (1, 3, 4)
PAIR = 16
STACK = PAIR * len(Q_PARTS)
E5, E6 = 1e-5, 1e-6
LN = (1.0, E5)
LN_LN = (1.0 + E5, E5 * E5)
LN_RMS = (1.0 + E6, E6 * E5)

CONSTS = [("ident", 128), ("count_ge", 128), ("ones", 128), ("headmask4", 4), ("headmask2", 2), ("pairmask", 2),
          ("cosq", 256), ("sinq", 256), ("rot", 128), ("expdesc", 32), ("token_at", 8), ("tile_end", 7),
          ("expert_at", 32), ("step_at", 40), ("neghalf", 8),
          ("ident64", 64), ("neghead16", 16), ("neghead4", 4), ("neghead8", 8)]
L0A = [("a0wk", 128), ("a0wv", 128), ("a0wq", 128), ("a0wo", 128), ("a0bv", 128), ("a0bo", 128),
       ("a0bk", 1), ("a0bq", 1)]
L0F = [("f0wr", 2048), ("f0ws", 256), ("f0cent", 16), ("f0eb", 16), ("f0br", 128)]
L1A = [("a1wk", 1024), ("a1wv", 1024), ("a1wq", 1024), ("a1wo", 1024), ("a1bo", 128), ("a1g", 1),
       ("a1b", 1), ("a1gate", 1)]
L1S = [("f1gw", 32), ("f1sgu", 512), ("f1sd", 256)]
L2A = [("a2wk", 128), ("a2wv", 128), ("a2wq", 128), ("a2wo", 128), ("a2bv", 128), ("a2bo", 128),
       ("a2bk", 1), ("a2bq", 1)]
L2F = [("f2g1", 1), ("f2g2", 1), ("f2wq", 128), ("f2wkc", 128), ("f2wvc", 32), ("f2wo", 128), ("f2wr", 8),
       ("f2eb", 8), ("f2w1", 1152), ("f2w3", 1152), ("f2w2", 1152)]
L3A = [("a3wk", 128), ("a3wv", 128), ("a3wq", 128), ("a3wo", 128), ("f3cent", 8), ("f3g", 8), ("f3b", 8),
       ("f3b1", 32), ("f3b2", 1024)]
L1M = 32 * 768
L3M = 8 * 1024
EARLY = 28 * 768
WORK = 11264
TURN = 6
GROUPS = [("consts", CONSTS), ("l0a", L0A), ("l0f", L0F), ("l1a", L1A), ("l1s", L1S),
          ("l2a", L2A), ("l2f", L2F), ("l3a", L3A)]


def words(group):
    return sum(n for _, n in group)


class Signal:

    def __init__(self, handle):
        self.handle, self.done = handle, 0


class Program:
    def __init__(self, nc, ctx, dram):
        self.nc, self.ctx, self.dram, self.signals = nc, ctx, dram, {}

        def sb(name, n, dt=F32):
            return ctx.enter_context(nc.sbuf_tensor(name, [P, n], dt))

        self.sb = sb
        self.c = {}
        self.loads = []
        self.work = sb("work", WORK)
        self.wmoe = sb("wmoe", L1M)
        late = L3M
        for name, group in GROUPS:
            if name == "l0f":
                t = self.wmoe[:, EARLY:EARLY + words(group)]
            elif name in ("l2a", "l2f", "l3a"):
                t = self.wmoe[:, late:late + words(group)]
                late += words(group)
            else:
                t = sb(name, words(group))[:, :]
            at = 0
            for part, n in group:
                self.c[part] = t[:, at:at + n]
                at += n
            self.loads.append((name, t))
        self.xl = self.wmoe[:, late:late + 1024]
        self.x = sb("x", 1024)
        self.xn = sb("xn", 1024)
        self.xnT = sb("xnT", 1024)
        self.ctxn = sb("ctxn", 256)
        self.ctxT = sb("ctxT", 512)
        self.small = sb("small", 2048)
        self.maskT0 = self.work[:, 4096:5120].bitcast(I32)
        self.maskT3 = self.work[:, 5120:5376]
        self.mb = sb("mb", 1024, BF16)
        self.mb3 = sb("mb3", 768, BF16)
        self.i64 = sb("i64", 512, BF16)
        self.i64big = sb("i64big", 512, BF16)
        self.nh = {16: sb("nh16", 1024, BF16), 4: sb("nh4", 1024, BF16), 8: sb("nh8", 512, BF16)}
        self.identb = sb("identb", 128, BF16)
        self.ps = ctx.enter_context(nc.psum_tensor("ps", [P, 8, BANK], F32))
        self.load_sem = {}
        for name in ["x", "ctx", "mask"] + [n for n, _ in self.loads] + ["moe1", "moe1b", "moe3"]:
            self.load_sem[name] = ctx.enter_context(nc.semaphore(f"loaded_{name}"))

    def sig(self, name):
        if name not in self.signals:
            self.signals[name] = Signal(self.ctx.enter_context(self.nc.semaphore(name)))
        return self.signals[name]

    def tiles(self, t):
        return t[:, 0:1024].rearrange("p (t d) -> p t d", d=P)


def keep_busy(k, pe, times, bank=7):
    for _ in range(times):
        pe.matmul(k.ps[:, bank, 0:256], k.identb[:, :], k.i64[:, 0:256], start=True, stop=True)


def start_loads(k):
    with k.nc.Block() as block:
        @block.sync
        def _(sp):
            order = dict(k.loads)
            sp.dma_start(order["consts"], k.dram["consts"]).then_inc(k.load_sem["consts"], 16)
            sp.dma_start(k.x[:, :], k.dram["x"]).then_inc(k.load_sem["x"], 16)
            sp.dma_start(k.ctxn[:, :], k.dram["ctx"]).then_inc(k.load_sem["ctx"], 16)
            sp.dma_start(order["l0a"], k.dram["l0a"]).then_inc(k.load_sem["l0a"], 16)
            sp.dma_start(k.maskT0[0:SC, :], k.dram["mask0"]).then_inc(k.load_sem["mask"], 16)
            for half in range(2):
                sp.dma_start(k.maskT3[half * SC:(half + 1) * SC, :], k.dram["mask3"]).then_inc(k.load_sem["mask"], 16)


def constants(k):
    c = k.c
    split, turned = k.sig("split"), k.sig("turned")
    with k.nc.Block() as block:
        @block.vector
        def _(dve):
            dve.wait_ge(k.load_sem["consts"], 16)
            def repeated(t):
                return t.rearrange("p (m n) -> p m n", n=SC), c["ident64"][:, None, :].to_broadcast([P, BANK // SC, SC])

            dst, src = repeated(k.i64[:, :])
            dve.tensor_copy(dst, src)
            dst, src = repeated(k.i64big[:, :])
            dve.tensor_scalar(dst, src, BIG, None, ALU.mult)
            for heads, keys in ((16, SC), (4, S), (8, SC)):
                dve.tensor_copy(k.nh[heads][:, :].rearrange("p (h s) -> p h s", s=keys),
                                c[f"neghead{heads}"][:, :, None].to_broadcast([P, heads, keys]))
            dve.tensor_copy(k.identb[:, :], c["ident"])
            dve.wait_ge(k.load_sem["mask"], 48)
            dve.tensor_scalar(k.mb[0:SC, :], k.maskT0[0:SC, :], 0.0, None, ALU.is_equal)
            rest = k.small[:, 0:256]
            low, high = slice(0, SC), slice(SC, P)
            dve.tensor_copy(k.mb3[:, 256:512], k.maskT3).then_inc(split.handle, 1)
            dve.tensor_copy(k.mb3[low, 0:256], k.maskT3[low, :])
            dve.wait_ge(split.handle, split.done + 1)
            dve.tensor_tensor(rest, k.maskT3, k.mb3[:, 256:512], ALU.subtract).then_inc(split.handle, 1)
            dve.wait_ge(split.handle, split.done + 2)
            dve.tensor_copy(k.mb3[high, 0:256], rest[high, :])
            dve.tensor_copy(k.mb3[:, 512:768], rest).then_inc(split.handle, 1)
            dve.wait_ge(split.handle, split.done + 3)
            dve.tensor_tensor(k.mb3[low, 256:512], rest[low, :], k.mb3[low, 512:768], ALU.subtract)

        @block.tensor
        def _(pe):
            pe.wait_ge(k.load_sem["consts"], 16)
            pe.wait_ge(k.load_sem["ctx"], 16)
            for i in range(2):
                pe.transpose(k.ps[:, 0, i * P:(i + 1) * P], k.ctxn[:, i * P:(i + 1) * P],
                             c["ident"]).then_inc(turned.handle, 1)

        @block.scalar
        def _(act):
            act.wait_ge(turned.handle, turned.done + 2)
            v = k.ctxT[:, :].rearrange("p (b two s) -> p b two s", b=B, two=2)
            for i in range(2):
                act.activation(v[:, :, i, :], k.ps[:, 0, 0:256].rearrange("p (b s) -> p b s", b=B), ACT.Copy)
    split.done += 3
    turned.done += 2


def norm_turn(k, outs, turned_src=0, scale=None, bias=None, beside=None):
    stats, aggr, var, rstd, normed, turned, centred = (k.sig(n) for n in (
        "ln_stats", "ln_aggr", "ln_var", "ln_rstd", "normed", "turned", "centred"))
    st = k.small[:, 0:48].rearrange("p (t s) -> p t s", s=6)
    mv = k.small[:, 48:64].rearrange("p (t s) -> p t s", s=2)
    n = len(outs)
    ve = k.small[:, 64:64 + 8 * n].rearrange("p (o t) -> p o t", o=n)
    rs = k.small[:, 96:96 + 8 * n].rearrange("p (o t) -> p o t", o=n)
    x3 = k.tiles(k.x)
    assert n <= 2
    other = 1 - turned_src if n == 2 else None
    nm = k.small[:, 112:120]
    src = k.tiles(outs[turned_src][0])
    with k.nc.Block() as block:
        @block.vector
        def _(dve):
            for g in range(2):
                four = range(4 * g, 4 * g + 4)
                for t in four:
                    dve.bn_stats(st[:, t, :], x3[:, t, :]).then_inc(stats.handle, 1)
                for t in four:
                    dve.wait_ge(stats.handle, stats.done + t + 1)
                    dve.bn_aggr(mv[:, t, :], st[:, t, :]).then_inc(aggr.handle, 1)
                dve.wait_ge(aggr.handle, aggr.done + 4 * g + 4)
                for o in range(n):
                    dve.tensor_scalar(ve[:, o, 4 * g:4 * g + 4], mv[:, 4 * g:4 * g + 4, 1], outs[o][1][0],
                                      outs[o][1][1], ALU.mult, ALU.add).then_inc(var.handle, 1)
            if other is not None:
                dve.tensor_scalar(nm, mv[:, :, 0], -1.0, None, ALU.mult).then_inc(var.handle, 1)
            for t in range(TILES):
                if t % 4 == 0:
                    dve.wait_ge(rstd.handle, rstd.done + t // 4 + 1)
                dve.tensor_scalar(src[:, t, :], x3[:, t, :], mv[:, t, 0:1], rs[:, turned_src, t:t + 1],
                                  ALU.subtract, ALU.mult).then_inc(normed.handle, 1)
            dve.wait_ge(turned.handle, turned.done + 8)
            if bias is not None:
                dve.tensor_scalar(k.xnT[:, 512:1024], k.ps[:, 1, :], scale, bias, ALU.mult, ALU.add)
            elif scale is not None:
                dve.tensor_scalar(k.xnT[:, 512:1024], k.ps[:, 1, :], scale, None, ALU.mult)
            else:
                dve.tensor_copy(k.xnT[:, 512:1024], k.ps[:, 1, :])

        @block.gpsimd
        def _(pool):
            for g in range(2):
                pool.wait_ge(var.handle, var.done + n * (g + 1))
                half = k.c["neghalf"][:, None, 0:4].to_broadcast([P, n, 4])
                pool.tensor_tensor(rs[:, :, 4 * g:4 * g + 4], ve[:, :, 4 * g:4 * g + 4], half,
                                   ALU.pow).then_inc(rstd.handle, 1)

        if beside:
            block.sync(beside)

        @block.tensor
        def _(pe):
            for t in range(TILES):
                pe.wait_ge(normed.handle, normed.done + t + 1)
                pe.transpose(k.ps[:, t // 4, (t % 4) * P:(t % 4 + 1) * P], src[:, t, :],
                             k.c["ident"]).then_inc(turned.handle, 1)

        @block.scalar
        def _(act):
            if other is not None:
                dst = k.tiles(outs[other][0])
                act.wait_ge(var.handle, var.done + 2 * n + 1)
                for t in range(TILES):
                    act.activation(dst[:, t, :], x3[:, t, :], ACT.Identity, bias=nm[:, t:t + 1]).then_inc(centred.handle, 1)
                act.wait_ge(rstd.handle, rstd.done + 2)
                for t in range(TILES):
                    act.wait_ge(centred.handle, centred.done + t + 1)
                    act.activation(dst[:, t, :], dst[:, t, :], ACT.Copy, scale=rs[:, other, t:t + 1])
            act.wait_ge(turned.handle, turned.done + 4)
            if scale is None:
                act.activation(k.xnT[:, 0:512], k.ps[:, 0, :], ACT.Copy)
            else:
                act.activation(k.xnT[:, 0:512], k.ps[:, 0, :], ACT.Identity, scale=scale,
                               bias=bias if bias is not None else 0.0)
    stats.done += TILES
    aggr.done += TILES
    var.done += 2 * n
    if other is not None:
        var.done += 1
        centred.done += TILES
    rstd.done += 2
    normed.done += TILES
    turned.done += TILES


def rms_turn(k, src, gain, eps):
    step, rstd, normed, turned = k.sig("rms_step"), k.sig("ln_rstd"), k.sig("normed"), k.sig("turned")
    ms, ve, rs = k.small[:, 48:56], k.small[:, 64:72], k.small[:, 72:80]
    sq, dst = k.tiles(k.work), k.tiles(k.xn)
    s3 = k.tiles(src)
    with k.nc.Block() as block:
        @block.vector
        def _(dve):
            dve.tensor_tensor(sq, s3, s3, ALU.mult).then_inc(step.handle, 1)
            dve.wait_ge(step.handle, step.done + 1)
            dve.tensor_reduce(ms, sq, X, ALU.add).then_inc(step.handle, 1)
            dve.wait_ge(step.handle, step.done + 2)
            dve.tensor_scalar(ve, ms, 1.0 / D, eps, ALU.mult, ALU.add).then_inc(step.handle, 1)
            dve.wait_ge(rstd.handle, rstd.done + 1)
            for t in range(TILES):
                dve.tensor_scalar(dst[:, t, :], s3[:, t, :], rs[:, t:t + 1], None, ALU.mult).then_inc(normed.handle, 1)
            dve.wait_ge(turned.handle, turned.done + 8)
            dve.tensor_scalar(k.xnT[:, 512:1024], k.ps[:, 1, :], gain, None, ALU.mult)

        @block.gpsimd
        def _(pool):
            pool.wait_ge(step.handle, step.done + 3)
            pool.tensor_tensor(rs, ve, k.c["neghalf"], ALU.pow).then_inc(rstd.handle, 1)

        @block.tensor
        def _(pe):
            for t in range(TILES):
                pe.wait_ge(normed.handle, normed.done + t + 1)
                pe.transpose(k.ps[:, t // 4, (t % 4) * P:(t % 4 + 1) * P], dst[:, t, :],
                             k.c["ident"]).then_inc(turned.handle, 1)

        @block.scalar
        def _(act):
            act.wait_ge(turned.handle, turned.done + 4)
            act.activation(k.xnT[:, 0:512], k.ps[:, 0, :], ACT.Identity, scale=gain)
    step.done += 3
    rstd.done += 1
    normed.done += TILES
    turned.done += TILES


def turn(k, src, dst, beside):
    turned = k.sig("turned")
    s3 = k.tiles(src)
    with k.nc.Block() as block:
        @block.tensor
        def _(pe):
            for t in range(TILES):
                pe.transpose(k.ps[:, t // 4, (t % 4) * P:(t % 4 + 1) * P], s3[:, t, :],
                             k.c["ident"]).then_inc(turned.handle, 1)

        block.sync(beside)

        @block.scalar
        def _(act):
            act.wait_ge(turned.handle, turned.done + 4)
            act.activation(dst[:, 0:512], k.ps[:, 0, :], ACT.Copy)

        @block.vector
        def _(dve):
            dve.wait_ge(turned.handle, turned.done + 8)
            dve.tensor_copy(dst[:, 512:1024], k.ps[:, 1, :])
    turned.done += TILES


def add_row(k, pool, dst, row):
    d3 = k.tiles(dst)
    pool.tensor_tensor(d3, d3, row[:, None, :].to_broadcast([P, TILES, D]), ALU.add)


class Core:

    def __init__(self, k, heads, hd, keys):
        self.heads, self.hd, self.keys = heads, hd, keys
        self.ct = heads * keys // P
        self.groups = heads * hd // P
        self.cols = self.ct * P
        w, at = k.work, 0

        def take(n):
            nonlocal at
            at += n
            assert at <= WORK
            return w[:, at - n:at]

        self.stacked = hd == 8
        if self.stacked:
            q = take(B * self.ct * S // 2)
            self.qst = q.bitcast(BF16).rearrange("p (b j n) -> p b j n", b=B, j=self.ct)
            self.kst = take(B * self.cols // 2).bitcast(BF16).rearrange("p (b n) -> p b n", b=B)
        else:
            self.qT = take(self.groups * 1024).rearrange("p (b g n) -> p b g n", b=B, g=self.groups)
            o = self.qT.rearrange("p b g n -> p (b g n)").rearrange("p (t n) -> p t n", t=TILES)
            self.o = [o[:, t, :] for t in range(TILES)]
            self.kblk = take(B * self.cols).rearrange("p (b n) -> p b n", b=B)
        self.probs = take(2 * self.ct * 256).rearrange("p (r j n) -> p r j n", r=2, j=self.ct)
        if self.stacked:
            self.v = take(B * self.ct * 32).rearrange("p (b j c) -> p b j c", b=B, j=self.ct)
            self.o = [q[:, b * self.ct * P:][:, 0:256] for b in range(B)]
            self.oT = [q[:, b * self.ct * P + 256:][:, 0:256] for b in range(B)]
        elif keys == SC:
            self.v = take(B * self.ct * 2 * (hd + 1)).rearrange("p (b j c) -> p b j c", b=B, j=self.ct)
        else:
            self.v = take(TILES * hd).rearrange("p (t c) -> p t c", t=TILES)
            self.oT = [self.qT[:, b, 0, :] for b in range(B)]
        self.ot = k.small[:, 1024:1024 + 2 * self.groups * P if self.groups == 1 else 2048]
        self.otw = self.groups * P
        free = self.probs.rearrange("p r j n -> p (r j n)")
        self.kT = free[:, 0:self.groups * 256]
        self.raw = free[:, 0:1024]
        if self.stacked:
            self.krest = free[:, 256:512]
            self.parts = free[:, 1024:2560].bitcast(BF16).rearrange("p (q n) -> p q n", q=3)
            self.kgot = free[:, 2560:3584].bitcast(BF16).rearrange("p (b j s) -> p b j s", j=self.ct, b=B)
            self.kparts = free[:, 3584:3968].bitcast(BF16).rearrange("p (q n) -> p q n", q=3)

    def group(self, j):
        return j if self.groups > 1 else 0

    def kview(self):
        return self.kblk.rearrange("p b (g h s) -> p b g h s", g=self.groups, s=self.keys)


def cut_in_parts(dve, src, parts, rest, cut):
    dve.tensor_copy(parts[:, 0], src).then_inc(cut.handle, 1)
    dve.wait_ge(cut.handle, cut.done + 1)
    dve.tensor_tensor(rest, src, parts[:, 0], ALU.subtract).then_inc(cut.handle, 1)
    dve.wait_ge(cut.handle, cut.done + 2)
    dve.tensor_copy(parts[:, 1], rest).then_inc(cut.handle, 1)
    dve.wait_ge(cut.handle, cut.done + 3)
    dve.tensor_tensor(parts[:, 2], rest, parts[:, 1], ALU.subtract).then_inc(cut.handle, 1)


def send_part(eng, parts, q, scratch, sent):
    eng.dma_start(scratch[q], parts[:, q]).then_inc(sent[q].handle, 16)


def fetch_part(eng, dst, order, q, scratch, sent, fetched):
    eng.wait_ge(sent[q].handle, sent[q].done + 16)
    for s in range(len(order)):
        if order[s] == q:
            eng.dma_start(dst[PAIR * s:PAIR * (s + 1)],
                          scratch[q].rearrange("(p r) (b n) -> r b p n", r=PAIR, b=B)).then_inc(fetched.handle, 16)


def project_v(k, a, pe, wv, vproj):
    ctx4 = k.ctxT[:, :].rearrange("p (b two s) -> p b two s", b=B, two=2)
    for b in range(B):
        pe.matmul(k.ps[:, 4 + b, 0:a.heads * a.hd], ctx4[:, b].rearrange("p two s -> p (two s)"), wv, start=True,
                  stop=True).then_inc(vproj.handle, 1)


def place_values(k, a, dve, cleared, vproj):
    hd = a.hd
    dve.wait_ge(cleared.handle, cleared.done + 1)
    for par in range(2):
        rows = slice(64 * par, 64 * par + 64)
        at = par * (hd + 1)
        dve.memset(a.v[rows, :, :, at + hd:at + hd + 1], 1.0)
        for b in range(B):
            dve.wait_ge(vproj.handle, vproj.done + b + 1)
            src = k.ps[rows, 4 + b, 0:a.heads * hd].rearrange("p (j two d) -> p j two d", two=2, d=hd)[:, :, par, :]
            dst = a.v[rows, b, :, at:at + hd]
            dve.tensor_copy(dst, src)


def fetch_keys(k, a):
    def sync_part(sp):
        for q in range(3):
            fetch_part(sp, a.kgot, K_PARTS, q, k.dram["kparts"], [k.sig(f"k_sent{i}") for i in range(3)],
                       k.sig("k_fetched"))
    return sync_part


def place_values_stacked(k, a, dve, bv, cleared, vproj):
    hd = a.hd
    dve.wait_ge(cleared.handle, cleared.done + 1)
    dve.wait_ge(vproj.handle, vproj.done + B)
    for par in range(2):
        rows = slice(64 * par, 64 * par + 64)
        at = par * hd
        dve.memset(a.v[rows, :, :, 2 * hd + at:3 * hd + at], 1.0)
        for b in range(B):
            src = k.ps[rows, 4, b * P:(b + 1) * P].rearrange("p (j two d) -> p j two d", two=2, d=hd)[:, :, par, :]
            dst = a.v[rows, b, :, at:at + hd]
            if bv is None:
                dve.tensor_copy(dst, src)
            else:
                row = bv[rows, :].rearrange("p (j two d) -> p j two d", two=2, d=hd)[:, :, par, :]
                dve.tensor_tensor(dst, src, row, ALU.add)


def project_all(k, a, wk, wv, wq, row=None):
    c = k.c
    kproj, kept, vproj, cleared = (k.sig(n) for n in ("k_proj", "k_kept", "v_proj", "v_cleared"))
    qproj, qkept = k.sig("q_proj"), k.sig("q_kept")
    ctx4 = k.ctxT[:, :].rearrange("p (b two s) -> p b two s", b=B, two=2)
    g = a.groups
    kv = a.kview()
    kt = a.kT.rearrange("p (g b s) -> p g b s", g=g, b=B)

    def spread(eng, b):
        eng.wait_ge(kept.handle, kept.done + g)
        for i in range(g):
            eng.tensor_tensor(kv[:, b, i], kt[:, i, b, None, :].to_broadcast([P, 2, SC]),
                              c["headmask2"][:, :, None].to_broadcast([P, 2, SC]), ALU.mult)

    with k.nc.Block() as block:
        @block.tensor
        def _(pe):
            for i in range(g):
                pe.matmul(k.ps[:, i, 0:256], wk[:, i * P:(i + 1) * P], ctx4[:, :, 0, :], start=True,
                          stop=True).then_inc(kproj.handle, 1)
            project_v(k, a, pe, wv, vproj)
            for n in range(2 * g):
                if n < 4:
                    pe.wait_ge(kept.handle, kept.done + n + 1)
                else:
                    pe.wait_ge(qkept.handle, qkept.done + n - 3)
                pe.matmul(k.ps[:, n % 4, :], wq[:, n // 2 * P:(n // 2 + 1) * P],
                          k.xnT[:, n % 2 * 512:(n % 2 + 1) * 512], start=True, stop=True).then_inc(qproj.handle, 1)

        @block.scalar
        def _(act):
            for i in range(g):
                act.wait_ge(kproj.handle, kproj.done + i + 1)
                act.activation(a.kT[:, i * 256:(i + 1) * 256], k.ps[:, i, 0:256], ACT.Copy).then_inc(kept.handle, 1)
            for n in range(2 * g):
                act.wait_ge(qproj.handle, qproj.done + n + 1)
                act.activation(a.qT[:, n % 2 * 2:n % 2 * 2 + 2, n // 2, :],
                               k.ps[:, n % 4, :].rearrange("p (b s) -> p b s", s=S), ACT.Copy).then_inc(qkept.handle, 1)

        @block.gpsimd
        def _(pool):
            pool.memset(a.v, 0.0).then_inc(cleared.handle, 1)
            spread(pool, 3)
            if row is not None:
                add_row(k, pool, k.x, row)

        @block.vector
        def _(dve):
            for b in range(B - 1):
                spread(dve, b)
            place_values(k, a, dve, cleared, vproj)
    qproj.done += 2 * g
    qkept.done += 2 * g
    kproj.done += g
    kept.done += g
    vproj.done += B
    cleared.done += 1


def project_k_stacked(k, a, wk, bk, rope, gather=None, rows=None):
    c = k.c
    kproj, kept, rot, step, ready, cut = (k.sig(n) for n in (
        "k_proj", "k_kept", "k_rot", "k_step", "k_ready", "k_cut"))
    sent = [k.sig(f"k_sent{q}") for q in range(3)]
    ctx4 = k.ctxT[:, :].rearrange("p (b two s) -> p b two s", b=B, two=2)
    with k.nc.Block() as block:
        @block.tensor
        def _(pe):
            pe.matmul(k.ps[:, 0, 0:256], wk, ctx4[:, :, 0, :], start=True, stop=True).then_inc(kproj.handle, 1)
            if rope:
                pe.wait_ge(kept.handle, kept.done + 1)
                pe.matmul(k.ps[:, 1, 0:256], c["rot"], a.kT, start=True, stop=True).then_inc(rot.handle, 1)

        @block.scalar
        def _(act):
            act.wait_ge(kproj.handle, kproj.done + 1)
            act.activation(a.kT, k.ps[:, 0, 0:256], ACT.Identity,
                           bias=bk if bk is not None else 0.0).then_inc(kept.handle, 1)
            for q in range(3):
                act.wait_ge(cut.handle, cut.done + PART_AT[q])
                send_part(act, a.kparts, q, k.dram["kparts"], sent)

        if gather:
            block.gpsimd(gather[0])
            block.sync(gather[1])
        elif rows is not None:
            @block.gpsimd
            def _(pool):
                pool.tensor_tensor(k.x[:, :], k.x[:, :], rows[:, :], ALU.add)

        @block.vector
        def _(dve):
            dve.wait_ge(kept.handle, kept.done + 1)
            if rope:
                tmp = k.small[:, 128:384].rearrange("p (b s) -> p b s", b=B)
                kr = a.kT.rearrange("p (b s) -> p b s", b=B)
                sin = c["sinq"][:, None, 0:SC].to_broadcast([P, B, SC])
                cos = c["cosq"][:, None, 0:SC].to_broadcast([P, B, SC])
                dve.wait_ge(rot.handle, rot.done + 1)
                dve.tensor_tensor(tmp, k.ps[:, 1, 0:256].rearrange("p (b s) -> p b s", b=B), sin, ALU.mult)
                dve.tensor_tensor(kr, kr, cos, ALU.mult).then_inc(step.handle, 1)
                dve.wait_ge(step.handle, step.done + 1)
                dve.tensor_tensor(kr, kr, tmp, ALU.add).then_inc(ready.handle, 1)
                dve.wait_ge(ready.handle, ready.done + 1)
            cut_in_parts(dve, a.kT, a.kparts, a.krest, cut)
            if gather:
                for t in range(TILES):
                    gather[2](dve, t)
                    dve.tensor_tensor(k.tiles(k.x)[:, t, :], k.tiles(k.x)[:, t, :], k.tiles(rows)[:, t, :], ALU.add)
    kproj.done += 1
    kept.done += 1
    cut.done += 4
    if rope:
        rot.done += 1
        step.done += 1
        ready.done += 1


def project_q(k, a, wq):
    proj = k.sig("q_proj")
    with k.nc.Block() as block:
        @block.tensor
        def _(pe):
            for h in range(2):
                pe.matmul(k.ps[:, h, :], wq, k.xnT[:, h * 512:(h + 1) * 512], start=True,
                          stop=True).then_inc(proj.handle, 1)

        @block.scalar
        def _(act):
            for h in range(2):
                act.wait_ge(proj.handle, proj.done + h + 1)
                act.activation(a.qT[:, 2 * h:2 * h + 2, 0, :], k.ps[:, h, :].rearrange("p (b s) -> p b s", s=S),
                               ACT.Copy)
    proj.done += 2


def project_q_stacked(k, a, wq, bq, rope, wv, bv, row=None):
    c = k.c
    proj, kept, rot, step = k.sig("q_proj"), k.sig("q_kept"), k.sig("q_rot"), k.sig("q_step")
    first, left, second, third = k.sig("q_part0"), k.sig("q_rest"), k.sig("q_part1"), k.sig("q_part2")
    sent, k_sent = [k.sig(f"q_sent{q}") for q in range(3)], [k.sig(f"k_sent{q}") for q in range(3)]
    fetched, k_fetched = k.sig("q_fetched"), k.sig("k_fetched")
    vproj, cleared = k.sig("v_proj"), k.sig("v_cleared")
    ctx4 = k.ctxT[:, :].rearrange("p (b two s) -> p b two s", b=B, two=2)
    raw = [a.raw[:, h * 512:(h + 1) * 512] for h in range(2)]
    parts = [a.parts[:, :, h * 512:(h + 1) * 512] for h in range(2)]

    def spread(eng, b):
        eng.tensor_tensor(a.kst[0:STACK, b, :].rearrange("p (j two s) -> p j two s", two=2, s=SC),
                          a.kgot[0:STACK, b, :, None, :].to_broadcast([STACK, a.ct, 2, SC]),
                          c["pairmask"][0:STACK, None, :, None].to_broadcast([STACK, a.ct, 2, SC]), ALU.mult)

    with k.nc.Block() as block:
        @block.tensor
        def _(pe):
            for h in range(2):
                pe.matmul(k.ps[:, h, :], wq, k.xnT[:, h * 512:(h + 1) * 512], start=True,
                          stop=True).then_inc(proj.handle, 1)
            if rope:
                for h in range(2):
                    pe.wait_ge(kept.handle, kept.done + h + 1)
                    pe.matmul(k.ps[:, 2 + h, :], c["rot"], raw[h], start=True, stop=True).then_inc(rot.handle, 1)
            for b in range(B):
                pe.matmul(k.ps[:, 4, b * P:(b + 1) * P], ctx4[:, b].rearrange("p two s -> p (two s)"), wv, start=True,
                          stop=True).then_inc(vproj.handle, 1)
            keep_busy(k, pe, 80)

        @block.scalar
        def _(act):
            for h in range(2):
                act.wait_ge(proj.handle, proj.done + h + 1)
                act.activation(raw[h], k.ps[:, h, :], ACT.Identity,
                               bias=bq if bq is not None else 0.0).then_inc(kept.handle, 1)
                if not rope:
                    act.activation(parts[h][:, 0], k.ps[:, h, :], ACT.Identity,
                                   bias=bq if bq is not None else 0.0).then_inc(first.handle, 1)
            for h in range(2):
                if rope:
                    act.wait_ge(step.handle, step.done + 2 * h + 2)
                    act.activation(parts[h][:, 0], raw[h], ACT.Copy).then_inc(first.handle, 1)
                act.wait_ge(left.handle, left.done + h + 1)
                act.activation(parts[h][:, 1], raw[h], ACT.Copy).then_inc(second.handle, 1)

        @block.gpsimd
        def _(pool):
            pool.memset(a.v, 0.0).then_inc(cleared.handle, 1)
            if row is not None:
                add_row(k, pool, k.x, row)
            pool.wait_ge(k_fetched.handle, k_fetched.done + 16 * len(K_PARTS))
            spread(pool, 3)

        @block.vector
        def _(dve):
            sin = c["sinq"][:, None, :].to_broadcast([P, 2, S])
            cos = c["cosq"][:, None, :].to_broadcast([P, 2, S])
            tmp = k.small[:, 0:512].rearrange("p (b s) -> p b s", s=S)
            for h in range(2):
                if rope:
                    q = raw[h].rearrange("p (b s) -> p b s", s=S)
                    dve.wait_ge(rot.handle, rot.done + h + 1)
                    if h:
                        dve.wait_ge(step.handle, step.done + 2 * h)
                    dve.tensor_tensor(q, q, cos, ALU.mult)
                    dve.tensor_tensor(tmp, k.ps[:, 2 + h, :].rearrange("p (b s) -> p b s", s=S), sin,
                                      ALU.mult).then_inc(step.handle, 1)
                    dve.wait_ge(step.handle, step.done + 2 * h + 1)
                    dve.tensor_tensor(q, q, tmp, ALU.add).then_inc(step.handle, 1)
            for h in range(2):
                dve.wait_ge(first.handle, first.done + h + 1)
                dve.tensor_tensor(raw[h], raw[h], parts[h][:, 0], ALU.subtract).then_inc(left.handle, 1)
            for h in range(2):
                dve.wait_ge(second.handle, second.done + h + 1)
                dve.tensor_tensor(parts[h][:, 2], raw[h], parts[h][:, 1], ALU.subtract).then_inc(third.handle, 1)
            place_values_stacked(k, a, dve, bv, cleared, vproj)
            dve.wait_ge(k_fetched.handle, k_fetched.done + 16 * len(K_PARTS))
            for b in range(B - 1):
                spread(dve, b)

        @block.sync
        def _(sp):
            for q, there in enumerate((first, second, third)):
                sp.wait_ge(there.handle, there.done + 2)
                send_part(sp, a.parts, q, k.dram["qparts"], sent)
            for q in range(3):
                fetch_part(sp, a.qst, Q_PARTS, q, k.dram["qparts"], sent, fetched)
    for s in sent + k_sent:
        s.done += 16
    k_fetched.done += 16 * len(K_PARTS)
    vproj.done += B
    cleared.done += 1
    for s in (proj, kept, first, left, second, third):
        s.done += 2
    if rope:
        rot.done += 2
        step.done += 4


def weigh_stacked(k, a, mask, scale, wo, dst, mT):
    made, expd, summed, kept, turned, inverted, normed, back, oT_kept, out_made, added = (k.sig(n) for n in (
        "st_made", "expd", "pv_done", "pv_kept", "o_turned", "recipd", "o_done", "o_back", "ot_kept", "wo_made",
        "wo_added"))
    r = k.small[:, 256:288].rearrange("p (y s) -> p y s", s=2)
    nh = k.nh[a.heads]
    pairs = a.ct // 2
    raw = [k.small[:, 1024 + i * 512:1024 + (i + 1) * 512] for i in range(2)]
    d3 = k.tiles(dst)
    with k.nc.Block() as block:
        @block.tensor
        def _(pe):
            for b in range(B + 3):
                if b < B:
                    for i in range(pairs):
                        n = b * pairs + i
                        if n >= 3:
                            pe.wait_ge(expd.handle, expd.done + n - 2)
                        for jj in range(2):
                            j = 2 * i + jj
                            out = k.ps[:, n % 3, jj * 256:(jj + 1) * 256]
                            for m, (by_key, ident) in enumerate(mask):
                                pe.matmul(out, ident[:, 0:P], by_key(b, 0, S), start=m == 0, stop=False)
                            pe.matmul(out, a.kst[0:STACK, b, j * P:(j + 1) * P], a.qst[0:STACK, b, j, :],
                                      start=not mask, stop=False)
                            ins = pe.matmul(out, nh[0:3 * a.heads, j * P:(j + 1) * P], mT[:, b * S:(b + 1) * S],
                                            start=False, stop=True)
                        ins.then_inc(made.handle, 1)
                if 2 <= b < B + 2:
                    c0 = b - 2
                    pe.wait_ge(kept.handle, kept.done + c0 + 1)
                    if c0:
                        pe.wait_ge(normed.handle, normed.done + c0)
                    for tl in range(2):
                        for ch in range(2):
                            ins = pe.transpose(k.ps[:, 6, (2 * tl + ch) * P:(2 * tl + ch + 1) * P],
                                               raw[c0 % 2][:, ch * 256 + tl * P:ch * 256 + (tl + 1) * P], k.c["ident"])
                    ins.then_inc(turned.handle, 1)
                if b >= 3:
                    c0 = b - 3
                    pe.wait_ge(normed.handle, normed.done + c0 + 1)
                    if c0:
                        pe.wait_ge(oT_kept.handle, oT_kept.done + c0)
                    for tl in range(2):
                        ins = pe.transpose(k.ps[:, 3, tl * P:(tl + 1) * P], a.o[c0][:, tl * P:(tl + 1) * P],
                                           k.c["ident"])
                    ins.then_inc(back.handle, 1)
                if 1 <= b < B + 1:
                    c0 = b - 1
                    pe.wait_ge(expd.handle, expd.done + pairs * b)
                    if c0 >= 2:
                        pe.wait_ge(kept.handle, kept.done + c0 - 1)
                    for j in range(a.ct):
                        row = j % 4 * 32
                        ins = pe.matmul(k.ps[row:row + 32, 4 + c0 % 2, j // 4 * 256:(j // 4 + 1) * 256],
                                        a.v[:, c0, j, :], a.probs[:, c0 % 2, j, :], start=True, stop=True)
                    ins.then_inc(summed.handle, 1)
                if b >= 3:
                    c0 = b - 3
                    pe.wait_ge(oT_kept.handle, oT_kept.done + c0 + 1)
                    if c0:
                        pe.wait_ge(added.handle, added.done + c0)
                    for tl in range(2):
                        ins = pe.matmul(k.ps[:, 7, tl * P:(tl + 1) * P], a.oT[c0][:, tl * P:(tl + 1) * P], wo,
                                        start=True, stop=True)
                    ins.then_inc(out_made.handle, 1)

        @block.scalar
        def _(act):
            for b in range(B + 1):
                for i in range(pairs if b < B else 0):
                    n = b * pairs + i
                    act.wait_ge(made.handle, made.done + n + 1)
                    act.activation(a.probs[:, b % 2, 2 * i:2 * i + 2, :],
                                   k.ps[:, n % 3, :].rearrange("p (j n) -> p j n", j=2), ACT.Exp,
                                   scale=scale).then_inc(expd.handle, 1)
                if b:
                    c0 = b - 1
                    act.wait_ge(summed.handle, summed.done + c0 + 1)
                    if c0 >= 2:
                        act.wait_ge(turned.handle, turned.done + c0 - 1)
                    act.activation(raw[c0 % 2], k.ps[:, 4 + c0 % 2, :], ACT.Copy).then_inc(kept.handle, 1)

        @block.vector
        def _(dve):
            for b in range(2, B + 3):
                if b < B + 2:
                    c0 = b - 2
                    dve.wait_ge(turned.handle, turned.done + c0 + 1)
                    v = k.ps[:, 6, :].rearrange("p (y c) -> p y c", c=32)
                    dve.reciprocal(r, v[:, :, 16:32:8]).then_inc(inverted.handle, 1)
                    dve.wait_ge(inverted.handle, inverted.done + c0 + 1)
                    dve.tensor_tensor(a.o[c0].rearrange("p (y s d) -> p y s d", s=2, d=8),
                                      v[:, :, 0:16].rearrange("p y (s d) -> p y s d", d=8),
                                      r[:, :, :, None].to_broadcast([P, 16, 2, 8]), ALU.mult).then_inc(normed.handle, 1)
                if b >= 3:
                    c0 = b - 3
                    dve.wait_ge(back.handle, back.done + c0 + 1)
                    dve.tensor_copy(a.oT[c0], k.ps[:, 3, 0:256]).then_inc(oT_kept.handle, 1)
                    dve.wait_ge(out_made.handle, out_made.done + c0 + 1)
                    x = d3[:, 2 * c0:2 * c0 + 2, :]
                    dve.tensor_tensor(x, k.ps[:, 7, 0:256].rearrange("p (t d) -> p t d", d=D), x,
                                      ALU.add).then_inc(added.handle, 1)
    made.done += B * pairs
    expd.done += B * pairs
    for s in (summed, kept, turned, inverted, normed, back, oT_kept, out_made, added):
        s.done += B


def weigh_shared(k, a, scale, wo, dst, mT):
    made, expd, summed, inverted, normed, out_made, added = (k.sig(n) for n in (
        "st_made", "expd", "pv_done", "recipd", "o_done", "wo_made", "wo_added"))
    nh = k.nh[a.heads]
    pairs = a.ct // 2
    d3 = k.tiles(dst)
    with k.nc.Block() as block:
        @block.tensor
        def _(pe):
            for b in range(B + 2):
                if b < B:
                    for i in range(pairs):
                        n = b * pairs + i
                        if n >= 4:
                            pe.wait_ge(expd.handle, expd.done + n - 3)
                        for jj in range(2):
                            j = 2 * i + jj
                            out = k.ps[:, n % 4, jj * 256:(jj + 1) * 256]
                            pe.matmul(out, a.kblk[:, b, j * P:(j + 1) * P], a.qT[:, b, 0, :], start=True, stop=False)
                            ins = pe.matmul(out, nh[0:3 * a.heads, j * P:(j + 1) * P], mT[:, b * S:(b + 1) * S],
                                            start=False, stop=True)
                        ins.then_inc(made.handle, 1)
                if b >= 2:
                    c0 = b - 2
                    pe.wait_ge(normed.handle, normed.done + c0 + 1)
                    if c0:
                        pe.wait_ge(added.handle, added.done + c0)
                    for tl in range(2):
                        ins = pe.matmul(k.ps[:, 7, tl * P:(tl + 1) * P], a.oT[c0][:, tl * P:(tl + 1) * P], wo,
                                        start=True, stop=True)
                    ins.then_inc(out_made.handle, 1)
                if 1 <= b < B + 1:
                    c0 = b - 1
                    pe.wait_ge(expd.handle, expd.done + pairs * b)
                    if c0 >= 2:
                        pe.wait_ge(normed.handle, normed.done + c0 - 1)
                    for col, by_half in ((0, lambda u: a.v[:, 2 * c0 + u, :]), (256, lambda u: k.c["ones"][:, 0:32])):
                        for u in range(2):
                            for h in range(a.heads):
                                ins = pe.matmul(k.ps[32 * h:32 * h + 32, 4 + c0 % 2, col:col + 256], by_half(u),
                                                a.probs[:, c0 % 2, 2 * h + u, :], start=u == 0, stop=u == 1)
                    ins.then_inc(summed.handle, 1)

        @block.scalar
        def _(act):
            for b in range(B):
                if b >= 2:
                    act.wait_ge(summed.handle, summed.done + b - 1)
                for i in range(pairs):
                    n = b * pairs + i
                    act.wait_ge(made.handle, made.done + n + 1)
                    act.activation(a.probs[:, b % 2, 2 * i:2 * i + 2, :],
                                   k.ps[:, n % 4, :].rearrange("p (j n) -> p j n", j=2), ACT.Exp,
                                   scale=scale).then_inc(expd.handle, 1)

        @block.vector
        def _(dve):
            for b in range(1, B + 2):
                if b < B + 1:
                    c0 = b - 1
                    dve.wait_ge(summed.handle, summed.done + c0 + 1)
                    dve.reciprocal(a.oT[c0], k.ps[:, 4 + c0 % 2, 256:512]).then_inc(inverted.handle, 1)
                    dve.wait_ge(inverted.handle, inverted.done + c0 + 1)
                    dve.tensor_tensor(a.oT[c0], a.oT[c0], k.ps[:, 4 + c0 % 2, 0:256], ALU.mult).then_inc(normed.handle, 1)
                if b >= 2:
                    c0 = b - 2
                    dve.wait_ge(out_made.handle, out_made.done + c0 + 1)
                    x = d3[:, 2 * c0:2 * c0 + 2, :]
                    dve.tensor_tensor(x, k.ps[:, 7, 0:256].rearrange("p (t d) -> p t d", d=D), x,
                                      ALU.add).then_inc(added.handle, 1)
    made.done += B * pairs
    expd.done += B * pairs
    for s in (summed, inverted, normed, out_made, added):
        s.done += B


def attend(k, a, mask, scale, wo, dst, load=None):
    nc, c = k.nc, k.c
    ct, cols, heads, hd = a.ct, a.cols, a.heads, a.hd
    banks = cols // BANK
    scored, topped, fetched = k.sig("scored"), k.sig("topped"), k.sig("q_fetched")
    mx = k.small[:, 0:TILES * heads]
    mx3 = mx.rearrange("p (t h) -> p t h", h=heads)
    step, turned = k.sig("max_step"), k.sig("turned")
    rest = k.small[:, 128:128 + TILES * heads].rearrange("p (t h) -> p t h", h=heads)
    parts = k.mparts[:, 0:TILES * 3 * heads].rearrange("p (t q h) -> p t q h", q=3, h=heads)
    mT = k.mT[0:3 * heads, :]
    psb = k.ps[:, 0:2, :].rearrange("p b n -> p (b n)").bitcast(BF16)
    slots = 3 if banks == 2 else 4
    with nc.Block() as block:
        @block.tensor
        def _(pe):
            if a.stacked:
                keep_busy(k, pe, 10)
            for t in range(TILES):
                if a.stacked and t == 0:
                    pe.wait_ge(fetched.handle, fetched.done + 16 * len(Q_PARTS))
                if t >= slots:
                    pe.wait_ge(topped.handle, topped.done + t - slots + 1)
                tok = slice(t % 2 * P, (t % 2 + 1) * P)
                for n in range(banks):
                    out = k.ps[:, banks * (t % slots) + n, :]
                    if a.stacked:
                        for m, (by_key, ident) in enumerate(mask):
                            pe.matmul(out, by_key(t // 2, t % 2 * P, P), ident, start=m == 0, stop=False)
                        for j in range(4 * n, 4 * n + 4):
                            ins = pe.matmul(out[:, j % 4 * P:(j % 4 + 1) * P], a.qst[0:STACK, t // 2, j, tok],
                                            a.kst[0:STACK, t // 2, j * P:(j + 1) * P], start=not mask, stop=not mask or j % 4 == 3)
                    elif a.groups == 1:
                        ins = pe.matmul(out, a.qT[:, t // 2, 0, tok], a.kblk[:, t // 2, n * BANK:(n + 1) * BANK],
                                        start=True, stop=True)
                    else:
                        for j in range(4):
                            ins = pe.matmul(out[:, j * P:(j + 1) * P], a.qT[:, t // 2, j, tok],
                                            a.kblk[:, t // 2, j * P:(j + 1) * P], start=True, stop=True)
                ins.then_inc(scored.handle, 1)
                if a.stacked:
                    keep_busy(k, pe, (4, 1, 0)[len(mask)])
            keep_busy(k, pe, 20)
            pe.wait_ge(step.handle, step.done + 4)
            for t in range(TILES):
                pe.transpose(psb[0:3 * heads, t * P:(t + 1) * P], parts[:, t].rearrange("p q h -> p (q h)"),
                             k.identb[:, :]).then_inc(turned.handle, 1)

        if load:
            block.sync(load)

        @block.vector
        def _(dve):
            for t in range(TILES):
                dve.wait_ge(scored.handle, scored.done + t + 1)
                b0 = banks * (t % slots)
                dve.tensor_reduce(mx3[:, t, :], k.ps[:, b0:b0 + banks, :].rearrange("p b (h s) -> p (b h) s", s=a.keys),
                                  X, ALU.max).then_inc(topped.handle, 1)
            dve.wait_ge(topped.handle, topped.done + TILES)
            dve.tensor_copy(parts[:, :, 0, :], mx3).then_inc(step.handle, 1)
            dve.wait_ge(step.handle, step.done + 1)
            dve.tensor_tensor(rest, mx3, parts[:, :, 0, :], ALU.subtract).then_inc(step.handle, 1)
            dve.wait_ge(step.handle, step.done + 2)
            dve.tensor_copy(parts[:, :, 1, :], rest).then_inc(step.handle, 1)
            dve.wait_ge(step.handle, step.done + 3)
            dve.tensor_tensor(parts[:, :, 2, :], rest, parts[:, :, 1, :], ALU.subtract).then_inc(step.handle, 1)
            dve.wait_ge(turned.handle, turned.done + TILES)
            dve.tensor_copy(mT[:, :], psb[0:3 * heads, 0:1024])
    scored.done += TILES
    topped.done += TILES
    if a.stacked:
        fetched.done += 16 * len(Q_PARTS)
    step.done += 4
    turned.done += TILES

    if a.stacked:
        weigh_stacked(k, a, mask, scale, wo, dst, mT)
        return
    if a.keys == S:
        weigh_shared(k, a, scale, wo, dst, mT)
        return

    made, expd, summed, freed, recipd = (k.sig("st_made"), k.sig("expd"), k.sig("pv_done"), k.sig("o_done"),
                                         k.sig("recipd"))
    pairs = ct // 2
    nh = k.nh[heads]
    vw = 2 * (hd + 1)
    per = 2
    vcols = per * vw
    obanks = ct // per
    with nc.Block() as block:
        @block.tensor
        def _(pe):
            for b in range(B + 1):
                if b < B:
                    for i in range(pairs):
                        n = b * pairs + i
                        if n >= 4:
                            pe.wait_ge(expd.handle, expd.done + n - 3)
                        for jj in range(2):
                            j = 2 * i + jj
                            out = k.ps[:, n % 4, jj * 256:(jj + 1) * 256]
                            pe.matmul(out, a.kblk[:, b, j * P:(j + 1) * P], a.qT[:, b, a.group(j), :],
                                      start=True, stop=False)
                            ins = pe.matmul(out, nh[0:3 * heads, j * P:(j + 1) * P], mT[:, b * S:(b + 1) * S],
                                            start=False, stop=True)
                        ins.then_inc(made.handle, 1)
                if b >= 1:
                    c0 = b - 1
                    pe.wait_ge(expd.handle, expd.done + pairs * b)
                    for tl in range(2):
                        t = 2 * c0 + tl
                        if t >= 2:
                            pe.wait_ge(freed.handle, freed.done + t - 1)
                        for j in range(ct):
                            lhs = a.probs[:, c0 % 2, j, tl * P:(tl + 1) * P]
                            bank = 4 + (t % 2) * obanks + j // per
                            ins = pe.matmul(k.ps[:, bank, (j % per) * vw:(j % per + 1) * vw], lhs,
                                            a.v[:, c0, j, :], start=True, stop=True)
                        ins.then_inc(summed.handle, 1)

        @block.scalar
        def _(act):
            for b in range(B):
                if b >= 2:
                    act.wait_ge(summed.handle, summed.done + 2 * (b - 1))
                for i in range(pairs):
                    n = b * pairs + i
                    act.wait_ge(made.handle, made.done + n + 1)
                    act.activation(a.probs[:, b % 2, 2 * i:2 * i + 2, :],
                                   k.ps[:, n % 4, :].rearrange("p (j n) -> p j n", j=2), ACT.Exp,
                                   scale=scale).then_inc(expd.handle, 1)

        @block.vector
        def _(dve):
            rec = k.small[:, 256:256 + 2 * heads]
            for t in range(TILES):
                dve.wait_ge(summed.handle, summed.done + t + 1)
                b0 = 4 + (t % 2) * obanks
                hb = heads // obanks
                acc = k.ps[:, b0:b0 + obanks, 0:vcols].rearrange("p b (h c) -> p b h c", c=hd + 1)
                r = rec[:, (t % 2) * heads:(t % 2 + 1) * heads].rearrange("p (b h o) -> p b h o", b=obanks, o=1)
                out = a.o[t].rearrange("p (b h c) -> p b h c", b=obanks, c=hd)
                parts_ = [(acc[:, i], r[:, i], out[:, i], [P, hb, hd]) for i in range(obanks)]
                for n_, (pa, pr, po, shape) in enumerate(parts_):
                    dve.reciprocal(pr, pa[:, :, hd:hd + 1]).then_inc(recipd.handle, 1)
                    dve.wait_ge(recipd.handle, recipd.done + t * obanks + n_ + 1)
                    ins = dve.tensor_tensor(po, pa[:, :, 0:hd], pr.to_broadcast(shape), ALU.mult)
                ins.then_inc(freed.handle, 1)
    made.done += B * pairs
    expd.done += B * pairs
    summed.done += TILES
    freed.done += TILES
    recipd.done += TILES * obanks

    kept, out_made, added = k.sig("ot_kept"), k.sig("wo_made"), k.sig("wo_added")
    g = a.groups
    d3 = k.tiles(dst)
    with nc.Block() as block:
        @block.tensor
        def _(pe):
            for t in range(TILES + 1):
                if t < TILES:
                    if t >= 2:
                        pe.wait_ge(kept.handle, kept.done + t - 1)
                    for i in range(g):
                        ins = pe.transpose(k.ps[:, t % 2, i * P:(i + 1) * P], a.o[t][:, i * P:(i + 1) * P], c["ident"])
                    ins.then_inc(turned.handle, 1)
                if t >= 1:
                    u = t - 1
                    pe.wait_ge(kept.handle, kept.done + u + 1)
                    if u >= 2:
                        pe.wait_ge(added.handle, added.done + u - 1)
                    for i in range(g):
                        ins = pe.matmul(k.ps[:, 2 + u % 2, 0:P], a.ot[:, (u % 2) * a.otw + i * P:(u % 2) * a.otw + (i + 1) * P],
                                        wo[:, i * P:(i + 1) * P], start=i == 0, stop=i == g - 1)
                    ins.then_inc(out_made.handle, 1)

        @block.scalar
        def _(act):
            for t in range(TILES):
                act.wait_ge(turned.handle, turned.done + t + 1)
                if t >= 2:
                    act.wait_ge(out_made.handle, out_made.done + t - 1)
                act.activation(a.ot[:, (t % 2) * a.otw:(t % 2 + 1) * a.otw], k.ps[:, t % 2, 0:a.otw],
                               ACT.Copy).then_inc(kept.handle, 1)

        @block.vector
        def _(dve):
            for t in range(TILES):
                dve.wait_ge(out_made.handle, out_made.done + t + 1)
                dve.tensor_tensor(d3[:, t, :], k.ps[:, 2 + t % 2, 0:P], d3[:, t, :], ALU.add).then_inc(added.handle, 1)
    turned.done += TILES
    kept.done += TILES
    out_made.done += TILES
    added.done += TILES


def first_argmax(dve, step, n, val, top, hot, tmp, desc, e):
    shape = [P, TILES, e]
    d = desc[:, None, 0:e].to_broadcast(shape)
    dve.tensor_reduce(top, val, X, ALU.max).then_inc(step, 1)
    dve.wait_ge(step, n + 1)
    dve.tensor_tensor(hot, val, top[:, :, None].to_broadcast(shape), ALU.is_equal).then_inc(step, 1)
    dve.wait_ge(step, n + 2)
    dve.tensor_tensor(hot, hot, d, ALU.mult).then_inc(step, 1)
    dve.wait_ge(step, n + 3)
    dve.tensor_reduce(tmp, hot, X, ALU.max).then_inc(step, 1)
    dve.wait_ge(step, n + 4)
    dve.tensor_tensor(hot, tmp[:, :, None].to_broadcast(shape), d, ALU.is_equal).then_inc(step, 1)
    dve.wait_ge(step, n + 5)
    return n + 5


def make_logits(k, pe, w, e, made):
    for t in range(TILES):
        ins = pe.matmul(k.ps[:, 0, t * e:(t + 1) * e], k.xnT[:, t * P:(t + 1) * P], w, start=True, stop=True)
    ins.then_inc(made.handle, 1)


def softmax_top2(k, w, lg, e, bias, hot1, hot2, p1, p2, scratch):
    step, expd, made = k.sig("gate_step"), k.sig("gate_exp"), k.sig("logits_made")
    v = lg.rearrange("p (t e) -> p t e", e=e)
    shape = [P, TILES, e]
    tmp, rest = scratch[:, 0:8], scratch[:, 8:8 + TILES * e].rearrange("p (t e) -> p t e", e=e)
    n0 = step.done
    with k.nc.Block() as block:
        @block.vector
        def _(dve):
            s = step.handle
            dve.wait_ge(made.handle, made.done + 1)
            dve.tensor_tensor(v, k.ps[:, 0, 0:TILES * e].rearrange("p (t e) -> p t e", e=e),
                              bias[:, None, :].to_broadcast(shape), ALU.add).then_inc(s, 1)
            dve.wait_ge(s, n0 + 1)
            dve.tensor_reduce(tmp, v, X, ALU.max).then_inc(s, 1)
            dve.wait_ge(s, n0 + 2)
            dve.tensor_tensor(v, v, tmp[:, :, None].to_broadcast(shape), ALU.subtract).then_inc(s, 1)
            dve.wait_ge(expd.handle, expd.done + 1)
            dve.tensor_reduce(tmp, v, X, ALU.add).then_inc(s, 1)
            dve.wait_ge(s, n0 + 4)
            dve.reciprocal(tmp, tmp).then_inc(s, 1)
            dve.wait_ge(s, n0 + 5)
            dve.tensor_tensor(v, v, tmp[:, :, None].to_broadcast(shape), ALU.mult).then_inc(s, 1)
            dve.wait_ge(s, n0 + 6)
            n = first_argmax(dve, s, n0 + 6, v, p1, hot1, tmp, k.c["expdesc"], e)
            dve.scalar_tensor_tensor(rest, hot1, -2.0, v, ALU.mult, ALU.add).then_inc(s, 1)
            dve.wait_ge(s, n + 1)
            first_argmax(dve, s, n + 1, rest, p2, hot2, tmp, k.c["expdesc"], e)

        @block.tensor
        def _(pe):
            make_logits(k, pe, w, e, made)

        @block.scalar
        def _(act):
            act.wait_ge(step.handle, n0 + 3)
            act.activation(lg, lg, ACT.Exp).then_inc(expd.handle, 1)
    made.done += 1
    step.done += 17
    expd.done += 1


def moe_linear(k):
    c, nc = k.c, k.nc
    w = k.work
    lg = w[:, 0:128]
    hot1 = w[:, 128:256].rearrange("p (t e) -> p t e", e=16)
    hot2 = w[:, 256:384].rearrange("p (t e) -> p t e", e=16)
    p1, p2 = w[:, 384:392], w[:, 392:400]
    gate = w[:, 400:400 + 144].rearrange("p (t e) -> p t e", e=18)
    gateT = w[:, 1024:2048]
    scratch = w[:, 600:800]
    ws = w[:, 800:928]
    softmax_top2(k, c["f0cent"], lg, 16, c["f0eb"], hot1, hot2, p1, p2, scratch)
    step, turned, made = k.sig("lin_step"), k.sig("turned"), k.sig("lin_made")
    n0 = step.done
    kept = k.sig("lin_kept")
    x3 = k.tiles(k.x)

    def sums_until(n):
        return n // 10 * 34 + (n % 10 // 2 + 1) * 8 if n % 10 < 8 else (n // 10 + 1) * 34

    with nc.Block() as block:
        @block.vector
        def _(dve):
            s = step.handle
            dve.tensor_tensor(hot1, hot1, hot2, ALU.add).then_inc(s, 1)
            dve.wait_ge(s, n0 + 1)
            dve.memset(gate[:, :, 16:18], 0.5)
            dve.tensor_tensor(gate[:, :, 0:16], hot1, lg.rearrange("p (t e) -> p t e", e=16), ALU.mult).then_inc(s, 1)
            dve.tensor_tensor(ws, c["f0ws"][:, 0:128], c["f0ws"][:, 128:256], ALU.add).then_inc(s, 1)
            dve.wait_ge(s, n0 + 3)
            dve.tensor_scalar(ws, ws, 0.5, None, ALU.mult).then_inc(s, 1)

        @block.gpsimd
        def _(pool):
            pool.tensor_tensor(k.x[:, :], k.x[:, :], k.xn[:, :], ALU.add)

        @block.tensor
        def _(pe):
            pe.wait_ge(step.handle, n0 + 4)
            for t in range(TILES):
                pe.transpose(k.ps[0:18, t // 4, t % 4 * P:(t % 4 + 1) * P], gate[:, t, :], c["ident"]).then_inc(turned.handle, 1)

        @block.scalar
        def _(act):
            act.wait_ge(turned.handle, turned.done + TILES)
            for h in range(2):
                act.activation(gateT[0:18, h * 512:(h + 1) * 512], k.ps[0:18, h, :], ACT.Copy)
    turned.done += TILES
    step.done += 4
    with nc.Block() as block:
        @block.tensor
        def _(pe):
            n = 0
            for t2 in range(0, TILES, 2):
                for q in range(5):
                    for t in (t2, t2 + 1):
                        tok = slice(t * P, (t + 1) * P)
                        if n >= 8:
                            pe.wait_ge(kept.handle, kept.done + sums_until(n - 8))
                        if q < 4:
                            ins = pe.matmul(k.ps[:, n % 8, :], k.xnT[:, tok], c["f0wr"][:, q * 512:(q + 1) * 512],
                                            start=True, stop=True)
                        else:
                            pe.matmul(k.ps[:, n % 8, 0:P], k.xnT[:, tok], ws, start=True, stop=False)
                            ins = pe.matmul(k.ps[:, n % 8, 0:P], gateT[0:18, tok], c["f0br"][0:18, :], start=False,
                                            stop=True)
                        ins.then_inc(made.handle, 1)
                        n += 1

        @block.vector
        def _(dve):
            m = 0
            for t2 in range(0, TILES, 2):
                for q in range(5):
                    n = 5 * t2 + 2 * q
                    for i in range(4 if q < 4 else 1):
                        for t in (t2, t2 + 1):
                            if i == 0:
                                dve.wait_ge(made.handle, made.done + n + t - t2 + 1)
                            if m >= 2:
                                dve.wait_ge(kept.handle, kept.done + m - 1)
                            out = k.ps[:, (n + t - t2) % 8, i * P:(i + 1) * P]
                            if q < 4:
                                e = 4 * q + i
                                ins = dve.scalar_tensor_tensor(x3[:, t, :], out, gate[:, t, e:e + 1], x3[:, t, :],
                                                               ALU.mult, ALU.add)
                            else:
                                ins = dve.tensor_tensor(x3[:, t, :], out, x3[:, t, :], ALU.add)
                            ins.then_inc(kept.handle, 1)
                            m += 1
    made.done += 40
    kept.done += 17 * TILES


def routing(k, gate, e, w, score, rows=None, scatter=None):
    nc, c = k.nc, k.c
    lg = w["lg"]
    shape = [P, TILES, e]
    lg3 = lg.rearrange("p (t e) -> p t e", e=e)
    hot = w["hot"].rearrange("p (t e) -> p t e", e=e)
    step, expd, made = k.sig("route_step"), k.sig("gate_exp"), k.sig("route_made")
    lg_made, lg_kept = k.sig("logits_made"), k.sig("logits_kept")
    n0 = step.done
    top, tmp8, pos, posi = w["top"], w["tmp8"], w["pos"], w["posi"]
    hotb, tot, incl, t1 = w["hotb"], w["tot"], w["incl"], w["t1"]
    ends, reach, mtab = w["ends"], w["reach"], w["mtab"]
    with nc.Block() as block:
        @block.vector
        def _(dve):
            s = step.handle
            fill_route_constants(k, w, dve)
            dve.wait_ge(lg_kept.handle, lg_kept.done + 1)
            n = first_argmax(dve, s, n0, lg3, top, hot, tmp8, c["expdesc"], e)
            dve.tensor_copy(hotb, w["hot"]).then_inc(s, 1)
            dve.wait_ge(expd.handle, expd.done + 1)
            dve.tensor_scalar(score, score, 1.0, None, ALU.add).then_inc(s, 1)
            dve.wait_ge(s, n + 2)
            dve.reciprocal(score, score).then_inc(s, 1)
            dve.wait_ge(made.handle, made.done + 2)
            dve.tensor_copy(tot.rearrange("p (e t) -> p t e", t=TILES),
                            k.ps[:, 2, 0:TILES * e].rearrange("p (t e) -> p t e", e=e)).then_inc(s, 1)
            dve.wait_ge(s, n + 4)
            dve.tensor_tensor_scan(incl, w["one256"], tot, 0.0,
                                   ALU.mult, ALU.add).then_inc(s, 1)
            dve.wait_ge(s, n + 5)
            inc3 = incl.rearrange("p (e t) -> p t e", t=TILES)
            t13 = t1.rearrange("p (t e) -> p t e", e=e)
            dve.tensor_tensor(t13, k.ps[:, 1, 0:TILES * e].rearrange("p (t e) -> p t e", e=e), inc3, ALU.add).then_inc(s, 1)
            dve.wait_ge(s, n + 6)
            dve.tensor_tensor(t1, t1, w["hot"], ALU.mult).then_inc(s, 1)
            dve.wait_ge(s, n + 7)
            dve.tensor_reduce(pos, t13, X, ALU.add).then_inc(s, 1)
            dve.wait_ge(s, n + 8)
            dve.tensor_copy(posi, pos).then_inc(s, 1)
            dve.tensor_copy(ends, incl.rearrange("p (e t) -> p e t", t=TILES)[:, :, TILES - 1]).then_inc(s, 1)
            dve.wait_ge(s, n + 10)
            dve.tensor_tensor(t13, ends[:, None, :].to_broadcast(shape), c["token_at"][:, :, None].to_broadcast(shape),
                              ALU.is_gt).then_inc(s, 1)
            dve.wait_ge(s, n + 11)
            m3 = mtab[:, 0:TILES * e].rearrange("p (t e) -> p t e", e=e)
            dve.tensor_copy(m3[:, :, 0:1], t13[:, :, 0:1])
            dve.tensor_tensor(m3[:, :, 1:e], t13[:, :, 1:e], t13[:, :, 0:e - 1], ALU.subtract)
            dve.memset(mtab[:, TILES * e:TILES * e + 1], 0.0)
            r3 = reach[0:1, 0:e * 7].rearrange("p (e t) -> p e t", t=7)
            dve.tensor_tensor(r3, ends[0:1, :, None].to_broadcast([1, e, 7]),
                              c["tile_end"][0:1, None, :].to_broadcast([1, e, 7]), ALU.is_gt).then_inc(s, 1)
            dve.wait_ge(s, n + 12)
            dve.tensor_reduce(w["re"][0:1, :], r3, X, ALU.add).then_inc(s, 1)
            dve.wait_ge(s, n + 13)
            dve.tensor_tensor(w["re"][0:1, :], w["re"][0:1, :], c["expert_at"][0:1, 0:e], ALU.add).then_inc(s, 1)
            dve.wait_ge(s, n + 14)
            steps = TILES + e
            p3 = w["walk"][0:1, 0:steps * (e - 1)].rearrange("p (i e) -> p i e", e=e - 1)
            dve.tensor_tensor(p3, c["step_at"][0:1, 0:steps, None].to_broadcast([1, steps, e - 1]),
                              w["re"][0:1, None, 0:e - 1].to_broadcast([1, steps, e - 1]), ALU.is_gt).then_inc(s, 1)
            dve.wait_ge(s, n + 15)
            ef, tf, mf = w["wf"][0:1, 0:40], w["wf"][0:1, 40:80], w["wf"][0:1, 80:120]
            dve.tensor_reduce(ef[:, 0:steps], p3, X, ALU.add).then_inc(s, 1)
            dve.wait_ge(s, n + 16)
            dve.tensor_tensor(tf[:, 0:steps], c["step_at"][0:1, 0:steps], ef[:, 0:steps], ALU.subtract).then_inc(s, 1)
            dve.wait_ge(s, n + 17)
            dve.scalar_tensor_tensor(mf[:, 0:steps], tf[:, 0:steps], float(e), ef[:, 0:steps], ALU.mult, ALU.add).then_inc(s, 1)
            dve.wait_ge(s, n + 18)
            dve.tensor_scalar(mf[:, 0:steps], mf[:, 0:steps], float(TILES * e), None, ALU.min)
            dve.tensor_scalar(tf[:, 0:steps], tf[:, 0:steps], float(TILES - 1), None, ALU.min).then_inc(s, 1)
            dve.wait_ge(s, n + 19)
            dve.tensor_copy(w["wi"][0:1, 0:40], ef)
            dve.tensor_copy(w["wi"][0:1, 40:80], tf)
            dve.tensor_copy(w["wi"][0:1, 80:120], mf)

        if rows is not None:
            @block.gpsimd
            def _(pool):
                pool.wait_ge(step.handle, n0 + 8)
                pool.tensor_tensor(k.tiles(rows), k.tiles(k.xn), score[:, :, None].to_broadcast([P, TILES, D]),
                                   ALU.mult)

        if scatter is not None:
            @block.gpsimd
            def _(pool):
                pool.wait_ge(step.handle, n0 + 14)
                scatter[0](pool)

            block.sync(scatter[1])

        @block.scalar
        def _(act):
            act.wait_ge(lg_made.handle, lg_made.done + 1)
            act.activation(lg, k.ps[:, 0, 0:TILES * e], ACT.Copy).then_inc(lg_kept.handle, 1)
            act.wait_ge(step.handle, n0 + 5)
            act.activation(score, top, ACT.Exp, scale=-1.0).then_inc(expd.handle, 1)

        @block.tensor
        def _(pe):
            make_logits(k, pe, gate, e, lg_made)
            pe.wait_ge(step.handle, n0 + 6)
            pe.matmul(k.ps[:, 1, 0:TILES * e], w["geb"], hotb, start=True, stop=True).then_inc(made.handle, 1)
            pe.matmul(k.ps[:, 2, 0:TILES * e], w["oneb"], hotb, start=True, stop=True).then_inc(made.handle, 1)
    lg_made.done += 1
    lg_kept.done += 1
    step.done += 24
    expd.done += 1
    made.done += 2


def route_buffers(k, e, base):
    sizes = [("lg", 8 * e), ("hot", 8 * e), ("tot", 8 * e), ("incl", 8 * e), ("t1", 8 * e), ("one256", 8 * e),
             ("mtab", 8 * e + 8), ("ends", e), ("re", e), ("walk", (8 + e) * (e - 1)), ("wf", 120),
             ("top", 8), ("tmp8", 8), ("pos", 8), ("score", 8), ("hotb", 4 * e), ("geb", 64), ("oneb", 64),
             ("posi", 8), ("wi", 128)]
    w = {}
    for name, n in sizes:
        v = k.work[:, base:base + n]
        base += n
        if name in ("posi", "score"):
            v = k.small[:, 900 + 8 * (name == "posi"):908 + 8 * (name == "posi")]
            base -= n
        if name in ("hotb", "geb", "oneb"):
            v = v.bitcast(BF16)
        if name in ("posi", "wi"):
            v = v.bitcast(I32)
        w[name] = v
    assert base <= WORK, base
    w["reach"] = w["lg"]
    return w


def fill_route_constants(k, w, dve):
    dve.memset(w["one256"], 1.0)
    dve.memset(w["wf"], 0.0)
    dve.tensor_copy(w["geb"], k.c["count_ge"])
    dve.tensor_copy(w["oneb"], k.c["ones"])


def scatter_rows(k, w, rows, scratch, sorted_rows):
    sent, back = k.sig("rows_scattered"), k.sig("sorted_loaded")
    r3 = k.tiles(rows)
    at = sent.done, back.done

    def pool_part(pool):
        for t in range(TILES):
            pool.indirect_dma_start(out=scratch, out_offset=bass.IndirectOffsetOnAxis(
                ap=w["posi"][:, t:t + 1].bitcast(U32), axis=0), in_=r3[:, t, :], in_offset=None).then_inc(sent.handle, 16)

    def sync_part(sp):
        sp.wait_ge(sent.handle, at[0] + 16 * TILES)
        sp.dma_start(k.tiles(sorted_rows), scratch.rearrange("(t p) d -> p t d", p=P)).then_inc(back.handle, 16)
        sp.wait_ge(back.handle, at[1] + 16)

    sent.done += 16 * TILES
    back.done += 16
    return pool_part, sync_part


def gather_rows(k, w, sorted_rows, scratch, rows):
    sent, back = k.sig("sorted_stored"), [k.sig(f"rows_gathered{t}") for t in range(TILES)]
    r3 = k.tiles(rows)
    at = sent.done, back[0].done

    def pool_part(pool):
        pool.wait_ge(sent.handle, at[0] + 16)
        for t in range(TILES):
            pool.indirect_dma_start(out=r3[:, t, :], out_offset=None, in_=scratch, in_offset=bass.IndirectOffsetOnAxis(
                ap=w["posi"][:, t:t + 1].bitcast(U32), axis=0)).then_inc(back[t].handle, 16)

    def sync_part(sp):
        sp.dma_start(scratch.rearrange("(t p) d -> p t d", p=P), k.tiles(sorted_rows)).then_inc(sent.handle, 16)

    def wait_rows(eng, t):
        eng.wait_ge(back[t].handle, at[1] + 16)

    sent.done += 16
    for b in back:
        b.done += 16
    return pool_part, sync_part, wait_rows


def walk_experts(k, w, e, srcT, y, layer):
    nc = k.nc
    steps = TILES + e
    assert (steps - 4) % TURN == 0
    gated = layer == 1
    ft = 2 if gated else 4
    each = 768 if gated else 1024
    wm = k.wmoe[:, 0:e * each].rearrange("p (e n) -> p e n", e=e)
    staged, up, act_done, hid, trn, hT_done, down, acc = (k.sig(n) for n in (
        "staged", "up_made", "silu_done", "hidden", "hidden_turned", "hT_kept", "down_made", "y_added"))
    base = {s: s.done for s in (staged, up, act_done, hid, trn, hT_done, down, acc)}
    at = 4096
    stage = [k.work[:, at + i * P:at + (i + 1) * P] for i in range(2)]
    sg = [k.work[:, at + 256 + i * 256:at + 512 + i * 256] for i in range(2)]
    hb = [k.work[:, at + 768 + i * 512:at + 768 + i * 512 + ft * P] for i in range(2)]
    ht = [k.work[:, at + 1792 + i * 512:at + 1792 + i * 512 + ft * P] for i in range(2)]
    tmp = [k.work[:, at + 2816 + i * P:at + 2816 + (i + 1) * P] for i in range(2)]
    y3 = k.tiles(y)
    s3 = srcT.rearrange("p (t n) -> p t n", n=P)
    mtab = w["mtab"]
    wi = w["wi"]

    def wait(eng, sig, n):
        eng.wait_ge(sig.handle, base[sig] + n)

    def entries(eng, kind, row, i, n, top):
        _, values = nc.values_load_multi_w_load_instructions(
            wi[0:1, bass.ds(i + 40 * row, n)], engines=(kind,), min_val=0, max_val=top,
            skip_runtime_bounds_check_because="routing() clamps the table, whose entries count comparisons")
        return values

    PE, ACTE, DVE = mybir.EngineType.PE, mybir.EngineType.Activation, mybir.EngineType.DVE

    with nc.Block() as block:
        @block.tensor
        def _(pe):
            def up_product(i, r, ex, free=True):
                wait(pe, staged, i + 1)
                if free:
                    wait(pe, hid, i - 1)
                pe.matmul(k.ps[:, r, :], stage[r], wm[:, ex, 0:512], start=True, stop=True).then_inc(up.handle, 1)

            def turn_hidden(i, r, free=True):
                wait(pe, hid, i + 1)
                if free:
                    wait(pe, hT_done, i - 1)
                for f in range(ft):
                    ins = pe.transpose(k.ps[:, 2 + r, f * P:(f + 1) * P], hb[r][:, f * P:(f + 1) * P], k.c["ident"])
                ins.then_inc(trn.handle, 1)

            def down_product(i, r, ex, free=True):
                wait(pe, hT_done, i + 1)
                if free:
                    wait(pe, acc, i - 1)
                for f in range(ft):
                    ins = pe.matmul(k.ps[:, 4 + r, 0:P], ht[r][:, f * P:(f + 1) * P],
                                    wm[:, ex, 512 + f * P:512 + (f + 1) * P], start=f == 0, stop=f == ft - 1)
                ins.then_inc(down.handle, 1)

            ex = entries(pe, PE, 0, 0, 4, e - 1)
            for i in range(4):
                up_product(i, i % 2, ex[i], i >= 2)
                if i >= 1:
                    turn_hidden(i - 1, (i - 1) % 2, i - 1 >= 2)
                if i >= 2:
                    down_product(i - 2, i % 2, ex[i - 2], i - 2 >= 2)
            with pe.Fori(4, steps, TURN) as i:
                ex = entries(pe, PE, 0, i - 2, TURN + 2, e - 1)
                for u in range(TURN):
                    up_product(i + u, u % 2, ex[u + 2])
                    turn_hidden(i + u - 1, (u + 1) % 2)
                    down_product(i + u - 2, u % 2, ex[u])
            ex = entries(pe, PE, 0, steps - 2, 2, e - 1)
            turn_hidden(steps - 1, 1)
            down_product(steps - 2, 0, ex[0])
            down_product(steps - 1, 1, ex[1])

        @block.scalar
        def _(act):
            def stage_in(i, r, t, ex, free=True):
                if free:
                    wait(act, up, i - 1)
                if gated:
                    act.activation(stage[r], s3[:, t, :], ACT.Copy).then_inc(staged.handle, 1)
                else:
                    act.activation(stage[r], s3[:, t, :], ACT.Identity, scale=k.c["f3g"][:, bass.ds(ex, 1)],
                                   bias=k.c["f3b"][:, bass.ds(ex, 1)]).then_inc(staged.handle, 1)

            def silu(i, r, ex, free=True):
                wait(act, up, i + 1)
                if free:
                    wait(act, hid, i - 1)
                act.activation(sg[r], k.ps[:, r, 0:256], ACT.Silu).then_inc(act_done.handle, 1)

            def relu(i, r, ex, free=True):
                wait(act, trn, i + 1)
                if free:
                    wait(act, down, i - 1)
                for f in range(ft):
                    ins = act.activation(ht[r][:, f * P:(f + 1) * P], k.ps[:, 2 + r, f * P:(f + 1) * P], ACT.Relu,
                                         bias=k.c["f3b1"].rearrange("p (e f) -> p e f", f=4)[:, ex, f:f + 1])
                ins.then_inc(hT_done.handle, 1)

            def expert(i, n):
                return [None] * n if gated else entries(act, ACTE, 0, i, n, e - 1)

            after = silu if gated else relu

            def both(i, r, t, ex, ex_next, free=True):
                if gated:
                    after(i, r, ex, free)
                    stage_in(i + 2, r, t, ex_next)
                else:
                    stage_in(i + 2, r, t, ex_next)
                    after(i, r, ex, free)

            t, ex = entries(act, ACTE, 1, 0, 4, TILES - 1), expert(0, 4)
            stage_in(0, 0, t[0], ex[0], False)
            stage_in(1, 1, t[1], ex[1], False)
            both(0, 0, t[2], ex[0], ex[2], False)
            both(1, 1, t[3], ex[1], ex[3], False)
            with act.Fori(2, steps - 2, TURN) as i:
                t, ex = entries(act, ACTE, 1, i + 2, TURN, TILES - 1), expert(i, TURN + 2)
                for u in range(TURN):
                    both(i + u, u % 2, t[u], ex[u], ex[u + 2])
            ex = expert(steps - 2, 2)
            after(steps - 2, 0, ex[0])
            after(steps - 1, 1, ex[1])

        @block.vector
        def _(dve):
            def hidden(i, r, free=True):
                wait(dve, act_done if gated else up, i + 1)
                if free:
                    wait(dve, trn, i - 1)
                if gated:
                    dve.tensor_tensor(hb[r], k.ps[:, r, 256:512], sg[r], ALU.mult).then_inc(hid.handle, 1)
                else:
                    dve.tensor_copy(hb[r], k.ps[:, r, :]).then_inc(hid.handle, 1)

            def keep_turned(i, r, free=True):
                if not gated:
                    return
                wait(dve, trn, i + 1)
                if free:
                    wait(dve, down, i - 1)
                dve.tensor_copy(ht[r], k.ps[:, 2 + r, 0:ft * P]).then_inc(hT_done.handle, 1)

            def add_up(i, r, t, m, ex, free=True):
                wait(dve, down, i + 1)
                src = k.ps[:, 4 + r, 0:P]
                if not gated:
                    dve.tensor_tensor(tmp[r], src, k.c["f3b2"].rearrange("p (e n) -> p e n", e=e)[:, ex, :],
                                      ALU.add).then_inc(act_done.handle, 1)
                    wait(dve, act_done, i + 1)
                    src = tmp[r]
                if free:
                    wait(dve, acc, i)
                dve.scalar_tensor_tensor(y3[:, t, :], src, mtab[:, bass.ds(m, 1)], y3[:, t, :],
                                         ALU.mult, ALU.add).then_inc(acc.handle, 1)

            def indices(i, n):
                return (entries(dve, DVE, 1, i, n, TILES - 1), entries(dve, DVE, 2, i, n, TILES * e),
                        [None] * n if gated else entries(dve, DVE, 0, i, n, e - 1))

            dve.memset(y[:, 0:1024], 0.0)
            t, m, ex = indices(0, 2)
            for i in range(4):
                hidden(i, i % 2, i >= 2)
                if i >= 1:
                    keep_turned(i - 1, (i - 1) % 2, i - 1 >= 2)
                if i >= 2:
                    add_up(i - 2, i % 2, t[i - 2], m[i - 2], ex[i - 2], i >= 3)
            with dve.Fori(4, steps, TURN) as i:
                t, m, ex = indices(i - 2, TURN)
                for u in range(TURN):
                    hidden(i + u, u % 2)
                    keep_turned(i + u - 1, (u + 1) % 2)
                    add_up(i + u - 2, u % 2, t[u], m[u], ex[u])
            t, m, ex = indices(steps - 2, 2)
            keep_turned(steps - 1, 1)
            add_up(steps - 2, 0, t[0], m[0], ex[0])
            add_up(steps - 1, 1, t[1], m[1], ex[1])
    for s in base:
        s.done += steps


def swiglu_dense(k, experts, wg, wu, wd, ft, weights, dst, beside=None):
    nc = k.nc
    made, silud, hid, down, acc = (k.sig(n) for n in ("up_made", "silu_done", "hidden", "down_made", "y_added"))
    b = {s: s.done for s in (made, silud, hid, down, acc)}
    sg = [k.work[:, 4096 + i * 512:4608 + i * 512] for i in range(2)]
    h = [k.work[:, 5120 + i * 512 * ft:5120 + (i + 1) * 512 * ft] for i in range(2)]
    d3 = k.tiles(dst)
    items = [(e, half) for e in experts for half in range(2)]

    with nc.Block() as block:
        if beside:
            block.gpsimd(beside[0])
            block.sync(beside[1])

        @block.tensor
        def _(pe):
            for i in range(len(items) + 1):
                if i < len(items):
                    e, half = items[i]
                    for f in range(ft):
                        n = i * ft + f
                        if n >= 2:
                            pe.wait_ge(hid.handle, b[hid] + n - 1)
                        rhs = k.xnT[:, half * 512:(half + 1) * 512]
                        pe.matmul(k.ps[:, 2 * (n % 2), :], wg(e, f), rhs, start=True, stop=True)
                        pe.matmul(k.ps[:, 2 * (n % 2) + 1, :], wu(e, f), rhs, start=True, stop=True).then_inc(made.handle, 1)
                if i >= 1:
                    m = i - 1
                    e, half = items[m]
                    pe.wait_ge(hid.handle, b[hid] + ft * (m + 1))
                    if m >= 2:
                        pe.wait_ge(acc.handle, b[acc] + 4 * (m - 1))
                    for q in range(4):
                        for f in range(ft):
                            ins = pe.matmul(k.ps[:, 4 + m % 2, q * P:(q + 1) * P],
                                            h[m % 2][:, f * 512 + q * P:f * 512 + (q + 1) * P], wd(e, f),
                                            start=f == 0, stop=f == ft - 1)
                    ins.then_inc(down.handle, 1)

        @block.scalar
        def _(act):
            for n in range(len(items) * ft):
                act.wait_ge(made.handle, b[made] + n + 1)
                if n >= 2:
                    act.wait_ge(hid.handle, b[hid] + n - 1)
                act.activation(sg[n % 2], k.ps[:, 2 * (n % 2), :], ACT.Silu).then_inc(silud.handle, 1)

        @block.vector
        def _(dve):
            def hidden(n):
                i, f = n // ft, n % ft
                dve.wait_ge(silud.handle, b[silud] + n + 1)
                if i >= 2:
                    dve.wait_ge(down.handle, b[down] + i - 1)
                dve.tensor_tensor(h[i % 2][:, f * 512:(f + 1) * 512], k.ps[:, 2 * (n % 2) + 1, :], sg[n % 2],
                                  ALU.mult).then_inc(hid.handle, 1)

            def add_up(m):
                e, half = items[m]
                dve.wait_ge(down.handle, b[down] + m + 1)
                for q in range(4):
                    t = half * 4 + q
                    if m >= 2 and q == 0:
                        dve.wait_ge(acc.handle, b[acc] + 4 * m - 4)
                    src = k.ps[:, 4 + m % 2, q * P:(q + 1) * P]
                    wt = weights(e, t)
                    if wt is None:
                        dve.tensor_tensor(d3[:, t, :], src, d3[:, t, :], ALU.add).then_inc(acc.handle, 1)
                    else:
                        dve.scalar_tensor_tensor(d3[:, t, :], src, wt, d3[:, t, :], ALU.mult, ALU.add).then_inc(acc.handle, 1)

            for i in range(len(items)):
                for f in range(ft):
                    hidden(i * ft + f)
                if i >= 1:
                    add_up(i - 1)
            add_up(len(items) - 1)
    made.done += len(items) * ft
    silud.done += len(items) * ft
    hid.done += len(items) * ft
    down.done += len(items)
    acc.done += 4 * len(items)


def landed(k, *names):
    def sync_part(sp):
        for name in names:
            sp.wait_ge(k.load_sem[name], 48 if name == "mask" else 16)
    return sync_part


def wait_load(k, *names):
    with k.nc.Block() as block:
        block.sync(landed(k, *names))


def build(nc, dram):
    with ExitStack() as ctx:
        k = Program(nc, ctx, dram)
        c = k.c
        k.mparts = k.sb("mparts", TILES * 48, BF16)
        k.mT = k.sb("mT", 1024, BF16)
        start_loads(k)
        wait_load(k, "consts", "x", "ctx", "mask", "l0a")
        constants(k)

        a = Core(k, H, 8, SC)
        project_k_stacked(k, a, c["a0wk"], c["a0bk"], False)
        norm_turn(k, [(k.xn, LN)], beside=fetch_keys(k, a))
        project_q_stacked(k, a, c["a0wq"], c["a0bq"], False, c["a0wv"], c["a0bv"], c["a0bo"])
        mask0 = [(lambda b, at, n: k.mb[0:SC, b * S + at:b * S + at + n], k.i64big[0:SC, :])]

        def load_layer_1(sp):
            for name in ("l0f", "l1a", "l1s"):
                sp.dma_start(dict(k.loads)[name], dram[name]).then_inc(k.load_sem[name], 16)
            sp.dma_start(k.wmoe[:, 0:EARLY], dram["moe1"][:, 0:EARLY]).then_inc(k.load_sem["moe1"], 16)

        attend(k, a, mask0, 8 ** -0.5, c["a0wo"], k.x, load_layer_1)

        norm_turn(k, [(k.xn, LN)], beside=landed(k, "l0f"))
        moe_linear(k)

        gate_step = k.sig("tanh_step")
        with nc.Block() as block:
            @block.sync
            def _(sp):
                sp.dma_start(k.wmoe[:, EARLY:L1M], dram["moe1"][:, EARLY:L1M]).then_inc(k.load_sem["moe1b"], 16)

            @block.scalar
            def _(act):
                act.wait_ge(k.load_sem["l1a"], 16)
                act.activation(k.small[:, 100:101], c["a1gate"], ACT.Tanh).then_inc(gate_step.handle, 1)

            @block.vector
            def _(dve):
                dve.wait_ge(gate_step.handle, 1)
                dve.tensor_scalar(c["a1wo"], c["a1wo"], k.small[:, 100:101], None, ALU.mult)
                dve.tensor_scalar(c["a1bo"], c["a1bo"], k.small[:, 100:101], None, ALU.mult)

        norm_turn(k, [(k.xn, LN_LN)], 0, c["a1g"], c["a1b"])
        for half in range(2):
            a = Core(k, 8, 64, SC)
            part = slice(half * 512, half * 512 + 512)
            project_all(k, a, c["a1wk"][:, part], c["a1wv"][:, part], c["a1wq"][:, part],
                        c["a1bo"] if half == 0 else None)
            attend(k, a, [], 64 ** -0.5, c["a1wo"][:, part], k.x)

        norm_turn(k, [(k.xn, LN)], beside=landed(k, "l1s"))
        w = route_buffers(k, 32, 7168)
        y, srt, xsT = k.work[:, 0:1024], k.work[:, 1024:2048], k.work[:, 2048:3072]
        xs = k.small[:, 1024:2048]
        routing(k, c["f1gw"], 32, w, w["score"], rows=xs)
        scatter = scatter_rows(k, w, xs, dram["scratch0"], srt)
        sgu, sd = c["f1sgu"], c["f1sd"]
        swiglu_dense(k, [0], lambda e, f: sgu[:, f * P:(f + 1) * P], lambda e, f: sgu[:, 256 + f * P:256 + (f + 1) * P],
                     lambda e, f: sd[:, f * P:(f + 1) * P], 2, lambda e, t: None, k.x, scatter)
        turn(k, srt, xsT, landed(k, "moe1", "moe1b"))
        walk_experts(k, w, 32, xsT, y, 1)
        gather = gather_rows(k, w, y, dram["scratch1"], xs)
        with nc.Block() as block:
            @block.sync
            def _(sp):
                sp.dma_start(dict(k.loads)["l2a"], dram["l2a"]).then_inc(k.load_sem["l2a"], 16)

        a = Core(k, H, 8, SC)
        wait_load(k, "l2a")
        project_k_stacked(k, a, c["a2wk"], c["a2bk"], True, gather, xs)
        norm_turn(k, [(k.xn, LN)], beside=fetch_keys(k, a))
        project_q_stacked(k, a, c["a2wq"], c["a2bq"], True, c["a2wv"], c["a2bv"], c["a2bo"])

        def load_layer_3(sp):
            for name in ("l2f", "l3a"):
                sp.dma_start(dict(k.loads)[name], dram[name]).then_inc(k.load_sem[name], 16)
            sp.dma_start(k.wmoe[:, 0:L3M], dram["moe3"]).then_inc(k.load_sem["moe3"], 16)

        attend(k, a, [], 8 ** -0.5, c["a2wo"], k.x, load_layer_3)

        xl = k.xl
        wait_load(k, "l2f", "l3a")
        norm_turn(k, [(xl, LN), (k.xn, LN_RMS)], 1, c["f2g1"])
        a = Core(k, 4, 32, S)
        kept, made = k.sig("k_kept"), k.sig("v_proj")
        with nc.Block() as block:
            @block.tensor
            def _(pe):
                for h in range(2):
                    pe.matmul(k.ps[:, h, :], c["f2wkc"], k.xnT[:, h * 512:(h + 1) * 512], start=True,
                              stop=True).then_inc(kept.handle, 1)
                for t in range(TILES):
                    ins = pe.matmul(k.ps[:, 2, t * 32:(t + 1) * 32], k.xnT[:, t * P:(t + 1) * P], c["f2wvc"],
                                    start=True, stop=True)
                ins.then_inc(made.handle, 1)

            @block.vector
            def _(dve):
                for b in range(B):
                    dve.wait_ge(kept.handle, kept.done + b // 2 + 1)
                    src = k.ps[:, b // 2, b % 2 * S:(b % 2 + 1) * S]
                    dve.tensor_tensor(a.kblk[:, b, :].rearrange("p (h s) -> p h s", s=S),
                                      src[:, None, :].to_broadcast([P, 4, S]),
                                      c["headmask4"][:, :, None].to_broadcast([P, 4, S]), ALU.mult)

            @block.scalar
            def _(act):
                act.wait_ge(made.handle, made.done + 1)
                act.activation(a.v[:, :, 0:32], k.ps[:, 2, 0:256].rearrange("p (t d) -> p t d", d=32), ACT.Copy)
        kept.done += 2
        made.done += 1
        project_q(k, a, c["f2wq"])
        attend(k, a, [], 32 ** -0.5, c["f2wo"], xl)
        rms_turn(k, xl, c["f2g2"], 1e-6)
        wk = k.work
        lg = wk[:, 0:64]
        hot1 = wk[:, 64:128].rearrange("p (t e) -> p t e", e=8)
        hot2 = wk[:, 128:192].rearrange("p (t e) -> p t e", e=8)
        p1, p2, comb = wk[:, 192:200], wk[:, 200:208], wk[:, 208:272].rearrange("p (t e) -> p t e", e=8)
        softmax_top2(k, c["f2wr"], lg, 8, c["f2eb"], hot1, hot2, p1, p2, wk[:, 300:400])
        step, expd = k.sig("gate_step"), k.sig("gate_exp")
        n0 = step.done
        with nc.Block() as block:
            @block.vector
            def _(dve):
                s = step.handle
                dve.tensor_tensor(p2, p2, p1, ALU.subtract).then_inc(s, 1)
                dve.wait_ge(expd.handle, expd.done + 1)
                dve.tensor_scalar(p1, p2, 1.0, None, ALU.add).then_inc(s, 1)
                dve.wait_ge(s, n0 + 2)
                dve.reciprocal(p1, p1).then_inc(s, 1)
                dve.wait_ge(s, n0 + 3)
                dve.tensor_tensor(p2, p2, p1, ALU.mult).then_inc(s, 1)
                dve.tensor_tensor(hot1, hot1, p1[:, :, None].to_broadcast([P, TILES, 8]), ALU.mult).then_inc(s, 1)
                dve.wait_ge(s, n0 + 5)
                dve.tensor_tensor(hot2, hot2, p2[:, :, None].to_broadcast([P, TILES, 8]), ALU.mult).then_inc(s, 1)
                dve.wait_ge(s, n0 + 6)
                dve.tensor_tensor(comb, hot1, hot2, ALU.add)

            @block.scalar
            def _(act):
                act.wait_ge(step.handle, n0 + 1)
                act.activation(p2, p2, ACT.Exp).then_inc(expd.handle, 1)
        step.done += 6
        expd.done += 1
        swiglu_dense(k, list(range(9)), lambda e, f: c["f2w1"][:, e * P:(e + 1) * P],
                     lambda e, f: c["f2w3"][:, e * P:(e + 1) * P], lambda e, f: c["f2w2"][:, e * P:(e + 1) * P], 1,
                     lambda e, t: comb[:, t, e:e + 1] if e < 8 else None, xl)

        a = Core(k, H, 8, SC)
        project_k_stacked(k, a, c["a3wk"], None, False, None, xl)
        norm_turn(k, [(k.xn, LN)], beside=fetch_keys(k, a))
        project_q_stacked(k, a, c["a3wq"], None, False, c["a3wv"], None)
        mask3 = [(lambda b, at, n: k.mb3[:, at:at + n], k.i64[:, :]),
                 (lambda b, at, n: k.mb3[0:SC, 256 + at:256 + at + n], k.i64[0:SC, :])]
        attend(k, a, mask3, D ** -0.5, c["a3wo"], k.x)

        norm_turn(k, [(k.xn, LN), (xs, LN_LN)])
        w = route_buffers(k, 8, 7168)
        routing(k, c["f3cent"], 8, w, w["score"], scatter=scatter_rows(k, w, xs, dram["scratch0"], srt))
        turn(k, srt, xsT, landed(k, "moe3"))
        walk_experts(k, w, 8, xsT, y, 3)
        gather = gather_rows(k, w, y, dram["scratch1"], xs)
        based, summed, stored = k.sig("x_based"), k.sig("x_summed"), k.sig("stored")
        with nc.Block() as block:
            block.gpsimd(gather[0])

            @block.vector
            def _(dve):
                x3 = k.tiles(k.x)
                dve.tensor_tensor(k.x[:, :], k.x[:, :], k.xn[:, :], ALU.add).then_inc(based.handle, 1)
                dve.wait_ge(based.handle, based.done + 1)
                for t in range(TILES):
                    gather[2](dve, t)
                    dve.scalar_tensor_tensor(x3[:, t, :], k.tiles(xs)[:, t, :], w["score"][:, t:t + 1], x3[:, t, :],
                                             ALU.mult, ALU.add).then_inc(summed.handle, 1)

            @block.sync
            def _(sp):
                gather[1](sp)
                for h in range(2):
                    half = slice(h * 512, (h + 1) * 512)
                    sp.wait_ge(summed.handle, summed.done + 4 * h + 4)
                    sp.dma_start(dram["out"][:, half], k.x[:, half]).then_inc(stored.handle, 16)
                sp.wait_ge(stored.handle, 32)


def shape_constants():
    r = np.arange(P)
    f = {}
    f["ident"] = np.eye(P)
    f["count_ge"] = -1.0 * (r[:, None] >= r[None, :])
    f["ones"] = np.ones((P, P))
    f["headmask4"] = r[:, None] // 32 == np.arange(4)
    f["headmask2"] = r[:, None] // 64 == np.arange(2)
    f["pairmask"] = r[:, None] % 16 // 8 == np.arange(2)
    f["ident64"] = r[:, None] % 64 == np.arange(64)
    for heads in (16, 4, 8):
        f[f"neghead{heads}"] = -((r[:, None] % heads == np.arange(heads)) & (r[:, None] < 3 * heads)).astype(np.float32)
    dim = 4
    freqs = np.exp(-np.arange(dim, dtype=np.float32) * np.log(np.float32(10000.0)) / np.float32(dim)).astype(np.float32)
    ang = (np.arange(S, dtype=np.float32)[None, :] * freqs[(r % 8) // 2][:, None]).astype(np.float32)
    f["cosq"], f["sinq"] = np.cos(ang), np.sin(ang)
    rot = np.zeros((P, P))
    rot[r[1::2], r[0::2]] = -1.0
    rot[r[0::2], r[1::2]] = 1.0
    f["rot"] = rot
    f["expdesc"] = np.broadcast_to(64 - np.arange(32), (P, 32))
    f["token_at"] = r[:, None] + P * np.arange(8)
    f["tile_end"] = np.broadcast_to(P * np.arange(1, 8), (P, 7))
    f["expert_at"] = np.broadcast_to(np.arange(32), (P, 32))
    f["step_at"] = np.broadcast_to(np.arange(40), (P, 40))
    f["neghalf"] = np.full((P, 8), -0.5)
    return {n: np.asarray(v, np.float32) for n, v in f.items()}


def kernel(**i):
    import concourse.bacc as bacc
    from concourse.bass_utils import run_bass_kernel_spmd as run

    i = {n: np.asarray(v) for n, v in i.items()}

    def rows(v):
        v = v.reshape(1, -1)
        return np.broadcast_to(v, (P, v.shape[1]))

    def by_in(w):
        return w.transpose(1, 0, 2).reshape(w.shape[1], -1)

    def by_tile(w):
        return w.reshape(-1, P, w.shape[-1]).transpose(1, 0, 2).reshape(P, -1)

    def pad(v):
        out = np.zeros((P, v.shape[1]), v.dtype)
        out[0:v.shape[0]] = v
        return out

    f = shape_constants()
    wkv, bkv = i["L0_xattn_W_kv"].reshape(D, H, 2, 8), i["L0_xattn_b_kv"].reshape(H, 2, 8)
    f["a0wk"], f["a0wv"] = wkv[:, :, 0].reshape(D, D), wkv[:, :, 1].reshape(D, D)
    f["a0bk"], f["a0bv"] = bkv[:, 0].reshape(D, 1), rows(bkv[:, 1])
    f["a0wq"], f["a0bq"] = i["L0_xattn_W_q"], i["L0_xattn_b_q"].reshape(D, 1)
    f["a0wo"], f["a0bo"] = i["L0_xattn_W_o"], rows(i["L0_xattn_b_o"])
    f["f0wr"] = by_in(i["L0_ffn_Wr"].transpose(0, 2, 1))
    f["f0ws"] = by_in(i["L0_ffn_Ws"].transpose(0, 2, 1))
    f["f0cent"], f["f0eb"] = i["L0_ffn_centroids"].T, rows(i["L0_ffn_expert_biases"])
    f["f0br"] = pad(np.concatenate([i["L0_ffn_br"], i["L0_ffn_bs"]]))
    f["a1wk"], f["a1wv"] = i["L1_xattn_w_kv"][:, :1024], i["L1_xattn_w_kv"][:, 1024:]
    f["a1wq"], f["a1wo"] = i["L1_xattn_w_q"], by_tile(i["L1_xattn_w_out"])
    f["a1bo"], f["a1g"], f["a1b"] = rows(i["L1_xattn_b_out"]), i["L1_xattn_ln_gamma"].reshape(D, 1), i["L1_xattn_ln_beta"].reshape(D, 1)
    f["a1gate"] = rows(i["L1_xattn_gate"])
    f["f1gw"] = i["L1_ffn_gate_w"]
    f["f1sgu"] = np.concatenate([i["L1_ffn_shared_gate_w"], i["L1_ffn_shared_up_w"]], 1)
    f["f1sd"] = by_tile(i["L1_ffn_shared_down_w"])
    for n in "kvq":
        f[f"a2w{n}"] = i[f"L2_xattn_w{n}"].T
    f["a2wo"], f["a2bo"] = i["L2_xattn_wo"].T, rows(i["L2_xattn_bo"])
    f["a2bk"], f["a2bq"], f["a2bv"] = i["L2_xattn_bk"].reshape(D, 1), i["L2_xattn_bq"].reshape(D, 1), rows(i["L2_xattn_bv"])
    f["f2g1"], f["f2g2"] = i["L2_ffn_g1"].reshape(D, 1), i["L2_ffn_g2"].reshape(D, 1)
    f["f2wq"], f["f2wkc"], f["f2wvc"] = i["L2_ffn_Wq"].T, np.tile(i["L2_ffn_Wkc"].T, (1, 4)), i["L2_ffn_Wvc"].T
    f["f2wo"], f["f2wr"], f["f2eb"] = i["L2_ffn_Wo"].T, i["L2_ffn_Wr"].T, rows(i["L2_ffn_expert_bias"])
    for n in "123":
        both = np.concatenate([i[f"L2_ffn_eW{n}"], i[f"L2_ffn_sW{n}"][None]])
        f[f"f2w{n}"] = by_in(both.transpose(0, 2, 1))
    f["a3wk"], f["a3wv"] = i["L3_xattn_Wkv"][:D].T, i["L3_xattn_Wkv"][D:].T
    f["a3wq"], f["a3wo"] = i["L3_xattn_Wq"].T, i["L3_xattn_Wout"].T
    f["f3cent"], f["f3g"], f["f3b"] = i["L3_ffn_centroids"].T, i["L3_ffn_ln_g"].T, i["L3_ffn_ln_b"].T
    f["f3b1"] = i["L3_ffn_b1"].reshape(8, 4, P).transpose(2, 0, 1).reshape(P, 32)
    f["f3b2"] = rows(i["L3_ffn_b2"])

    arrays = {}
    for name, group in GROUPS:
        for n, wd in group:
            assert f[n].shape == (P, wd), (n, f[n].shape)
        arrays[name] = np.concatenate([f[n] for n, _ in group], 1)
    arrays["moe1"] = by_in(np.concatenate([
        i["L1_ffn_routed_gate_w"], i["L1_ffn_routed_up_w"],
        i["L1_ffn_routed_down_w"].reshape(32, 2, P, D).transpose(0, 2, 1, 3).reshape(32, P, 256)], 2))
    arrays["moe3"] = by_in(np.concatenate([
        i["L3_ffn_w1"], i["L3_ffn_w2"].reshape(8, 4, P, D).transpose(0, 2, 1, 3).reshape(8, P, 512)], 2))
    arrays["x"] = by_tile(i["x"].reshape(B * S, D))
    arrays["ctx"] = by_tile(i["ctx_1024"].reshape(B * SC, D))
    arrays["mask0"] = i["mask_BxSxS2_ik0"].transpose(2, 0, 1).reshape(SC, B * S)
    arrays["mask3"] = i["mask_SxS2_fk0"].T
    arrays = {n: np.ascontiguousarray(a) for n, a in arrays.items()}

    nc = bacc.Bacc("TRN2", target_bir_lowering=False, num_devices=1)
    dram = {n: nc.dram_tensor(n + "_in", a.shape, mybir.dt.from_np(a.dtype), kind="ExternalInput").ap()
            for n, a in arrays.items()}
    dram["out"] = nc.dram_tensor("out", [P, TILES * D], F32, kind="ExternalOutput").ap()
    dram["scratch0"] = nc.dram_tensor("sorted_in", [B * S, D], F32, kind="Internal").ap()
    dram["kparts"] = nc.dram_tensor("kparts", [3, P, B * SC], BF16, kind="Internal").ap()
    dram["qparts"] = nc.dram_tensor("qparts", [3, P, B * S], BF16, kind="Internal").ap()
    dram["scratch1"] = nc.dram_tensor("sorted_out", [B * S, D], F32, kind="Internal").ap()
    build(nc, dram)
    r = run(nc, [{n + "_in": a for n, a in arrays.items()}], core_ids=[0])
    out = r.results[0]["out"]
    return out.reshape(P, TILES, D).transpose(1, 0, 2).reshape(B, S, D)
```
